# Optimizing a Trainium2 kernel written in Bass

```python
import numpy as np
import jax
import jax.numpy as jnp

def _softmax(x, axis=-1):
    return jax.nn.softmax(x, axis=axis)

def _gelu(x):
    return jax.nn.gelu(x, approximate=True)

def _silu(x):
    return jax.nn.silu(x)

def _sigmoid(x):
    return jax.nn.sigmoid(x)

def _layernorm(x, axis=-1, eps=1e-05):
    m = jnp.mean(x, axis=axis, keepdims=True)
    v = jnp.var(x, axis=axis, keepdims=True)
    return (x - m) / jnp.sqrt(v + eps)

def _scatter_add(tgt, idx, src, axis=0):
    return tgt.at[idx].add(src)

def _segment_sum(src, seg, n):
    return jax.ops.segment_sum(src, seg, n)
kernel_name = 'mk_decoder_postln_d2_seqx_r8_d29778'

def setup_inputs(seed: int=0):
    np.random.seed(seed)
    _w = jnp.asarray

    def _rec_inputs():
        import jax
        import jax.numpy as jnp
        _rk = jax.random.key(seed)
        x = -0.0002928 + 1 * jax.random.normal(jax.random.fold_in(_rk, 1), (32, 64, 128), jnp.float32)
        _lenS = 64 - jax.random.randint(jax.random.fold_in(_rk, 7), (32,), 0, max(1, 64 // 4) + 1, jnp.int32)
        _lenS2 = 64 - jax.random.randint(jax.random.fold_in(_rk, 8), (32,), 0, max(1, 64 // 4) + 1, jnp.int32)
        _ctx_1024P = jax.random.normal(jax.random.fold_in(_rk, 11), (32, 16, 128), jnp.float32)
        _ctx_1024c = jax.random.dirichlet(jax.random.fold_in(_rk, 511), 0.3 * jnp.ones((16,), jnp.float32), (32, 64))
        _ctx_1024t = jnp.einsum('bsk,bkd->bsd', _ctx_1024c, _ctx_1024P)
        _ctx_1024t = _ctx_1024t * jax.lax.rsqrt(jnp.mean(jnp.square(_ctx_1024t)) + 1e-12) * 0.953939
        ctx_1024 = -1.39393e-06 + 0.999914 * (_ctx_1024t + 0.3 * jax.random.normal(jax.random.fold_in(_rk, 611), (32, 64, 128), jnp.float32))
        return (x, ctx_1024)
    x, ctx_1024 = _rec_inputs()

    def _L0_attn_setup():
        import jax, jax.numpy as jnp
        import numpy as np
        B, N, E, H, DEPTH = (2, 256, 128, 8, 12)
        D = E // H // 2
        LN_EPS = 1e-05
        key = jax.random.key(seed)
        ks = jax.random.split(key, 10)
        w = lambda k: jax.random.normal(k, (E, E), jnp.float32) * E ** (-0.5)
        lp = lambda k: jax.random.normal(k, (D,), jnp.float32) * 0.1
        return {'x': jax.random.normal(ks[0], (B, N, E), jnp.float32), 'Wq': w(ks[1]), 'Wk': w(ks[2]), 'Wv': w(ks[3]), 'Wo': w(ks[4]), 'lq1': lp(ks[5]), 'lk1': lp(ks[6]), 'lq2': lp(ks[7]), 'lk2': lp(ks[8]), 'ln_g': jnp.ones((2 * D,), jnp.float32), 'ln_b': jnp.zeros((2 * D,), jnp.float32)}
    _L0_attn_all = _L0_attn_setup()
    _L0_attn_in = {k: v for k, v in _L0_attn_all.items() if k in ('Wq', 'Wk', 'Wv', 'Wo', 'lq1', 'lk1', 'lq2', 'lk2', 'ln_g', 'ln_b')}
    del _L0_attn_all

    def _L0_xattn_setup():
        import jax, jax.numpy as jnp
        import numpy as np
        B, T, D, H = (2, 256, 128, 16)
        DH = D // H
        key = jax.random.key(seed)
        ks = jax.random.split(key, 11)
        s = 1.0 / np.sqrt(D)
        return {'q': jax.random.normal(ks[0], (B, T, D), jnp.float32), 'k': jax.random.normal(ks[1], (B, T, D), jnp.float32), 'v': jax.random.normal(ks[2], (B, T, D), jnp.float32), 'wq_w': jax.random.normal(ks[3], (D, D), jnp.float32) * s, 'wq_b': jnp.zeros((D,), jnp.float32), 'wk_w': jax.random.normal(ks[4], (D, D), jnp.float32) * s, 'wk_b': jnp.zeros((D,), jnp.float32), 'wv_w': jax.random.normal(ks[5], (D, D), jnp.float32) * s, 'wv_b': jnp.zeros((D,), jnp.float32), 'wo_w': jax.random.normal(ks[6], (D, D), jnp.float32) * s, 'wo_b': jnp.zeros((D,), jnp.float32)}
    _L0_xattn_all = _L0_xattn_setup()
    _L0_xattn_in = {k: v for k, v in _L0_xattn_all.items() if k in ('wq_w', 'wq_b', 'wk_w', 'wk_b', 'wv_w', 'wv_b', 'wo_w', 'wo_b')}
    del _L0_xattn_all

    def _L0_ffn_setup():
        import jax, jax.numpy as jnp
        import numpy as np
        HIDDEN = 128
        NUM_EXPERTS = 8
        BATCH, SEQ = (4, 512)
        key = jax.random.key(seed)
        ks = jax.random.split(key, 6)
        s = 1.0 / np.sqrt(HIDDEN)
        tokens = jax.random.normal(ks[0], (BATCH, SEQ, HIDDEN), dtype=jnp.float32)
        gate_w = jax.random.uniform(ks[1], (NUM_EXPERTS, HIDDEN), jnp.float32, -s, s)
        expert_w = jax.random.uniform(ks[2], (NUM_EXPERTS, HIDDEN, HIDDEN), jnp.float32, -s, s)
        expert_b = jax.random.uniform(ks[3], (NUM_EXPERTS, HIDDEN), jnp.float32, -s, s)
        combine_w = jax.random.uniform(ks[4], (HIDDEN, HIDDEN), jnp.float32, -s, s)
        return {'tokens': tokens, 'gate_w': gate_w, 'expert_w': expert_w, 'expert_b': expert_b, 'combine_w': combine_w}
    _L0_ffn_all = _L0_ffn_setup()
    _L0_ffn_in = {k: v for k, v in _L0_ffn_all.items() if k in ('gate_w', 'expert_w', 'expert_b', 'combine_w')}
    del _L0_ffn_all

    def _L1_attn_setup():
        import jax, jax.numpy as jnp
        import numpy as np
        S, B, F = (256, 2, 128)
        H, D = (16, 64)
        P = H * D
        key = jax.random.key(seed)
        k1, k2, k3 = jax.random.split(key, 3)
        return {'src': jax.random.normal(k1, (S, B, F), dtype=jnp.float32), 'in_proj_weight': jax.random.normal(k2, (3 * P, F), dtype=jnp.float32) * (1.0 / np.sqrt(F)), 'in_proj_bias': jnp.zeros((3 * P,), dtype=jnp.float32), 'out_proj_weight': jax.random.normal(k3, (F, P), dtype=jnp.float32) * (1.0 / np.sqrt(P)), 'out_proj_bias': jnp.zeros((F,), dtype=jnp.float32)}
    _L1_attn_all = _L1_attn_setup()
    _L1_attn_in = {k: v for k, v in _L1_attn_all.items() if k in ('in_proj_weight', 'in_proj_bias', 'out_proj_weight', 'out_proj_bias')}
    del _L1_attn_all

    def _L1_xattn_setup():
        import jax, jax.numpy as jnp
        import numpy as np
        D1, D2, D3 = (128, 128, 128)
        key = jax.random.key(seed)
        k1, k2, kw, kb = jax.random.split(key, 4)
        x1 = jax.random.normal(k1, (8, 256, D1), dtype=jnp.float32)
        x2 = jax.random.normal(k2, (8, 256, D2), dtype=jnp.float32)
        bound = 1.0 / np.sqrt(D1 + D2)
        W = jax.random.uniform(kw, (D3, D1 + D2), minval=-bound, maxval=bound, dtype=jnp.float32)
        b = jax.random.uniform(kb, (D3,), minval=-bound, maxval=bound, dtype=jnp.float32)
        return {'x1': x1, 'x2': x2, 'W': W, 'b': b}
    _L1_xattn_all = _L1_xattn_setup()
    _L1_xattn_in = {k: v for k, v in _L1_xattn_all.items() if k in ('W', 'b')}
    del _L1_xattn_all

    def _L1_ffn_setup():
        import jax, jax.numpy as jnp
        import numpy as np
        E = 8
        K = 2
        D = 128
        H = 4 * D
        EPS = 1e-05
        TEMP = 1.5
        key = jax.random.key(seed)
        ks = jax.random.split(key, 6)
        B, T = (2, 256)
        x = jax.random.normal(ks[0], (B, T, D), dtype=jnp.float32)
        gamma = jnp.ones((D,), dtype=jnp.float32)
        beta = jnp.zeros((D,), dtype=jnp.float32)
        router_w = jax.random.normal(ks[1], (E, D), dtype=jnp.float32) * 0.02
        W1 = jax.random.normal(ks[2], (E, D, H), dtype=jnp.float32) * 0.02
        W2 = jax.random.normal(ks[3], (E, H, D), dtype=jnp.float32) * 0.02
        return {'x': x, 'gamma': gamma, 'beta': beta, 'router_w': router_w, 'W1': W1, 'W2': W2}
    _L1_ffn_all = _L1_ffn_setup()
    _L1_ffn_in = {k: v for k, v in _L1_ffn_all.items() if k in ('gamma', 'beta', 'router_w', 'W1', 'W2')}
    del _L1_ffn_all
    return {'x': x, 'ctx_1024': ctx_1024, 'L0_attn_Wq': _L0_attn_in['Wq'], 'L0_attn_Wk': _L0_attn_in['Wk'], 'L0_attn_Wv': _L0_attn_in['Wv'], 'L0_attn_Wo': _L0_attn_in['Wo'], 'L0_attn_lq1': _L0_attn_in['lq1'], 'L0_attn_lk1': _L0_attn_in['lk1'], 'L0_attn_lq2': _L0_attn_in['lq2'], 'L0_attn_lk2': _L0_attn_in['lk2'], 'L0_attn_ln_g': _L0_attn_in['ln_g'], 'L0_attn_ln_b': _L0_attn_in['ln_b'], 'L0_xattn_wq_w': _L0_xattn_in['wq_w'], 'L0_xattn_wq_b': _L0_xattn_in['wq_b'], 'L0_xattn_wk_w': _L0_xattn_in['wk_w'], 'L0_xattn_wk_b': _L0_xattn_in['wk_b'], 'L0_xattn_wv_w': _L0_xattn_in['wv_w'], 'L0_xattn_wv_b': _L0_xattn_in['wv_b'], 'L0_xattn_wo_w': _L0_xattn_in['wo_w'], 'L0_xattn_wo_b': _L0_xattn_in['wo_b'], 'L0_ffn_gate_w': _L0_ffn_in['gate_w'], 'L0_ffn_expert_w': _L0_ffn_in['expert_w'], 'L0_ffn_expert_b': _L0_ffn_in['expert_b'], 'L0_ffn_combine_w': _L0_ffn_in['combine_w'], 'L1_attn_in_proj_weight': _L1_attn_in['in_proj_weight'], 'L1_attn_in_proj_bias': _L1_attn_in['in_proj_bias'], 'L1_attn_out_proj_weight': _L1_attn_in['out_proj_weight'], 'L1_attn_out_proj_bias': _L1_attn_in['out_proj_bias'], 'L1_xattn_W': _L1_xattn_in['W'], 'L1_xattn_b': _L1_xattn_in['b'], 'L1_ffn_gamma': _L1_ffn_in['gamma'], 'L1_ffn_beta': _L1_ffn_in['beta'], 'L1_ffn_router_w': _L1_ffn_in['router_w'], 'L1_ffn_W1': _L1_ffn_in['W1'], 'L1_ffn_W2': _L1_ffn_in['W2']}

def reference(x, ctx_1024, L0_attn_Wq, L0_attn_Wk, L0_attn_Wv, L0_attn_Wo, L0_attn_lq1, L0_attn_lk1, L0_attn_lq2, L0_attn_lk2, L0_attn_ln_g, L0_attn_ln_b, L0_xattn_wq_w, L0_xattn_wq_b, L0_xattn_wk_w, L0_xattn_wk_b, L0_xattn_wv_w, L0_xattn_wv_b, L0_xattn_wo_w, L0_xattn_wo_b, L0_ffn_gate_w, L0_ffn_expert_w, L0_ffn_expert_b, L0_ffn_combine_w, L1_attn_in_proj_weight, L1_attn_in_proj_bias, L1_attn_out_proj_weight, L1_attn_out_proj_bias, L1_xattn_W, L1_xattn_b, L1_ffn_gamma, L1_ffn_beta, L1_ffn_router_w, L1_ffn_W1, L1_ffn_W2):
    import jax
    import jax.numpy as jnp

    def _L0_attn_ref(x, Wq, Wk, Wv, Wo, lq1, lk1, lq2, lk2, ln_g, ln_b):
        import jax, jax.numpy as jnp
        import numpy as np
        B, N, E, H, DEPTH = (2, 256, 128, 8, 12)
        D = E // H // 2
        LN_EPS = 1e-05
        b, n, e = x.shape
        lam_init = 0.8 - 0.6 * np.exp(-0.3 * DEPTH)
        q = (x @ Wq).reshape(b, n, 2 * H, D).transpose(0, 2, 1, 3) * D ** (-0.5)
        k = (x @ Wk).reshape(b, n, 2 * H, D).transpose(0, 2, 1, 3)
        v = (x @ Wv).reshape(b, n, H, 2 * D).transpose(0, 2, 1, 3)
        scores = jnp.einsum('bhqd,bhkd->bhqk', q, k)
        attn = jax.nn.softmax(scores, axis=-1).reshape(b, H, 2, n, n)
        lam = jnp.exp(jnp.sum(lq1 * lk1)) - jnp.exp(jnp.sum(lq2 * lk2)) + lam_init
        w_diff = attn[:, :, 0] - lam * attn[:, :, 1]
        o = jnp.einsum('bhqk,bhkd->bhqd', w_diff, v)
        mu = o.mean(-1, keepdims=True)
        var = ((o - mu) ** 2).mean(-1, keepdims=True)
        o = (o - mu) * jax.lax.rsqrt(var + LN_EPS) * ln_g + ln_b
        o = o.transpose(0, 2, 1, 3).reshape(b, n, e)
        return o @ Wo

    def _L0_xattn_ref(q, k, v, wq_w, wq_b, wk_w, wk_b, wv_w, wv_b, wo_w, wo_b):
        import jax, jax.numpy as jnp
        import numpy as np
        B, T, D, H = (2, 256, 128, 16)
        DH = D // H
        b, t, d = q.shape
        wq = (q @ wq_w.T + wq_b).reshape(b, t, H, DH)
        wk = (k @ wk_w.T + wk_b).reshape(b, t, H, DH)
        wv = (v @ wv_w.T + wv_b).reshape(b, t, H, DH)
        scores = jnp.einsum('bthd,bshd->bhts', wq, wk) / jnp.sqrt(jnp.float32(DH))
        probs = jax.nn.softmax(scores, axis=-1)
        attn = jnp.einsum('bhts,bshd->bthd', probs, wv)
        attn = attn.reshape(b, t, d)
        return attn @ wo_w.T + wo_b

    def _L0_ffn_ref(tokens, gate_w, expert_w, expert_b, combine_w):
        import jax, jax.numpy as jnp
        import numpy as np
        HIDDEN = 128
        NUM_EXPERTS = 8
        BATCH, SEQ = (4, 512)
        B, S, H = tokens.shape
        logits = jnp.einsum('bsh,eh->bse', tokens, gate_w)
        probs = jax.nn.softmax(logits, axis=-1)
        top2_w, top2_idx = jax.lax.top_k(probs, 2)
        flat = tokens.reshape(B * S, H)
        flat_idx = top2_idx.reshape(B * S, 2)
        flat_w = top2_w.reshape(B * S, 2)
        expert_out = jax.nn.silu(jnp.einsum('nh,edh->ned', flat, expert_w) + expert_b[None, :, :])
        gathered = jnp.take_along_axis(expert_out, flat_idx[:, :, None], axis=1)
        mixed = jnp.sum(gathered * flat_w[:, :, None], axis=1)
        out = jnp.einsum('bsh,dh->bsd', mixed.reshape(B, S, H), combine_w)
        return out

    def _L1_attn_ref(src, in_proj_weight, in_proj_bias, out_proj_weight, out_proj_bias):
        import jax, jax.numpy as jnp
        import numpy as np
        S, B, F = (256, 2, 128)
        H, D = (16, 64)
        P = H * D
        s, b, f = src.shape
        h, d = (H, D)
        qkv = jnp.einsum('sbf,pf->sbp', src, in_proj_weight) + in_proj_bias
        q, k, v = jnp.split(qkv, 3, axis=-1)

        def to_heads(x):
            return jnp.swapaxes(x.reshape(s, b * h, d), 0, 1)
        q = to_heads(q) / np.sqrt(d)
        k = to_heads(k)
        v = to_heads(v)
        attn = jnp.einsum('nsd,ntd->nst', q, k)
        attn = jax.nn.softmax(attn, axis=-1)
        out = jnp.einsum('nst,ntd->nsd', attn, v)
        out = jnp.swapaxes(out, 0, 1).reshape(s * b, h * d)
        out = out @ out_proj_weight.T + out_proj_bias
        return out.reshape(s, b, f)

    def _L1_xattn_ref(x1, x2, W, b):
        import jax, jax.numpy as jnp
        import numpy as np
        D1, D2, D3 = (128, 128, 128)
        d1 = x1.shape[-1]
        W1 = W[:, :d1]
        W2 = W[:, d1:]
        part1 = jnp.einsum('bld,ed->ble', x1, W1)
        part2 = jnp.einsum('bld,ed->be', x2, W2) / x2.shape[1]
        return part1 + part2[:, None, :] + b

    def _L1_ffn_ref(x, gamma, beta, router_w, W1, W2):
        import jax, jax.numpy as jnp
        import numpy as np
        E = 8
        K = 2
        D = 128
        H = 4 * D
        EPS = 1e-05
        TEMP = 1.5
        res = x
        mu = jnp.mean(x, axis=-1, keepdims=True)
        var = jnp.mean(jnp.square(x - mu), axis=-1, keepdims=True)
        xn = (x - mu) * jax.lax.rsqrt(var + EPS) * gamma + beta
        logits = jnp.einsum('btd,ed->bte', xn, router_w)
        probs = jax.nn.softmax(logits / TEMP, axis=-1)
        w, idx = jax.lax.top_k(probs, K)
        wdense = jnp.sum(jax.nn.one_hot(idx, E, dtype=w.dtype) * w[..., None], axis=-2)
        h = jax.nn.silu(jnp.einsum('btd,edf->betf', xn, W1))
        y = jnp.einsum('betf,efd->betd', h, W2)
        out = jnp.einsum('bte,betd->btd', wdense, y)
        return out + res
    x = _layernorm(x + _L0_attn_ref(x, L0_attn_Wq, L0_attn_Wk, L0_attn_Wv, L0_attn_Wo, L0_attn_lq1, L0_attn_lk1, L0_attn_lq2, L0_attn_lk2, L0_attn_ln_g, L0_attn_ln_b), axis=-1)
    x = _layernorm(x + _L0_xattn_ref(x, ctx_1024, ctx_1024, L0_xattn_wq_w, L0_xattn_wq_b, L0_xattn_wk_w, L0_xattn_wk_b, L0_xattn_wv_w, L0_xattn_wv_b, L0_xattn_wo_w, L0_xattn_wo_b), axis=-1)
    x = _layernorm(x + _L0_ffn_ref(x, L0_ffn_gate_w, L0_ffn_expert_w, L0_ffn_expert_b, L0_ffn_combine_w), axis=-1)
    x = _layernorm(x + _L1_attn_ref(x, L1_attn_in_proj_weight, L1_attn_in_proj_bias, L1_attn_out_proj_weight, L1_attn_out_proj_bias), axis=-1)
    x = _layernorm(x + _L1_xattn_ref(x, ctx_1024, L1_xattn_W, L1_xattn_b), axis=-1)
    x = _layernorm(x + _L1_ffn_ref(x, L1_ffn_gamma, L1_ffn_beta, L1_ffn_router_w, L1_ffn_W1, L1_ffn_W2), axis=-1)
    return x

_drawn_inputs = setup_inputs


def setup_inputs(seed=0):
    import zlib

    import numpy as np

    out = dict(_drawn_inputs(seed))
    spreads = {'L0_attn_ln_g': (1.0, 0.2),
     'L0_attn_ln_b': (0.0, 0.1),
     'L0_xattn_wq_b': (0.0, 0.37),
     'L0_xattn_wk_b': (0.0, 0.8),
     'L0_xattn_wv_b': (0.0, 0.1),
     'L0_xattn_wo_b': (0.0, 0.1),
     'L1_attn_in_proj_bias': (0.0, 0.1),
     'L1_attn_out_proj_bias': (0.0, 0.1),
     'L1_ffn_gamma': (1.0, 0.6),
     'L1_ffn_beta': (0.0, 0.8)}
    factors = {'L0_attn_lq1': 5.468,
     'L0_attn_lk1': 3.253,
     'L0_ffn_expert_b': 8.0,
     'L1_ffn_router_w': 8.0,
     'L1_ffn_W1': 8.0,
     'L1_ffn_W2': 8.0}
    for name, (base, spread) in spreads.items():
        noise = np.random.default_rng([zlib.crc32(name.encode()), seed]).standard_normal(out[name].shape)
        drawn = base * np.exp(spread * noise) if base else spread * noise
        out[name] = jnp.asarray(drawn.astype(out[name].dtype))
    for name, factor in factors.items():
        out[name] = (out[name] * factor).astype(out[name].dtype)
    return out
```

```python
from contextlib import ExitStack

import numpy as np

import concourse.bass as bass
from concourse import mybir

F32 = mybir.dt.float32
BF16 = mybir.dt.bfloat16
U32 = mybir.dt.uint32
ACT = mybir.ActivationFunctionType
ALU = mybir.AluOpType
AX = mybir.AxisListType

P = 128
B, S, E = 32, 64, 128
NT = B * S // P
LN_EPS = 1e-5
CHUNK = 512

NPAIR, HD, VD = 8, 8, 16
H1, D1 = 16, 64
NJ = H1 // 2
NE = 8
FF = 512
NF = FF // P
LAM_INIT = 0.8 - 0.6 * float(np.exp(-0.3 * 12))
ROUTER_TEMP = 1.5
MASKED = -1e30


def ge(engine, semaphore, value):
    if not isinstance(value, int) or value > 0:
        engine.wait_ge(semaphore, value)


def upto(value, most):
    return min(value, most) if isinstance(value, int) else value


def pipelined(engine, parts, n=NT):
    most, least = max(lag for lag, _ in parts), min(lag for lag, _ in parts)

    def step(i):
        for lag, part in parts:
            if not isinstance(i, int) or 0 <= i + lag < n:
                part(i + lag)

    lo, hi = 1 - least, n - most - 1
    for i in range(-most, lo):
        step(i)
    with engine.Fori(lo, hi) as i:
        step(i)
    for i in range(hi, n - least):
        step(i)


class Norm:

    def __init__(self, nc, ctx, tag):
        self.nc = nc
        sb = lambda name, shape: ctx.enter_context(nc.sbuf_tensor(f"{tag}_{name}", shape, F32))
        sem = lambda name: ctx.enter_context(nc.semaphore(f"{tag}_{name}"))
        self.y, self.out = sb("y", [P, P]), sb("normed", [P, P])
        self.stats, self.mv, self.rstd = sb("stats", [P, 6]), sb("mv", [P, 2]), sb("rstd", [P, 2])
        self.y_ready, self.stats_ready, self.mv_ready = sem("y_ready"), sem("stats_ready"), sem("mv_ready")
        self.ve_ready, self.rstd_ready, self.normed = sem("ve_ready"), sem("rstd_ready"), sem("normed_ready")

    def statistics(self, dve, t, src, residual):
        nc = self.nc
        ge(dve, self.normed, t)
        nc.vector.tensor_tensor(self.y[:], src, residual, ALU.add).then_inc(self.y_ready, 1)
        dve.wait_ge(self.y_ready, t + 1)
        self.moments(dve, t, self.y[:])

    def moments(self, dve, t, src):
        nc = self.nc
        nc.vector.bn_stats(self.stats[:], src).then_inc(self.stats_ready, 1)
        dve.wait_ge(self.stats_ready, t + 1)
        dve.nop(nofuse=True)
        nc.vector.bn_aggr(self.mv[:], self.stats[:]).then_inc(self.mv_ready, 1)

    def power(self, pool, t, neghalf, eps):
        nc = self.nc
        pool.wait_ge(self.mv_ready, t + 1)
        ge(pool, self.normed, t)
        nc.gpsimd.tensor_tensor(self.rstd[:, 0:1], self.mv[:, 1:2], eps, ALU.add).then_inc(self.ve_ready, 1)
        pool.wait_ge(self.ve_ready, t + 1)
        nc.gpsimd.tensor_tensor(self.rstd[:, 1:2], self.rstd[:, 0:1], neghalf, ALU.pow).then_inc(self.rstd_ready, 1)

    def scaling(self, dve, t, src=None, dst=None):
        dve.wait_ge(self.rstd_ready, t + 1)
        self.nc.vector.tensor_scalar(self.out[:] if dst is None else dst, self.y[:] if src is None else src, self.mv[:, 0:1],
                                     self.rstd[:, 1:2], ALU.subtract, ALU.mult).then_inc(self.normed, 1)


def pair_attention(nc, banks, self_diff, w, q_src, kv_src, km, vb, residual, res_next, xt_next, c, logits=None):
    tag = "self" if self_diff else "cross"
    with ExitStack() as ctx:
        def sb(name, shape, dt=F32):
            return ctx.enter_context(nc.sbuf_tensor(f"{tag}_{name}", shape, dt))

        def sem(name):
            return ctx.enter_context(nc.semaphore(f"{tag}_{name}"))

        qt = sb("qt", [P, B * S])
        kt = sb("kt", [P, B * S])
        xdup = sb("xdup", [P, 2, 2, S])
        q2 = sb("q2", [P, 2, 2, S])
        score = sb("score", [P, 2, CHUNK])
        prob = sb("prob", [P, 2, CHUNK])
        probt = sb("probt", [P, 2, CHUNK])
        top = sb("top", [P, 2, NPAIR])
        rsum = sb("rsum", [P, 2, NPAIR])
        rhalf = sb("rhalf", [P, 2, NPAIR, 2])
        on = sb("on", [P, 2, NPAIR, VD])
        ot = sb("ot", [P, P])
        xnt = sb("xnt", [P, P])
        norm = Norm(nc, ctx, tag)
        ps_s, ps_t, ps_o, ps_v, ps_d, ps_a = banks[0:2], banks[2:4], banks[4], banks[5], banks[6], banks[7]

        proj_done, proj_out = sem("proj_done"), sem("proj_out")
        xdup_ready, q2_ready, km_ready = sem("xdup_ready"), sem("q2_ready"), sem("km_ready")
        values_done, scores_done = sem("values_done"), sem("scores_done")
        vb_ready, top_ready, score_ready = sem("vb_ready"), sem("top_ready"), sem("score_ready")
        prob_ready, transp_done, probt_ready = sem("prob_ready"), sem("transp_done"), sem("probt_ready")
        pv_done, rsum_ready, on_ready = sem("pv_done"), sem("rsum_ready"), sem("on_ready")
        comb_done, back_done, ot_ready, xt_ready = sem("comb_done"), sem("back_done"), sem("ot_ready"), sem("xt_ready")
        wo_done, res_ready = sem("wo_done"), sem("res_ready")
        if not self_diff:
            rhalf_ready, xnt_ready, gate_done, gate_out = sem("rhalf_ready"), sem("xnt_ready"), sem("gate_done"), sem("gate_out")
        else:
            ones_ready = sem("ones_ready")
            hn_c = sb("hn_c", [P, NPAIR, VD])
            hn_sq = sb("hn_sq", [P, NPAIR, VD])
            hn_o = sb("hn_o", [P, NPAIR, VD])
            hn_m, hn_v = sb("hn_m", [P, NPAIR]), sb("hn_v", [P, NPAIR])
            hn_r = sb("hn_r", [P, 2, NPAIR])
            comb = sb("comb", [P, 2, P])
            lam_prod, lam = sb("lam_prod", [P, 2, HD]), sb("lam", [P, 5])
            hn_step, hn_var, hn_ve, hn_rstd, hn_done = sem("hn_step"), sem("hn_var"), sem("hn_ve"), sem("hn_rstd"), sem("hn_done")
            lam_step, lam_exp, hnt_done = sem("lam_step"), sem("lam_exp"), sem("hnt_done")

        YLAG = -2 if self_diff else -1
        block = ctx.enter_context(nc.Block())

        @block.tensor
        def _(pe):
            for n in range(8):
                src, wgt = (kv_src, w["k"]) if n < 4 else (q_src, w["q"])
                ge(pe, proj_out, n - 1)
                nc.tensor.matmul(ps_s[n % 2][:], wgt, src[:, CHUNK * (n % 4):CHUNK * (n % 4 + 1)],
                                 start=True, stop=True).then_inc(proj_done, 1)
            pe.wait_ge(proj_out, 8)
            if self_diff:
                pe.wait_ge(lam_step, 5)

            def scores(t):
                ge(pe, vb_ready, 2 * t)
                for u in range(2):
                    pe.wait_ge(xdup_ready, 2 * t + u + 1)
                    nc.tensor.matmul(ps_v[:, P * u:P * (u + 1)], xdup[:, u].rearrange("p d s -> p (d s)"), w["v"],
                                     start=True, stop=True).then_inc(values_done, 1)
                for u in range(2):
                    pe.wait_ge(q2_ready, 2 * t + u + 1)
                    pe.wait_ge(km_ready, 2 * t + u + 1)
                    ge(pe, score_ready, 2 * (t - 1) + u + 1)
                    nc.tensor.matmul(ps_s[u][:], q2[:, u].rearrange("p d s -> p (d s)"), km[:, 2 * t + u, :],
                                     start=True, stop=True).then_inc(scores_done, 1)

            def transposes(t):
                for u in range(2):
                    pe.wait_ge(prob_ready, 2 * t + u + 1)
                    ge(pe, probt_ready, 2 * (t - 1) + u + 1)
                    for j in range(4):
                        last = nc.tensor.transpose(ps_t[u][:, P * j:P * (j + 1)], prob[:, u, P * j:P * (j + 1)], c["ident"])
                    last.then_inc(transp_done, 1)

            def weighted(t):
                ge(pe, on_ready, 2 * t)
                for u in range(2):
                    pe.wait_ge(probt_ready, 2 * t + u + 1)
                    pe.wait_ge(vb_ready, 2 * t + u + 1)
                    for j in range(4):
                        last = nc.tensor.matmul(ps_o[:, 136 * u + 34 * j:136 * u + 34 * (j + 1)],
                                                probt[:, u, P * j:P * (j + 1)],
                                                vb[:, 2 * t + u, j].rearrange("p h d -> p (h d)"), start=True, stop=True)
                    last.then_inc(pv_done, 1)

            def combine(t):
                pe.wait_ge(on_ready, 2 * t + 2)
                if self_diff:
                    ge(pe, norm.y_ready, t - 1)
                    for u in range(2):
                        last = nc.tensor.matmul(ps_d[:, 0:P], comb[:, u, :], on[:, u].rearrange("p h d -> p (h d)"),
                                                start=u == 0, stop=u == 1)
                else:
                    ge(pe, norm.y_ready, t)
                    for u in range(2):
                        last = nc.tensor.matmul(ps_d[:, S * u:S * (u + 1)], on[:, u].rearrange("p h d -> p (h d)"),
                                                c["both"], start=True, stop=True)
                last.then_inc(comb_done, 1)

            def back(t):
                pe.wait_ge(norm.normed, t + 1)
                ge(pe, xt_ready, t)
                if self_diff:
                    pe.wait_ge(ot_ready, t + 1)
                else:
                    ge(pe, gate_out, t)
                nc.tensor.transpose(ps_a[:, 0:P], norm.out[:], c["ident"]).then_inc(back_done, 1)

            def heads_back(t):
                pe.wait_ge(hn_done, t + 1)
                ge(pe, ot_ready, t)
                ge(pe, xt_ready, t - 1)
                nc.tensor.transpose(ps_a[:, P:2 * P], hn_o[:].rearrange("p h d -> p (h d)"), c["ident"]).then_inc(hnt_done, 1)

            def project(t):
                pe.wait_ge(ot_ready, t + 1)
                if self_diff:
                    pe.wait_ge(hn_step, upto(3 * (t + 1) + 2, 3 * (NT - 1) + 2))
                nc.tensor.matmul(ps_d[:, P:2 * P], ot[:], w["o"], start=True, stop=True).then_inc(wo_done, 1)

            def gate(t):
                pe.wait_ge(xnt_ready, t + 1)
                pe.wait_ge(xt_ready, t + 1)
                nc.tensor.matmul(ps_a[:, 2 * P:2 * P + NE], xnt[:], w["gate"], start=True, stop=True).then_inc(gate_done, 1)

            if self_diff:
                pipelined(pe, [(-1, combine), (-3, back), (-2, heads_back), (1, scores), (-2, project), (0, transposes),
                               (0, weighted)])
            else:
                pipelined(pe, [(-1, combine), (-2, back), (1, scores), (-1, project), (0, transposes), (0, weighted),
                               (-2, gate)])

        @block.vector
        def _(dve):
            if self_diff:
                nc.vector.tensor_copy(vb[:, :, :, :, VD].rearrange("p b j h -> p (b j) h"),
                                      c["half"].unsqueeze(1).broadcast_to([P, B * 4, 2])).then_inc(ones_ready, 1)
                nc.vector.tensor_tensor(lam_prod[:], w["lam"][:, 0:2, :], w["lam"][:, 2:4, :], ALU.mult).then_inc(lam_step, 1)
                dve.wait_ge(lam_step, 1)
                nc.vector.reduce_sum(lam[:, 0:2], lam_prod[:], axis=AX.X).then_inc(lam_step, 1)
                dve.wait_ge(lam_exp, 1)
                nc.vector.tensor_scalar(lam[:, 4:5], lam[:, 2:3], lam[:, 3:4], LAM_INIT, ALU.subtract, ALU.add).then_inc(lam_step, 1)
                dve.wait_ge(lam_step, 3)
                for u in range(2):
                    nc.vector.scalar_tensor_tensor(comb[:, u, :], c["second"][:, u, :], lam[:, 4:5], c["first"][:, u, :],
                                                   ALU.mult, ALU.add).then_inc(lam_step, 1)

            def softmax(t):
                for u in range(2):
                    pe_tile = ps_s[u][:].rearrange("p (h k) -> p h k", h=NPAIR)
                    dve.wait_ge(scores_done, 2 * t + u + 1)
                    ge(dve, score_ready, 2 * (t - 1) + u + 1)
                    nc.vector.reduce_max(top[:, u, :], pe_tile, axis=AX.X).then_inc(top_ready, 1)
                    dve.wait_ge(top_ready, 2 * t + u + 1)
                    ge(dve, prob_ready, 2 * (t - 1) + u + 1)
                    nc.vector.tensor_tensor(score[:, u].rearrange("p (h k) -> p h k", h=NPAIR), pe_tile,
                                            top[:, u, :].unsqueeze(2).broadcast_to([P, NPAIR, S]),
                                            ALU.subtract).then_inc(score_ready, 1)

            def value_blocks(t):
                dve.wait_ge(values_done, 2 * t + 2)
                for u in range(2):
                    nc.vector.tensor_tensor(vb[:, 2 * t + u, :, :, 0:VD],
                                            ps_v[:, P * u:P * (u + 1)].rearrange("p (j h d) -> p j h d", j=4, h=2),
                                            c["half"].unsqueeze(1).unsqueeze(3).broadcast_to([P, 4, 2, VD]),
                                            ALU.mult).then_inc(vb_ready, 1)

            def over_sums(t):
                dve.wait_ge(pv_done, 2 * t + 2)
                for u in range(2):
                    o = ps_o[:, 136 * u:136 * (u + 1)].rearrange("p (h d) -> p h d", h=NPAIR)
                    ge(dve, on_ready, 2 * (t - 1) + u + 1)
                    nc.vector.reciprocal(rsum[:, u, :], o[:, :, VD]).then_inc(rsum_ready, 1)
                for u in range(2):
                    o = ps_o[:, 136 * u:136 * (u + 1)].rearrange("p (h d) -> p h d", h=NPAIR)
                    dve.wait_ge(rsum_ready, 2 * t + u + 1)
                    ge(dve, comb_done, t)
                    if self_diff:
                        nc.vector.tensor_tensor(on[:, u], o[:, :, 0:VD], rsum[:, u, :].unsqueeze(2).broadcast_to([P, NPAIR, VD]),
                                                ALU.mult).then_inc(on_ready, 1)
                    else:
                        nc.vector.tensor_tensor(rhalf[:, u], rsum[:, u, :].unsqueeze(2).broadcast_to([P, NPAIR, 2]),
                                                c["half"].unsqueeze(1).broadcast_to([P, NPAIR, 2]), ALU.mult).then_inc(rhalf_ready, 1)
                        dve.wait_ge(rhalf_ready, 2 * t + u + 1)
                        nc.vector.tensor_tensor(on[:, u].rearrange("p h (a d) -> p h a d", a=2),
                                                o[:, :, 0:VD].rearrange("p h (a d) -> p h a d", a=2),
                                                rhalf[:, u].unsqueeze(3).broadcast_to([P, NPAIR, 2, HD]), ALU.mult).then_inc(on_ready, 1)

            def head_centre(t):
                d = ps_d[:, 0:P].rearrange("p (h d) -> p h d", h=NPAIR)
                dve.wait_ge(comb_done, t + 1)
                ge(dve, hn_done, t)
                nc.vector.reduce_sum(hn_m[:], d, axis=AX.X).then_inc(hn_step, 1)
                dve.wait_ge(hn_step, 3 * t + 1)
                nc.vector.scalar_tensor_tensor(hn_c[:], hn_m[:].unsqueeze(2).broadcast_to([P, NPAIR, VD]), -1.0 / VD, d,
                                               ALU.mult, ALU.add).then_inc(hn_step, 1)
                dve.wait_ge(hn_step, 3 * t + 2)
                nc.vector.scalar_tensor_tensor(hn_sq[:], hn_c[:], 1.0 / VD, hn_c[:], ALU.mult, ALU.mult).then_inc(hn_step, 1)
                dve.wait_ge(hn_step, 3 * t + 3)
                nc.vector.reduce_sum(hn_v[:], hn_sq[:], axis=AX.X).then_inc(hn_var, 1)

            def head_scale(t):
                dve.wait_ge(hn_rstd, t + 1)
                ge(dve, hnt_done, t)
                nc.vector.tensor_tensor(hn_o[:], hn_c[:], hn_r[:, 1, :].unsqueeze(2).broadcast_to([P, NPAIR, VD]),
                                        ALU.mult).then_inc(hn_done, 1)

            def statistics(t):
                dve.wait_ge(wo_done, t + 1)
                norm.statistics(dve, t, ps_d[:, P:2 * P], residual(t))

            def scaling(t):
                ge(dve, back_done, t)
                ge(dve, res_ready, t)
                norm.scaling(dve, t)

            if self_diff:
                dve.wait_ge(ones_ready, 1)
                pipelined(dve, [(-1, head_centre), (1, softmax), (-1, head_scale), (-2, statistics), (1, value_blocks),
                                (0, over_sums), (-2, scaling)])
            else:
                pipelined(dve, [(1, softmax), (-1, statistics), (1, value_blocks), (0, over_sums), (-1, scaling)])

        @block.scalar
        def _(act):
            for n in range(8):
                act.wait_ge(proj_done, n + 1)
                dst = (kt if n < 4 else qt)[:, CHUNK * (n % 4):CHUNK * (n % 4 + 1)]
                bias = w["kb"] if n < 4 else w["qb"]
                if bias is None:
                    nc.scalar.activation(dst, ps_s[n % 2][:], ACT.Copy).then_inc(proj_out, 1)
                else:
                    nc.scalar.activation(dst, ps_s[n % 2][:], ACT.Identity, bias=bias).then_inc(proj_out, 1)
            if self_diff:
                act.wait_ge(lam_step, 2)
                nc.scalar.activation(lam[:, 2:4], lam[:, 0:2], ACT.Exp).then_inc(lam_exp, 1)

            def exponent(t):
                for u in range(2):
                    act.wait_ge(score_ready, 2 * t + u + 1)
                    ge(act, transp_done, 2 * (t - 1) + u + 1)
                    nc.scalar.activation(prob[:, u, :], score[:, u, :], ACT.Exp).then_inc(prob_ready, 1)

            def probs_t(t):
                for u in range(2):
                    act.wait_ge(transp_done, 2 * t + u + 1)
                    ge(act, pv_done, 2 * (t - 1) + u + 1)
                    nc.scalar.activation(probt[:, u, :], ps_t[u][:], ACT.Copy).then_inc(probt_ready, 1)

            def feature_major(t):
                act.wait_ge(back_done, t + 1)
                if self_diff:
                    act.wait_ge(hnt_done, upto(t + 2, NT))
                else:
                    ge(act, gate_done, t)
                    nc.scalar.activation(xnt[:], ps_a[:, 0:P], ACT.Copy).then_inc(xnt_ready, 1)
                nc.scalar.activation(xt_next[:, bass.ds(P * t, P)], ps_a[:, 0:P], ACT.Copy).then_inc(xt_ready, 1)

            def outputs_t(t):
                if self_diff:
                    act.wait_ge(hnt_done, t + 1)
                    ge(act, wo_done, t)
                    nc.scalar.activation(ot[:], ps_a[:, P:2 * P], ACT.Identity, bias=w["ob"], scale=w["og"]).then_inc(ot_ready, 1)
                else:
                    act.wait_ge(comb_done, t + 1)
                    ge(act, wo_done, t)
                    nc.scalar.activation(ot[:], ps_d[:, 0:P], ACT.Identity, bias=w["vb"]).then_inc(ot_ready, 1)

            def gate_logits(t):
                act.wait_ge(gate_done, t + 1)
                nc.scalar.activation(logits[:, t, :], ps_a[:, 2 * P:2 * P + NE], ACT.Copy).then_inc(gate_out, 1)

            if self_diff:
                pipelined(act, [(-3, feature_major), (-2, outputs_t), (0, probs_t), (1, exponent)])
            else:
                pipelined(act, [(-1, outputs_t), (-2, feature_major), (0, probs_t), (1, exponent), (-2, gate_logits)])

        @block.gpsimd
        def _(pool):
            pool.wait_ge(proj_out, 8)

            def operands(t):
                for u in range(2):
                    ge(pool, values_done, 2 * (t - 1) + u + 1)
                    nc.gpsimd.tensor_copy(xdup[:, u], kv_src[:, bass.ds(P * t + S * u, S)].unsqueeze(1).broadcast_to([P, 2, S])
                                          ).then_inc(xdup_ready, 1)
                for u in range(2):
                    ge(pool, scores_done, 2 * (t - 1) + u + 1)
                    nc.gpsimd.tensor_tensor(q2[:, u], qt[:, bass.ds(P * t + S * u, S)].unsqueeze(1).broadcast_to([P, 2, S]),
                                            c["parity"].unsqueeze(2).broadcast_to([P, 2, S]), ALU.mult).then_inc(q2_ready, 1)
                    nc.gpsimd.tensor_tensor(km[:, 2 * t + u, :].rearrange("p (h k) -> p h k", h=NPAIR),
                                            kt[:, bass.ds(P * t + S * u, S)].unsqueeze(1).broadcast_to([P, NPAIR, S]),
                                            c["pair"].unsqueeze(2).broadcast_to([P, NPAIR, S]), ALU.mult).then_inc(km_ready, 1)

            def head_power(t):
                pool.wait_ge(hn_var, t + 1)
                ge(pool, hn_done, t)
                nc.gpsimd.tensor_tensor(hn_r[:, 0, :], hn_v[:], c["eps"], ALU.add).then_inc(hn_ve, 1)
                pool.wait_ge(hn_ve, t + 1)
                nc.gpsimd.tensor_tensor(hn_r[:, 1, :], hn_r[:, 0, :], c["neghalf"], ALU.pow).then_inc(hn_rstd, 1)

            def power(t):
                norm.power(pool, t, c["neghalf"][:, 0:1], c["eps"][:, 0:1])

            def keep_residual(t):
                pool.wait_ge(norm.normed, t + 1)
                if self_diff:
                    nc.gpsimd.tensor_tensor(res_next[:, t, :], norm.out[:], w["next_bias"], ALU.add).then_inc(res_ready, 1)
                else:
                    nc.gpsimd.tensor_copy(res_next[:, t, :], norm.out[:]).then_inc(res_ready, 1)

            if self_diff:
                pipelined(pool, [(-1, head_power), (-2, power), (-2, keep_residual), (2, operands)])
            else:
                pipelined(pool, [(-1, power), (-1, keep_residual), (2, operands)])
            pool.wait_ge(res_ready, NT)


def route(nc, ctx, tag, logits, iota, temp):
    sb = lambda name, shape, dt=F32: ctx.enter_context(nc.sbuf_tensor(f"{tag}_{name}", shape, dt))
    sem = lambda name: ctx.enter_context(nc.semaphore(f"{tag}_{name}"))
    ranked, ex = sb("ranked", [P, NT, NE]), sb("ex", [P, NT, NE])
    place, placef = sb("place", [P, NT, NE], U32), sb("placef", [P, NT, 2])
    prob = sb("prob", [P, 2, NT])
    total = sb("total", [P, NT])
    one, two, weight = sb("one", [P, NT, NE]), sb("two", [P, NT, NE]), sb("weight", [P, NT, NE])
    step, ready, exped = sem("step"), sem("ready"), sem("exped")
    weights_ready = sem("weights_ready")

    def before(dve):
        for t in range(NT):
            nc.vector.max(ranked[:, t, :], logits[:, t, :]).then_inc(step, 1)
        for t in range(NT):
            dve.wait_ge(step, t + 1)
            nc.vector.max_index(place[:, t, :], ranked[:, t, :], logits[:, t, :]).then_inc(step, 1)
        nc.vector.tensor_tensor(ex[:], ranked[:], ranked[:, :, 0:1].broadcast_to([P, NT, NE]), ALU.subtract).then_inc(ready, 1)

    def exponent(act):
        act.wait_ge(ready, 1)
        nc.scalar.activation(ex[:], ex[:], ACT.Exp, scale=1.0 / temp).then_inc(exped, 1)

    def after(dve):
        dve.wait_ge(step, 2 * NT)
        nc.vector.tensor_copy(placef[:], place[:, :, 0:2]).then_inc(step, 1)
        dve.wait_ge(exped, 1)
        nc.vector.reduce_sum(total[:], ex[:], axis=AX.X).then_inc(step, 1)
        dve.wait_ge(step, 2 * NT + 2)
        nc.vector.reciprocal(prob[:, 0, :], total[:]).then_inc(step, 1)
        nc.vector.tensor_tensor(one[:], iota.unsqueeze(1).broadcast_to([P, NT, NE]),
                                placef[:, :, 0:1].broadcast_to([P, NT, NE]), ALU.is_equal).then_inc(step, 1)
        nc.vector.tensor_tensor(two[:], iota.unsqueeze(1).broadcast_to([P, NT, NE]),
                                placef[:, :, 1:2].broadcast_to([P, NT, NE]), ALU.is_equal).then_inc(step, 1)
        dve.wait_ge(step, 2 * NT + 3)
        nc.vector.tensor_tensor(prob[:, 1, :], ex[:, :, 1], prob[:, 0, :], ALU.mult).then_inc(step, 1)
        dve.wait_ge(step, 2 * NT + 6)
        nc.vector.tensor_tensor(one[:], one[:], prob[:, 0, :].unsqueeze(2).broadcast_to([P, NT, NE]), ALU.mult).then_inc(step, 1)
        nc.vector.tensor_tensor(two[:], two[:], prob[:, 1, :].unsqueeze(2).broadcast_to([P, NT, NE]), ALU.mult).then_inc(step, 1)
        dve.wait_ge(step, 2 * NT + 8)
        nc.vector.tensor_tensor(weight[:], one[:], two[:], ALU.add).then_inc(weights_ready, 1)
        dve.wait_ge(weights_ready, 1)

    return before, exponent, after, weight


def first_experts(nc, banks, w, xt, x_res, logits, xpos, c):
    with ExitStack() as ctx:
        def sb(name, shape, dt=F32):
            return ctx.enter_context(nc.sbuf_tensor(f"moe_{name}", shape, dt))

        def sem(name):
            return ctx.enter_context(nc.semaphore(f"moe_{name}"))

        xs = sb("xs", [P, P])
        act_out = sb("act_out", [P, NE, P])
        mixed, mixt = sb("mixed", [P, P]), sb("mixt", [P, P])
        norm = Norm(nc, ctx, "moe")
        before, exponent, after, weight = route(nc, ctx, "moe_route", logits, c["iota"], 1.0)
        xs_ready, expert_done, silu_ready = sem("xs_ready"), sem("expert_done"), sem("silu_ready")
        mix_step, mt_done, mt_ready, comb_done = sem("mix_step"), sem("mt_done"), sem("mt_ready"), sem("comb_done")
        back_done, xp_ready = sem("back_done"), sem("xp_ready")
        ps_e, ps_m, ps_y, ps_b = banks[0:2], banks[2], banks[3], banks[4]
        xpos_v = xpos[:].rearrange("f (p s) -> f s p", s=B)
        block = ctx.enter_context(nc.Block())

        @block.tensor
        def _(pe):
            def experts(t):
                pe.wait_ge(xs_ready, t + 1)
                for h in range(2):
                    ge(pe, silu_ready, 2 * (t - 1) + h + 1)
                    cols = slice(CHUNK * h, CHUNK * (h + 1))
                    nc.tensor.matmul(ps_e[h][:], c["ones3"], w["eb3"][:, cols], start=True, stop=False)
                    nc.tensor.matmul(ps_e[h][:], xs[:], w["expert"][:, cols], start=False, stop=True).then_inc(expert_done, 1)

            def mixed_t(t):
                pe.wait_ge(mix_step, NE * (t + 1))
                ge(pe, mt_ready, t)
                nc.tensor.transpose(ps_m[:, 0:P], mixed[:], c["ident"]).then_inc(mt_done, 1)

            def combine(t):
                pe.wait_ge(mt_ready, t + 1)
                ge(pe, norm.y_ready, t)
                nc.tensor.matmul(ps_y[:, 0:P], mixt[:], w["combine"], start=True, stop=True).then_inc(comb_done, 1)

            def back(t):
                pe.wait_ge(norm.normed, t + 1)
                ge(pe, xp_ready, t)
                nc.tensor.transpose(ps_b[:, 0:P], norm.out[:], c["ident"]).then_inc(back_done, 1)

            pipelined(pe, [(-1, combine), (-2, back), (1, experts), (0, mixed_t)])

        @block.scalar
        def _(act):
            exponent(act)

            def silu(t):
                for h in range(2):
                    act.wait_ge(expert_done, 2 * t + h + 1)
                    ge(act, mix_step, NE * (t - 1) + 4 * h + 4)
                    nc.scalar.activation(act_out[:, 4 * h:4 * h + 4, :], ps_e[h][:].rearrange("p (e d) -> p e d", e=4),
                                         ACT.Silu).then_inc(silu_ready, 1)

            def mixed_t(t):
                act.wait_ge(mt_done, t + 1)
                ge(act, comb_done, t)
                nc.scalar.activation(mixt[:], ps_m[:, 0:P], ACT.Copy).then_inc(mt_ready, 1)

            def positions(t):
                act.wait_ge(back_done, t + 1)
                nc.scalar.activation(xpos_v[:, bass.ds(2 * t, 2), :], ps_b[:, 0:P].rearrange("f (s p) -> f s p", s=2),
                                     ACT.Copy).then_inc(xp_ready, 1)

            pipelined(act, [(-1, mixed_t), (-2, positions), (1, silu)])

        @block.vector
        def _(dve):
            before(dve)
            after(dve)

            def mix(t):
                for e in range(NE):
                    if e % 4 == 0:
                        dve.wait_ge(silu_ready, 2 * t + e // 4 + 1)
                    if e == 0:
                        ge(dve, mt_done, t)
                        ins = nc.vector.tensor_scalar(mixed[:], act_out[:, e, :], weight[:, t, e:e + 1], None, ALU.mult)
                    else:
                        dve.wait_ge(mix_step, NE * t + e)
                        ins = nc.vector.scalar_tensor_tensor(mixed[:], act_out[:, e, :], weight[:, t, e:e + 1], mixed[:],
                                                             ALU.mult, ALU.add)
                    ins.then_inc(mix_step, 1)

            def statistics(t):
                dve.wait_ge(comb_done, t + 1)
                norm.statistics(dve, t, ps_y[:, 0:P], x_res[:, t, :])

            def scaling(t):
                ge(dve, back_done, t)
                norm.scaling(dve, t)

            pipelined(dve, [(-1, statistics), (0, mix), (-1, scaling)])

        @block.gpsimd
        def _(pool):
            def tokens(t):
                ge(pool, expert_done, 2 * t)
                nc.gpsimd.tensor_copy(xs[:], xt[:, bass.ds(P * t, P)]).then_inc(xs_ready, 1)

            def power(t):
                norm.power(pool, t, c["neghalf"][:, 0:1], c["eps"][:, 0:1])

            pipelined(pool, [(-1, power), (2, tokens)])


def sequence_attention(nc, banks, w, xpos, ct, res, res_next, xt_next, c):
    with ExitStack() as ctx:
        def sb(name, shape, dt=F32):
            return ctx.enter_context(nc.sbuf_tensor(f"seq_{name}", shape, dt))

        def sem(name):
            return ctx.enter_context(nc.semaphore(f"seq_{name}"))

        xg = sb("xg", [P, 2, P])
        q2 = sb("q2", [P, NJ, 4, 2, B])
        kg = sb("kg", [P, NJ, P])
        vg = sb("vg", [P, 2, 4, P])
        qb = sb("qb", [P, 2, NJ, 4])
        score = sb("score", [P, 2, NJ, 2, B])
        prob = sb("prob", [P, 2, NJ, S])
        probn = sb("probn", [P, 2, NJ, S])
        probt = sb("probt", [P, 2, 4, P])
        top, total, rsum = sb("top", [P, 2, NJ]), sb("total", [P, 2, NJ]), sb("rsum", [P, 2, NJ])
        ot = sb("ot", [P, 4, 2, 2, 2, B])
        csum, context = sb("csum", [P, 4, B]), sb("context", [P, P])
        norm = Norm(nc, ctx, "seq")
        ps_p, ps_s, ps_t, ps_o, ps_y = banks[0:2], banks[2:4], banks[4], banks[5:7], banks[7]

        xg_ready, qkv_done, qkv_out = sem("xg_ready"), sem("qkv_done"), sem("qkv_out")
        setup, scores_done, top_ready, score_ready = sem("setup"), sem("scores_done"), sem("top_ready"), sem("score_ready")
        prob_ready, total_ready, rsum_ready, probn_ready = sem("prob_ready"), sem("total_ready"), sem("rsum_ready"), sem("probn_ready")
        transp_done, probt_ready, pv_done, ot_ready = sem("transp_done"), sem("probt_ready"), sem("pv_done"), sem("ot_ready")
        wo_done, rest_done, rest_ready = sem("wo_done"), sem("rest_done"), sem("rest_ready")
        back_done, xt_ready, res_ready = sem("back_done"), sem("xt_ready"), sem("res_ready")
        context_done = sem("context_done")
        block = ctx.enter_context(nc.Block())
        slots = [(n, jj, s) for n in range(2) for jj in range(4) for s in range(2)]

        @block.tensor
        def _(pe):
            def qk(t):
                pe.wait_ge(xg_ready, 2 * t + 1)
                for n in range(4):
                    ge(pe, qkv_out, 8 * t + (-1, 0, 2, 4)[n])
                    for j in range(4):
                        col = P * (4 * n + j)
                        last = nc.tensor.matmul(ps_p[n % 2][:, P * j:P * (j + 1)], w["in"][:, col:col + P], xg[:, 0, :],
                                                start=True, stop=True)
                    last.then_inc(qkv_done, 1)

            def v(t):
                pe.wait_ge(xg_ready, 2 * t + 2)
                for n in range(2):
                    pe.wait_ge(qkv_out, 8 * t + 5 + n)
                    nc.tensor.matmul(ps_p[n][:], xg[:, n, :],
                                     w["in"][:, 2 * H1 * D1:].rearrange("p (j a d) -> p a j d", a=2, d=P)[:, n],
                                     start=True, stop=True).then_inc(qkv_done, 1)

            def scores(t):
                pe.wait_ge(qkv_out, 8 * t + 6)
                for n, jj, s in slots:
                    j = 2 * jj + (s ^ n)
                    if jj == 0 and s == 0:
                        ge(pe, score_ready, 4 * (t - 1) + 2 * n + 2)
                    last = nc.tensor.matmul(ps_s[n][:, S * (2 * jj + s):S * (2 * jj + s + 1)],
                                            q2[:, j, 2 * n:2 * n + 2].rearrange("p b a s -> p (b a s)"),
                                            kg[:, j, S * n:S * (n + 1)], start=True, stop=True)
                    if jj == 3 and s == 1:
                        last.then_inc(scores_done, 1)

            def weighted(t):
                for n in range(2):
                    pe.wait_ge(probn_ready, 2 * t + n + 1)
                    ge(pe, probt_ready, 2 * t + n)
                    if n == 0:
                        ge(pe, xt_ready, t - 1)
                    for j in range(4):
                        last = nc.tensor.transpose(ps_t[:, P * j:P * (j + 1)], probn[:, n, 2 * j:2 * j + 2].rearrange("p a k -> p (a k)"),
                                                   c["ident"])
                    last.then_inc(transp_done, 1)
                for n in range(2):
                    pe.wait_ge(probt_ready, 2 * t + n + 1)
                    pe.wait_ge(qkv_out, 8 * t + 8)
                    ge(pe, ot_ready, 8 * t + 4 * n)
                    for jj in range(4):
                        for s in range(2):
                            rows = slice(64 * s, 64 * (s + 1))
                            last = nc.tensor.matmul(ps_o[s][:, P * jj:P * (jj + 1)], vg[rows, s ^ n, jj, :], probt[rows, n, jj, :],
                                                    start=True, stop=True)
                    last.then_inc(pv_done, 1)

            def project(t):
                pe.wait_ge(ot_ready, 8 * t + 8)
                pe.wait_ge(rest_ready, upto(t + 3, NT))
                ge(pe, norm.y_ready, t)
                for j in range(NJ):
                    last = nc.tensor.matmul(ps_y[:, 0:P], ot[:, j // 2, j % 2].rearrange("p n b s -> p (n b s)"), w["out"][:, j, :],
                                            start=j == 0, stop=j == NJ - 1)
                last.then_inc(wo_done, 1)

            def residual_t(t):
                pe.wait_ge(xg_ready, 2 * t + 1)
                ge(pe, rest_ready, t)
                ge(pe, norm.y_ready, t - 2)
                nc.tensor.transpose(ps_y[:, P:2 * P], xg[:, 0, :], c["ident"]).then_inc(rest_done, 1)

            def back(t):
                pe.wait_ge(norm.normed, t + 1)
                pe.wait_ge(probt_ready, upto(2 * (t + 2), 2 * NT))
                ge(pe, xt_ready, t)
                nc.tensor.transpose(ps_t[:, 0:P], norm.out[:], c["ident"]).then_inc(back_done, 1)

            pe.wait_ge(setup, 5)
            nc.tensor.matmul(ps_s[0][:, 0:P], csum[:].rearrange("f r b -> f (r b)"), w["x_w2"], start=True, stop=True
                             ).then_inc(context_done, 1)
            pe.wait_ge(setup, 6)
            pipelined(pe, [(1, residual_t), (1, qk), (-1, project), (-2, back), (0, weighted), (1, v), (1, scores)])

        @block.vector
        def _(dve):
            nc.vector.memset(score[:], MASKED).then_inc(setup, 1)
            nc.vector.tensor_scalar(qb[:, 0], w["in_b"][:, 0:NJ].unsqueeze(2).broadcast_to([P, NJ, 4]), c["h2"][:, 0:1], None, ALU.mult).then_inc(setup, 1)
            nc.vector.tensor_scalar(qb[:, 1], w["in_b"][:, 0:NJ].unsqueeze(2).broadcast_to([P, NJ, 4]), c["h2"][:, 1:2], None, ALU.mult).then_inc(setup, 1)
            nc.vector.reduce_sum(csum[:, 0, :], ct.rearrange("f (b s) -> f b s", b=B), axis=AX.X).then_inc(setup, 1)
            dve.wait_ge(setup, 4)
            nc.vector.tensor_copy(csum[:, 1:4, :], csum[:, 0:1, :].broadcast_to([P, 3, B])).then_inc(setup, 1)
            dve.wait_ge(context_done, 1)
            nc.vector.scalar_tensor_tensor(context[:], ps_s[0][:, 0:P], 1.0 / S, w["x_b"], ALU.mult, ALU.add).then_inc(setup, 1)
            dve.wait_ge(setup, 6)

            def residual(t):
                dve.wait_ge(rest_done, t + 1)
                nc.vector.tensor_tensor(res[:, t, :], ps_y[:, P:2 * P], w["out_b"], ALU.add).then_inc(rest_ready, 1)

            def qk(t):
                for n in range(4):
                    src = ps_p[n % 2][:].rearrange("p (j s) -> p j s", s=B)
                    dve.wait_ge(qkv_done, 6 * t + n + 1)
                    if n < 2:
                        ge(dve, scores_done, 2 * t)
                        for a in range(2):
                            bias = qb[:, a, 4 * n:4 * n + 4].rearrange("p j b -> p (j b)").unsqueeze(2).broadcast_to([P, 16, B])
                            nc.vector.scalar_tensor_tensor(q2[:, 4 * n:4 * n + 4, :, a, :].rearrange("p j b s -> p (j b) s"), src, c["h2"][:, a:a + 1], bias,
                                                           ALU.mult, ALU.add).then_inc(qkv_out, 1)
                    else:
                        jj = 4 * (n - 2)
                        bias = w["in_b"][:, NJ + jj:NJ + jj + 4].unsqueeze(2).broadcast_to([P, 4, P])
                        nc.vector.tensor_tensor(kg[:, jj:jj + 4, :], ps_p[n % 2][:].rearrange("p (j s) -> p j s", j=4), bias,
                                                ALU.add).then_inc(qkv_out, 1)

            def v(t):
                for n in range(2):
                    dve.wait_ge(qkv_done, 6 * t + 5 + n)
                    ge(dve, pv_done, 2 * t)
                    nc.vector.tensor_tensor(vg[:, n], ps_p[n][:].rearrange("p (j d) -> p j d", j=4),
                                            w["v_b"].rearrange("p (j a d) -> p a j d", a=2, d=P)[:, n], ALU.add).then_inc(qkv_out, 1)

            def softmax(t):
                for n in range(2):
                    dve.wait_ge(scores_done, 2 * t + n + 1)
                    ge(dve, prob_ready, 2 * (t - 1) + n + 1)
                    for b in range(2):
                        rows = slice(64 * b, 64 * (b + 1))
                        src = ps_s[n][rows].rearrange("p (j b s) -> p j b s", j=NJ, b=2)[:, :, b, :]
                        ge(dve, score_ready, 4 * (t - 1) + 2 * n + b + 1)
                        nc.vector.reduce_max(top[rows, n, :], src, axis=AX.X).then_inc(top_ready, 1)
                    for b in range(2):
                        rows = slice(64 * b, 64 * (b + 1))
                        src = ps_s[n][rows].rearrange("p (j b s) -> p j b s", j=NJ, b=2)[:, :, b, :]
                        dve.wait_ge(top_ready, 4 * t + 2 * n + b + 1)
                        nc.vector.tensor_tensor(score[rows, n, :, b, :], src, top[rows, n, :].unsqueeze(2).broadcast_to([64, NJ, B]),
                                                ALU.subtract).then_inc(score_ready, 1)

            def sums(t):
                for n in range(2):
                    dve.wait_ge(prob_ready, 2 * t + n + 1)
                    ge(dve, probn_ready, 2 * (t - 1) + n + 1)
                    nc.vector.reduce_sum(total[:, n, :], prob[:, n], axis=AX.X).then_inc(total_ready, 1)
                    dve.wait_ge(total_ready, 2 * t + n + 1)
                    nc.vector.reciprocal(rsum[:, n, :], total[:, n, :]).then_inc(rsum_ready, 1)

            def statistics(t):
                dve.wait_ge(wo_done, t + 1)
                norm.statistics(dve, t, ps_y[:, 0:P], res[:, t, :])

            def scaling(t):
                ge(dve, back_done, t)
                ge(dve, res_ready, t)
                norm.scaling(dve, t)

            pipelined(dve, [(1, residual), (1, qk), (-1, statistics), (-1, scaling), (1, v), (1, softmax), (1, sums)])

        @block.scalar
        def _(act):
            def exponent(t):
                for n in range(2):
                    act.wait_ge(score_ready, 4 * t + 2 * n + 2)
                    ge(act, probn_ready, 2 * (t - 1) + n + 1)
                    nc.scalar.activation(prob[:, n], score[:, n].rearrange("p j b s -> p j (b s)"), ACT.Exp).then_inc(prob_ready, 1)

            def probs_t(t):
                for n in range(2):
                    act.wait_ge(transp_done, 2 * t + n + 1)
                    ge(act, pv_done, 2 * (t - 1) + n + 1)
                    nc.scalar.activation(probt[:, n], ps_t[:].rearrange("p (j q) -> p j q", j=4), ACT.Copy).then_inc(probt_ready, 1)

            def outputs_t(t):
                for n in range(2):
                    act.wait_ge(pv_done, 2 * t + n + 1)
                    ge(act, wo_done, t)
                    for s in range(2):
                        for a in range(2):
                            rows = slice(64 * a, 64 * (a + 1))
                            src = ps_o[s][rows].rearrange("p (j b a s) -> p j b a s", j=4, b=2, a=2)[:, :, :, a, :]
                            nc.scalar.activation(ot[rows, :, s ^ n, n], src, ACT.Copy).then_inc(ot_ready, 1)

            def feature_major(t):
                act.wait_ge(back_done, t + 1)
                nc.scalar.activation(xt_next[:, bass.ds(P * t, P)], ps_t[:, 0:P], ACT.Copy).then_inc(xt_ready, 1)

            pipelined(act, [(-2, feature_major), (0, probs_t), (0, outputs_t), (1, exponent)])

        @block.gpsimd
        def _(pool):
            def tokens(t):
                ge(pool, scores_done, 2 * t)
                for n in range(2):
                    src = xpos[:, bass.ds(P * t, P)]
                    if n == 0:
                        nc.gpsimd.tensor_copy(xg[:, 0, :], src).then_inc(xg_ready, 1)
                    else:
                        nc.gpsimd.tensor_copy(xg[:, 1, 0:S], xpos[:, bass.ds(P * t + S, S)])
                        nc.gpsimd.tensor_copy(xg[:, 1, S:P], xpos[:, bass.ds(P * t, S)]).then_inc(xg_ready, 1)

            def normalise(t):
                for n in range(2):
                    pool.wait_ge(rsum_ready, 2 * t + n + 1)
                    ge(pool, transp_done, 2 * (t - 1) + n + 1)
                    nc.gpsimd.tensor_tensor(probn[:, n], prob[:, n], rsum[:, n, :].unsqueeze(2).broadcast_to([P, NJ, S]),
                                            ALU.mult).then_inc(probn_ready, 1)

            def power(t):
                norm.power(pool, t, c["neghalf"][:, 0:1], c["eps"][:, 0:1])

            def keep_residual(t):
                pool.wait_ge(norm.normed, t + 1)
                nc.gpsimd.tensor_tensor(res_next[:, t, :], norm.out[:], context[:], ALU.add).then_inc(res_ready, 1)

            pool.wait_ge(setup, 6)
            pipelined(pool, [(-1, power), (-1, keep_residual), (1, normalise), (2, tokens)])
            pool.wait_ge(res_ready, NT)


def position_linear(nc, banks, w, xt, x_res, logits, xn_next, res_next, c):
    with ExitStack() as ctx:
        def sb(name, shape, dt=F32):
            return ctx.enter_context(nc.sbuf_tensor(f"lin_{name}", shape, dt))

        def sem(name):
            return ctx.enter_context(nc.semaphore(f"lin_{name}"))

        xs, xnt = sb("xs", [P, P]), sb("xnt", [P, P])
        outer, inner = Norm(nc, ctx, "lin_outer"), Norm(nc, ctx, "lin_inner")
        xs_ready, lin_done, back_done, xnt_ready = sem("xs_ready"), sem("lin_done"), sem("back_done"), sem("xnt_ready")
        xn_ready, gate_done, gate_out, kept = sem("xn_ready"), sem("gate_done"), sem("gate_out"), sem("kept")
        ps_y, ps_b, ps_g = banks[0], banks[1], banks[2]
        block = ctx.enter_context(nc.Block())

        @block.tensor
        def _(pe):
            def linear(t):
                pe.wait_ge(xs_ready, t + 1)
                ge(pe, outer.y_ready, t)
                nc.tensor.matmul(ps_y[:, 0:P], xs[:], w["x_w1"], start=True, stop=True).then_inc(lin_done, 1)

            def back(t):
                pe.wait_ge(inner.normed, t + 1)
                ge(pe, xn_ready, t)
                nc.tensor.transpose(ps_b[:, 0:P], inner.out[:], c["ident"]).then_inc(back_done, 1)

            def gate(t):
                pe.wait_ge(xnt_ready, t + 1)
                ge(pe, gate_out, t)
                nc.tensor.matmul(ps_g[:, 0:NE], xnt[:], w["router"], start=True, stop=True).then_inc(gate_done, 1)

            pipelined(pe, [(1, linear), (-1, back), (-2, gate)])

        @block.vector
        def _(dve):
            def statistics(t):
                dve.wait_ge(lin_done, t + 1)
                outer.statistics(dve, t, ps_y[:, 0:P], x_res[:, t, :])

            def inner_scaling(t):
                ge(dve, back_done, t)
                inner.scaling(dve, t, outer.out[:])

            def scaling(t):
                ge(dve, inner.normed, t)
                ge(dve, kept, t)
                outer.scaling(dve, t)

            def inner_statistics(t):
                dve.wait_ge(outer.normed, t + 1)
                inner.moments(dve, t, outer.out[:])

            pipelined(dve, [(0, statistics), (-1, inner_scaling), (0, scaling), (0, inner_statistics)])

        @block.scalar
        def _(act):
            def feature_major(t):
                act.wait_ge(back_done, t + 1)
                ge(act, gate_done, t)
                nc.scalar.activation(xnt[:], ps_b[:, 0:P], ACT.Identity, bias=w["beta"], scale=w["gamma"]).then_inc(xnt_ready, 1)
                nc.scalar.activation(xn_next[:, bass.ds(P * t, P)], ps_b[:, 0:P], ACT.Identity, bias=w["beta"],
                                     scale=w["gamma"]).then_inc(xn_ready, 1)

            def gate_logits(t):
                act.wait_ge(gate_done, t + 1)
                nc.scalar.activation(logits[:, t, :], ps_g[:, 0:NE], ACT.Copy).then_inc(gate_out, 1)

            pipelined(act, [(-1, feature_major), (-2, gate_logits)])

        @block.gpsimd
        def _(pool):
            def tokens(t):
                ge(pool, lin_done, t)
                nc.gpsimd.tensor_copy(xs[:], xt[:, bass.ds(P * t, P)]).then_inc(xs_ready, 1)

            def powers(t):
                outer.power(pool, t, c["neghalf"][:, 0:1], c["eps"][:, 0:1])
                inner.power(pool, t, c["neghalf"][:, 0:1], c["eps"][:, 0:1])

            def keep(t):
                nc.gpsimd.tensor_tensor(res_next[:, t, :], outer.out[:], outer.out[:], ALU.add).then_inc(kept, 1)

            pipelined(pool, [(0, powers), (0, keep), (2, tokens)])
            pool.wait_ge(kept, NT)


def last_experts(nc, banks, w1_dram, w2_dram, xn, acc, logits, out_dram, c):
    with ExitStack() as ctx:
        def sb(name, shape, dt=F32):
            return ctx.enter_context(nc.sbuf_tensor(f"ffn_{name}", shape, dt))

        def sem(name):
            return ctx.enter_context(nc.semaphore(f"ffn_{name}"))

        w1 = sb("w1", [P, 2, FF])
        w2 = sb("w2", [P, 2, NF, P])
        ht = sb("ht", [P, 2, NF, CHUNK])
        yout = sb("yout", [P, NT, P])
        norm = Norm(nc, ctx, "ffn")
        before, exponent, after, weight = route(nc, ctx, "ffn_route", logits, c["iota"], ROUTER_TEMP)
        w_in = [sem(f"w_in{k}") for k in range(2)]
        hid_done, silu_ready, out_done, acc_ready, out_sent = sem("hid_done"), sem("silu_ready"), sem("out_done"), sem("acc_ready"), sem("out_sent")
        ps_h, ps_z = banks[0:2], banks[2:4]
        CH = B * S // CHUNK
        block = ctx.enter_context(nc.Block())

        def experts(engine, pair):
            pair(0)
            with engine.Fori(1, NE // 2 - 1) as i:
                pair(i)
            pair(NE // 2 - 1)

        @block.sync
        def _(sp):
            for e in range(NE):
                ge(sp, out_done, CH * (e - 1))
                ge(sp, w_in[e % 2], 32 * (e // 2))
                sp.dma_start(w1[:, e % 2, :], w1_dram[e]).then_inc(w_in[e % 2], 16)
                sp.dma_start(w2[:, e % 2], w2_dram[e].rearrange("(f p) d -> p f d", p=P)).then_inc(w_in[e % 2], 16)
            for t in range(NT):
                sp.wait_ge(norm.normed, t + 1)
                sp.dma_start(out_dram[:, 4 * t:4 * t + 4, :].rearrange("s p d -> p s d"), yout[:, t, :]).then_inc(out_sent, 16)
            sp.wait_ge(out_sent, 16 * NT)

        @block.tensor
        def _(pe):
            def hidden(i, k, ch):
                q = 2 * CH * i + CH * k + ch
                pe.wait_ge(w_in[k], 32 * (i + 1))
                for f in range(NF):
                    ge(pe, silu_ready, NF * q + f - 1)
                    nc.tensor.matmul(ps_h[f % 2][:], w1[:, k, P * f:P * (f + 1)], xn[:, CHUNK * ch:CHUNK * (ch + 1)],
                                     start=True, stop=True).then_inc(hid_done, 1)

            def output(i, k, ch):
                q = 2 * CH * i + CH * k + ch
                pe.wait_ge(silu_ready, NF * (q + 1))
                ge(pe, acc_ready, q - 1)
                for tt in range(4):
                    for f in range(NF):
                        last = nc.tensor.matmul(ps_z[q_parity(ch)][:, P * tt:P * (tt + 1)], ht[:, q_parity(ch), f, P * tt:P * (tt + 1)],
                                                w2[:, k, f, :], start=f == 0, stop=f == NF - 1)
                last.then_inc(out_done, 1)

            def pair(i):
                for u in range(2 * CH):
                    if u < 2 * CH - 1:
                        hidden(i, (u + 1) // CH, (u + 1) % CH)
                    elif not isinstance(i, int) or i < NE // 2 - 1:
                        hidden(i + 1, 0, 0)
                    output(i, u // CH, u % CH)

            hidden(0, 0, 0)
            experts(pe, pair)

        @block.scalar
        def _(act):
            exponent(act)

            def pair(i):
                for u in range(2 * CH):
                    q = 2 * CH * i + u
                    ge(act, out_done, q - 1)
                    for f in range(NF):
                        act.wait_ge(hid_done, NF * q + f + 1)
                        nc.scalar.activation(ht[:, u % 2, f, :], ps_h[f % 2][:], ACT.Silu).then_inc(silu_ready, 1)

            experts(act, pair)

        @block.vector
        def _(dve):
            before(dve)
            after(dve)

            def pair(i):
                for u in range(2 * CH):
                    q = 2 * CH * i + u
                    dve.wait_ge(out_done, q + 1)
                    ge(dve, acc_ready, q - CH + 1)
                    for tt in range(4):
                        t = 4 * (u % CH) + tt
                        e = 2 * i + u // CH
                        last = nc.vector.scalar_tensor_tensor(acc[:, t, :], ps_z[u % 2][:, P * tt:P * (tt + 1)],
                                                              weight[:, t, bass.ds(e, 1)], acc[:, t, :], ALU.mult, ALU.add)
                    last.then_inc(acc_ready, 1)

            experts(dve, pair)

            def statistics(t):
                if isinstance(t, int) and t == 0:
                    dve.wait_ge(acc_ready, CH * NE)
                ge(dve, norm.normed, t)
                norm.moments(dve, t, acc[:, t, :])

            def scaling(t):
                norm.scaling(dve, t, acc[:, t, :], yout[:, t, :])

            pipelined(dve, [(0, statistics), (0, scaling)])

        @block.gpsimd
        def _(pool):
            pipelined(pool, [(0, lambda t: norm.power(pool, t, c["neghalf"][:, 0:1], c["eps"][:, 0:1]))])


def q_parity(ch):
    return ch % 2


def build(nc, a, out_dram):
    with ExitStack() as ctx:
        def sb(name, shape, dt=F32):
            return ctx.enter_context(nc.sbuf_tensor(name, shape, dt))

        banks = [ctx.enter_context(nc.psum_tensor(f"bank{n}", [P, CHUNK], F32)) for n in range(8)]
        xt_a, xt_b, ct = sb("xt_a", [P, B * S]), sb("xt_b", [P, B * S]), sb("ct", [P, B * S])
        res_a, res_b = sb("res_a", [P, NT, P]), sb("res_b", [P, NT, P])
        logits = sb("logits", [P, NT, NE])
        shapes = {name: list(ap.shape) for name, ap in a.items()}
        held = {}
        for name in a:
            if name in ("x", "xt", "ct", "w1", "w2"):
                continue
            held[name] = sb(f"w_{name}", shapes[name])
        eb3 = sb("eb3", [3, NE * P], BF16)
        ones3 = sb("ones3", [3, P], BF16)

        loaded = ctx.enter_context(nc.semaphore("loaded"))
        split = ctx.enter_context(nc.semaphore("split"))
        with ExitStack() as parts:
            part = [parts.enter_context(nc.sbuf_tensor(f"eb_part{n}", [3, NE * P], F32)) for n in range(3)]
            short = [parts.enter_context(nc.sbuf_tensor(f"eb_short{n}", [3, NE * P], BF16)) for n in range(3)]
            block = parts.enter_context(nc.Block())

            @block.sync
            def _(sp):
                sp.dma_start(xt_a[:], a["xt"]).then_inc(loaded, 16)
                sp.dma_start(ct[:], a["ct"]).then_inc(loaded, 16)
                sp.dma_start(res_a[:], a["x"].rearrange("(t p) d -> p t d", p=P)).then_inc(loaded, 16)
                for name in held:
                    sp.dma_start(held[name][:], a[name]).then_inc(loaded, 16)
                sp.wait_ge(loaded, 16 * (len(held) + 3))

            @block.vector
            def _(dve):
                dve.wait_ge(loaded, 16 * (len(held) + 3))
                n = 0
                nc.vector.memset(ones3[:], 1.0)
                for k in range(3):
                    src = held["eb"][:] if k == 0 else part[k - 1][:]
                    if n:
                        dve.wait_ge(split, n)
                    nc.vector.tensor_copy(short[k][:], src).then_inc(split, 1)
                    n += 1
                    dve.wait_ge(split, n)
                    nc.vector.tensor_tensor(part[k][:], src, short[k][:], ALU.subtract).then_inc(split, 1)
                    n += 1
                sel = held["third"]
                dve.wait_ge(split, n)
                nc.vector.tensor_scalar(eb3[:], short[0][:], sel[:, 0:1], None, ALU.mult).then_inc(split, 1)
                for k in (1, 2):
                    n += 1
                    dve.wait_ge(split, n)
                    nc.vector.scalar_tensor_tensor(eb3[:], short[k][:], sel[:, k:k + 1], eb3[:], ALU.mult, ALU.add).then_inc(split, 1)

        h = {name: t[:] for name, t in held.items()}
        c = {name: h[name] for name in ("ident", "pair", "half", "first", "second", "both", "neghalf", "eps", "iota", "h2")}
        c["parity"] = h["parity"]
        c["ones3"] = ones3[:]
        with ExitStack() as keys:
            km = keys.enter_context(nc.sbuf_tensor("km", [P, B, CHUNK], F32))
            vb = keys.enter_context(nc.sbuf_tensor("vb", [P, B, 4, 2, VD + 1], F32))
            w = {"q": h["self_q"], "k": h["self_k"], "v": h["self_v"], "o": h["self_o"], "qb": None, "kb": None,
                 "lam": h["lam"], "og": h["ln_g"], "ob": h["ln_b"], "next_bias": h["cross_ob"]}
            pair_attention(nc, banks, True, w, xt_a, xt_a, km, vb, lambda t: res_a[:, t, :], res_b, xt_b, c)
            w = {"q": h["cross_q"], "k": h["cross_k"], "v": h["cross_v"], "o": h["cross_o"], "qb": h["cross_qb"],
                 "kb": h["cross_kb"], "vb": h["cross_vb"], "gate": h["gate"]}
            pair_attention(nc, banks, False, w, xt_b, ct, km, vb, lambda t: res_b[:, t, :], res_a, xt_a, c, logits)
        w = {"eb3": eb3[:], "expert": h["expert"], "combine": h["combine"]}
        first_experts(nc, banks, w, xt_a, res_a, logits, xt_b, c)
        w = {"in": h["in"], "in_b": h["in_b"], "v_b": h["v_b"], "out": h["out"], "out_b": h["out_b"],
             "x_w2": h["x_w2"], "x_b": h["x_b"]}
        sequence_attention(nc, banks, w, xt_b, ct[:], res_a, res_b, xt_a, c)
        w = {"x_w1": h["x_w1"], "router": h["router"], "gamma": h["gamma"], "beta": h["beta"]}
        position_linear(nc, banks, w, xt_a, res_b, logits, xt_b, res_a, c)
        last_experts(nc, banks, a["w1"], a["w2"], xt_b, res_a, logits, out_dram, c)


def constants():
    p = np.arange(P)
    f = lambda x: np.ascontiguousarray(x, dtype=np.float32)
    token = np.arange(P)
    place = np.stack([(token[None, :] == S * u + p[:, None] % S) for u in range(2)], axis=1)
    par = (p // S)[:, None, None]
    return {
        "ident": f(np.eye(P)),
        "pair": f(p[:, None] // VD == np.arange(NPAIR)),
        "parity": f(((p // HD) % 2)[:, None] == np.arange(2)) * np.float32(HD ** -0.5),
        "half": f((p // S)[:, None] == np.arange(2)),
        "first": f(place & (par == 0)),
        "second": -f(place & (par == 1)),
        "both": f(p[:, None] % S == np.arange(S)),
        "neghalf": f(np.full((P, NE), -0.5)),
        "eps": f(np.full((P, NE), LN_EPS)),
        "iota": f(np.broadcast_to(np.arange(NE), (P, NE))),
        "h2": f((p // D1)[:, None] == np.arange(2)) * np.float32(D1 ** -0.5),
        "third": f(np.eye(3)),
    }


def kernel(**inputs):
    import concourse.bacc as bacc
    from concourse.bass_utils import run_bass_kernel_spmd

    v = {name: np.asarray(x) for name, x in inputs.items()}
    rows = lambda x, n=P: np.broadcast_to(x.reshape(1, -1), (n, x.size))
    col = lambda x: x.reshape(-1, P).T
    arrays = {
        "x": v["x"].reshape(B * S, E),
        "xt": v["x"].reshape(B * S, E).T,
        "ct": v["ctx_1024"].reshape(B * S, E).T,
        "self_q": v["L0_attn_Wq"], "self_k": v["L0_attn_Wk"], "self_v": v["L0_attn_Wv"], "self_o": v["L0_attn_Wo"],
        "lam": np.broadcast_to(np.stack([v["L0_attn_lq1"], v["L0_attn_lq2"], v["L0_attn_lk1"], v["L0_attn_lk2"]]), (P, 4, HD)),
        "ln_g": np.tile(v["L0_attn_ln_g"], NPAIR).reshape(P, 1), "ln_b": np.tile(v["L0_attn_ln_b"], NPAIR).reshape(P, 1),
        "cross_q": v["L0_xattn_wq_w"].T, "cross_k": v["L0_xattn_wk_w"].T, "cross_v": v["L0_xattn_wv_w"].T,
        "cross_o": v["L0_xattn_wo_w"].T, "cross_qb": col(v["L0_xattn_wq_b"]), "cross_kb": col(v["L0_xattn_wk_b"]),
        "cross_vb": col(v["L0_xattn_wv_b"]), "cross_ob": rows(v["L0_xattn_wo_b"]),
        "gate": v["L0_ffn_gate_w"].T,
        "expert": v["L0_ffn_expert_w"].transpose(2, 0, 1).reshape(E, NE * E),
        "eb": rows(v["L0_ffn_expert_b"], 3), "combine": v["L0_ffn_combine_w"].T,
        "in": v["L1_attn_in_proj_weight"].T, "in_b": col(v["L1_attn_in_proj_bias"]),
        "v_b": rows(v["L1_attn_in_proj_bias"][2 * H1 * D1:]),
        "out": v["L1_attn_out_proj_weight"].T.reshape(NJ, P, E).transpose(1, 0, 2),
        "out_b": rows(v["L1_attn_out_proj_bias"]),
        "x_w1": v["L1_xattn_W"][:, :E].T, "x_w2": v["L1_xattn_W"][:, E:].T, "x_b": rows(v["L1_xattn_b"]),
        "gamma": col(v["L1_ffn_gamma"]), "beta": col(v["L1_ffn_beta"]), "router": v["L1_ffn_router_w"].T,
        "w1": v["L1_ffn_W1"], "w2": v["L1_ffn_W2"],
    }
    arrays.update(constants())
    arrays = {name: np.ascontiguousarray(x) for name, x in arrays.items()}
    nc = bacc.Bacc("TRN2", target_bir_lowering=False, num_devices=1)
    a = {name: nc.dram_tensor(f"in_{name}", x.shape, mybir.dt.from_np(x.dtype), kind="ExternalInput").ap()
         for name, x in arrays.items()}
    out = nc.dram_tensor("out", (B, S, E), F32, kind="ExternalOutput").ap()
    build(nc, a, out)
    r = run_bass_kernel_spmd(nc, [{f"in_{name}": x for name, x in arrays.items()}], core_ids=[0])
    return r.results[0]["out"]
```

```python
from contextlib import ExitStack

import numpy as np

import concourse.bass as bass
from concourse import mybir

F32 = mybir.dt.float32
BF16 = mybir.dt.bfloat16
U32 = mybir.dt.uint32
ACT = mybir.ActivationFunctionType
ALU = mybir.AluOpType
AX = mybir.AxisListType

P = 128
B, S, E = 32, 64, 128
NT = B * S // P
LN_EPS = 1e-5
CHUNK = 512

NPAIR, HD, VD = 8, 8, 16
H1, D1 = 16, 64
NJ = H1 // 2
NE = 8
FF = 512
NF = FF // P
LAM_INIT = 0.8 - 0.6 * float(np.exp(-0.3 * 12))
ROUTER_TEMP = 1.5
MASKED = -1e30


def ge(engine, semaphore, value):
    if not isinstance(value, int) or value > 0:
        engine.wait_ge(semaphore, value)


def upto(value, most):
    return min(value, most) if isinstance(value, int) else value


def pipelined(engine, parts, n=NT):
    most, least = max(lag for lag, _ in parts), min(lag for lag, _ in parts)

    def step(i, parity):
        for lag, part in parts:
            if not isinstance(i, int) or 0 <= i + lag < n:
                part(i + lag, (parity + lag) % 2)

    lo, hi = 2 - least, n - most
    hi -= (hi - lo) % 2
    for i in range(-most, lo):
        step(i, i % 2)
    with engine.Fori(lo, hi - 1, 2) as i:
        step(i, lo % 2)
        step(i + 1, (lo + 1) % 2)
    for i in range(hi, n - least):
        step(i, i % 2)


class Norm:

    def __init__(self, nc, ctx, tag):
        self.nc = nc
        sb = lambda name, shape: ctx.enter_context(nc.sbuf_tensor(f"{tag}_{name}", shape, F32))
        sem = lambda name: ctx.enter_context(nc.semaphore(f"{tag}_{name}"))
        self.y, self.out = sb("y", [P, P]), sb("normed", [P, P])
        self.stats, self.mv, self.rstd = sb("stats", [P, 6]), sb("mv", [P, 2]), sb("rstd", [P, 2])
        self.y_ready, self.stats_ready, self.mv_ready = sem("y_ready"), sem("stats_ready"), sem("mv_ready")
        self.rstd_ready, self.normed = sem("rstd_ready"), sem("normed_ready")

    def statistics(self, dve, t, src, residual):
        nc = self.nc
        ge(dve, self.normed, t)
        nc.vector.tensor_tensor(self.y[:], src, residual, ALU.add).then_inc(self.y_ready, 1)
        dve.wait_ge(self.y_ready, t + 1)
        self.moments(dve, t, self.y[:])

    def moments(self, dve, t, src):
        nc = self.nc
        nc.vector.bn_stats(self.stats[:], src).then_inc(self.stats_ready, 1)
        dve.wait_ge(self.stats_ready, t + 1)
        dve.nop(nofuse=True)
        nc.vector.bn_aggr(self.mv[:], self.stats[:]).then_inc(self.mv_ready, 1)

    def power(self, pool, t, neghalf, eps):
        nc = self.nc
        pool.wait_ge(self.mv_ready, t + 1)
        ge(pool, self.normed, t)
        nc.gpsimd.tensor_tensor(self.rstd[:, 0:1], self.mv[:, 1:2], eps, ALU.add).then_inc(self.rstd_ready, 1)
        pool.wait_ge(self.rstd_ready, 2 * t + 1)
        nc.gpsimd.tensor_tensor(self.rstd[:, 1:2], self.rstd[:, 0:1], neghalf, ALU.pow).then_inc(self.rstd_ready, 1)

    def scaling(self, dve, t, src=None, dst=None):
        dve.wait_ge(self.rstd_ready, 2 * t + 2)
        self.nc.vector.tensor_scalar(self.out[:] if dst is None else dst, self.y[:] if src is None else src, self.mv[:, 0:1],
                                     self.rstd[:, 1:2], ALU.subtract, ALU.mult).then_inc(self.normed, 1)


def pair_attention(nc, banks, self_diff, w, q_src, kv_src, km, vb, residual, res_next, xt_next, c, logits=None):
    tag = "self" if self_diff else "cross"
    with ExitStack() as ctx:
        def sb(name, shape, dt=F32):
            return ctx.enter_context(nc.sbuf_tensor(f"{tag}_{name}", shape, dt))

        def sem(name):
            return ctx.enter_context(nc.semaphore(f"{tag}_{name}"))

        qt = sb("qt", [P, B * S])
        kt = sb("kt", [P, B * S])
        xdup = sb("xdup", [P, 2, 2, 2, S])
        q2 = sb("q2", [P, 2, 2, 2, S])
        score = sb("score", [P, 2, CHUNK])
        prob = sb("prob", [P, 2, CHUNK])
        probt = sb("probt", [P, 2, CHUNK])
        top = sb("top", [P, 2, NPAIR])
        rsum = sb("rsum", [P, 2, NPAIR])
        rhalf = sb("rhalf", [P, 2, NPAIR, 2])
        on = sb("on", [P, 2, NPAIR, VD])
        ot = sb("ot", [P, P])
        xnt = sb("xnt", [P, P])
        norm = Norm(nc, ctx, tag)
        ps_s, ps_t, ps_o, ps_v, ps_d, ps_a = banks[0:2], banks[2:4], banks[4], banks[5], banks[6], banks[7]

        proj_done, proj_out = sem("proj_done"), sem("proj_out")
        xdup_ready, q2_ready, km_ready = sem("xdup_ready"), sem("q2_ready"), sem("km_ready")
        values_done, scores_done = sem("values_done"), sem("scores_done")
        vb_ready, top_ready, score_ready = sem("vb_ready"), sem("top_ready"), sem("score_ready")
        prob_ready, transp_done, probt_ready = sem("prob_ready"), sem("transp_done"), sem("probt_ready")
        pv_done, rsum_ready, on_ready = sem("pv_done"), sem("rsum_ready"), sem("on_ready")
        comb_done, back_done, ot_ready, xt_ready = sem("comb_done"), sem("back_done"), sem("ot_ready"), sem("xt_ready")
        wo_done, res_ready = sem("wo_done"), sem("res_ready")
        if not self_diff:
            rhalf_ready, xnt_ready, gate_done, gate_out = sem("rhalf_ready"), sem("xnt_ready"), sem("gate_done"), sem("gate_out")
        else:
            ones_ready = sem("ones_ready")
            hn_c = sb("hn_c", [P, NPAIR, VD])
            hn_sq = sb("hn_sq", [P, NPAIR, VD])
            hn_o = sb("hn_o", [P, NPAIR, VD])
            hn_m, hn_v = sb("hn_m", [P, NPAIR]), sb("hn_v", [P, NPAIR])
            hn_r = sb("hn_r", [P, 2, NPAIR])
            comb = sb("comb", [P, 2, P])
            lam_prod, lam = sb("lam_prod", [P, 2, HD]), sb("lam", [P, 5])
            hn_step, hn_var, hn_rstd, hn_done = sem("hn_step"), sem("hn_var"), sem("hn_rstd"), sem("hn_done")
            lam_step, lam_exp, hnt_done = sem("lam_step"), sem("lam_exp"), sem("hnt_done")

        YLAG = -2 if self_diff else -1
        block = ctx.enter_context(nc.Block())

        @block.tensor
        def _(pe):
            for n in range(8):
                src, wgt = (kv_src, w["k"]) if n < 4 else (q_src, w["q"])
                ge(pe, proj_out, n - 1)
                nc.tensor.matmul(ps_s[n % 2][:], wgt, src[:, CHUNK * (n % 4):CHUNK * (n % 4 + 1)],
                                 start=True, stop=True).then_inc(proj_done, 1)
            pe.wait_ge(proj_out, 8)
            if self_diff:
                pe.wait_ge(lam_step, 5)

            def scores(t, p):
                ge(pe, vb_ready, 2 * t)
                pe.wait_ge(xdup_ready, t + 1)
                for u in range(2):
                    nc.tensor.matmul(ps_v[:, P * u:P * (u + 1)], xdup[:, p, u].rearrange("p d s -> p (d s)"), w["v"],
                                     start=True, stop=True).then_inc(values_done, 1)
                pe.wait_ge(q2_ready, 2 * t + 2)
                for u in range(2):
                    pe.wait_ge(km_ready, 2 * t + u + 1)
                    ge(pe, score_ready, 2 * (t - 1) + u + 1)
                    nc.tensor.matmul(ps_s[u][:], q2[:, p, u].rearrange("p d s -> p (d s)"), km[:, 2 * t + u, :],
                                     start=True, stop=True).then_inc(scores_done, 1)

            def transposes(t, p):
                for u in range(2):
                    pe.wait_ge(prob_ready, 2 * t + u + 1)
                    ge(pe, probt_ready, 2 * (t - 1) + u + 1)
                    for j in range(4):
                        last = nc.tensor.transpose(ps_t[u][:, P * j:P * (j + 1)], prob[:, u, P * j:P * (j + 1)], c["ident"])
                    last.then_inc(transp_done, 1)

            def weighted(t, p):
                ge(pe, on_ready, 2 * t)
                for u in range(2):
                    pe.wait_ge(probt_ready, 2 * t + u + 1)
                    pe.wait_ge(vb_ready, 2 * t + u + 1)
                    for j in range(4):
                        last = nc.tensor.matmul(ps_o[:, 136 * u + 34 * j:136 * u + 34 * (j + 1)],
                                                probt[:, u, P * j:P * (j + 1)],
                                                vb[:, 2 * t + u, j].rearrange("p h d -> p (h d)"), start=True, stop=True)
                    last.then_inc(pv_done, 1)

            def combine(t, p):
                pe.wait_ge(on_ready, 2 * t + 2)
                if self_diff:
                    ge(pe, norm.y_ready, t - 1)
                    for u in range(2):
                        last = nc.tensor.matmul(ps_d[:, 0:P], comb[:, u, :], on[:, u].rearrange("p h d -> p (h d)"),
                                                start=u == 0, stop=u == 1)
                else:
                    ge(pe, norm.y_ready, t)
                    for u in range(2):
                        last = nc.tensor.matmul(ps_d[:, S * u:S * (u + 1)], on[:, u].rearrange("p h d -> p (h d)"),
                                                c["both"], start=True, stop=True)
                last.then_inc(comb_done, 1)

            def back(t, p):
                pe.wait_ge(norm.normed, t + 1)
                ge(pe, xt_ready, t)
                if self_diff:
                    pe.wait_ge(ot_ready, t + 1)
                else:
                    ge(pe, gate_out, t)
                nc.tensor.transpose(ps_a[:, 0:P], norm.out[:], c["ident"]).then_inc(back_done, 1)

            def heads_back(t, p):
                pe.wait_ge(hn_done, t + 1)
                ge(pe, ot_ready, t)
                ge(pe, xt_ready, t - 1)
                nc.tensor.transpose(ps_a[:, P:2 * P], hn_o[:].rearrange("p h d -> p (h d)"), c["ident"]).then_inc(hnt_done, 1)

            def project(t, p):
                pe.wait_ge(ot_ready, t + 1)
                if self_diff:
                    pe.wait_ge(hn_step, upto(3 * (t + 1) + 2, 3 * (NT - 1) + 2))
                nc.tensor.matmul(ps_d[:, P:2 * P], ot[:], w["o"], start=True, stop=True).then_inc(wo_done, 1)

            def gate(t, p):
                pe.wait_ge(xnt_ready, t + 1)
                pe.wait_ge(xt_ready, t + 1)
                nc.tensor.matmul(ps_a[:, 2 * P:2 * P + NE], xnt[:], w["gate"], start=True, stop=True).then_inc(gate_done, 1)

            if self_diff:
                pipelined(pe, [(1, scores), (-1, combine), (-3, back), (-2, heads_back), (0, transposes), (-2, project),
                               (0, weighted)])
            else:
                pipelined(pe, [(1, scores), (-1, combine), (-2, back), (0, transposes), (-1, project), (-2, gate),
                               (0, weighted)])

        @block.vector
        def _(dve):
            if self_diff:
                nc.vector.tensor_copy(vb[:, :, :, :, VD].rearrange("p b j h -> p (b j) h"),
                                      c["half"].unsqueeze(1).broadcast_to([P, B * 4, 2])).then_inc(ones_ready, 1)
                nc.vector.tensor_tensor(lam_prod[:], w["lam"][:, 0:2, :], w["lam"][:, 2:4, :], ALU.mult).then_inc(lam_step, 1)
                dve.wait_ge(lam_step, 1)
                nc.vector.reduce_sum(lam[:, 0:2], lam_prod[:], axis=AX.X).then_inc(lam_step, 1)
                dve.wait_ge(lam_exp, 1)
                nc.vector.tensor_scalar(lam[:, 4:5], lam[:, 2:3], lam[:, 3:4], LAM_INIT, ALU.subtract, ALU.add).then_inc(lam_step, 1)
                dve.wait_ge(lam_step, 3)
                for u in range(2):
                    nc.vector.scalar_tensor_tensor(comb[:, u, :], c["second"][:, u, :], lam[:, 4:5], c["first"][:, u, :],
                                                   ALU.mult, ALU.add).then_inc(lam_step, 1)

            def softmax(t, p):
                for u in range(2):
                    pe_tile = ps_s[u][:].rearrange("p (h k) -> p h k", h=NPAIR)
                    dve.wait_ge(scores_done, 2 * t + u + 1)
                    ge(dve, score_ready, 2 * (t - 1) + u + 1)
                    nc.vector.reduce_max(top[:, u, :], pe_tile, axis=AX.X).then_inc(top_ready, 1)
                    dve.wait_ge(top_ready, 2 * t + u + 1)
                    ge(dve, prob_ready, 2 * (t - 1) + u + 1)
                    nc.vector.tensor_tensor(score[:, u].rearrange("p (h k) -> p h k", h=NPAIR), pe_tile,
                                            top[:, u, :].unsqueeze(2).broadcast_to([P, NPAIR, S]),
                                            ALU.subtract).then_inc(score_ready, 1)

            def value_blocks(t, p):
                dve.wait_ge(values_done, 2 * t + 2)
                for u in range(2):
                    nc.vector.tensor_tensor(vb[:, 2 * t + u, :, :, 0:VD],
                                            ps_v[:, P * u:P * (u + 1)].rearrange("p (j h d) -> p j h d", j=4, h=2),
                                            c["half"].unsqueeze(1).unsqueeze(3).broadcast_to([P, 4, 2, VD]),
                                            ALU.mult).then_inc(vb_ready, 1)

            def over_sums(t, p):
                dve.wait_ge(pv_done, 2 * t + 2)
                for u in range(2):
                    o = ps_o[:, 136 * u:136 * (u + 1)].rearrange("p (h d) -> p h d", h=NPAIR)
                    ge(dve, on_ready, 2 * (t - 1) + u + 1)
                    nc.vector.reciprocal(rsum[:, u, :], o[:, :, VD]).then_inc(rsum_ready, 1)
                for u in range(2):
                    o = ps_o[:, 136 * u:136 * (u + 1)].rearrange("p (h d) -> p h d", h=NPAIR)
                    dve.wait_ge(rsum_ready, 2 * t + u + 1)
                    ge(dve, comb_done, t)
                    if self_diff:
                        nc.vector.tensor_tensor(on[:, u], o[:, :, 0:VD], rsum[:, u, :].unsqueeze(2).broadcast_to([P, NPAIR, VD]),
                                                ALU.mult).then_inc(on_ready, 1)
                    else:
                        nc.vector.tensor_tensor(rhalf[:, u], rsum[:, u, :].unsqueeze(2).broadcast_to([P, NPAIR, 2]),
                                                c["half"].unsqueeze(1).broadcast_to([P, NPAIR, 2]), ALU.mult).then_inc(rhalf_ready, 1)
                        dve.wait_ge(rhalf_ready, 2 * t + u + 1)
                        nc.vector.tensor_tensor(on[:, u].rearrange("p h (a d) -> p h a d", a=2),
                                                o[:, :, 0:VD].rearrange("p h (a d) -> p h a d", a=2),
                                                rhalf[:, u].unsqueeze(3).broadcast_to([P, NPAIR, 2, HD]), ALU.mult).then_inc(on_ready, 1)

            def head_centre(t, p):
                d = ps_d[:, 0:P].rearrange("p (h d) -> p h d", h=NPAIR)
                dve.wait_ge(comb_done, t + 1)
                ge(dve, hn_done, t)
                nc.vector.reduce_sum(hn_m[:], d, axis=AX.X).then_inc(hn_step, 1)
                dve.wait_ge(hn_step, 3 * t + 1)
                nc.vector.scalar_tensor_tensor(hn_c[:], hn_m[:].unsqueeze(2).broadcast_to([P, NPAIR, VD]), -1.0 / VD, d,
                                               ALU.mult, ALU.add).then_inc(hn_step, 1)
                dve.wait_ge(hn_step, 3 * t + 2)
                nc.vector.scalar_tensor_tensor(hn_sq[:], hn_c[:], 1.0 / VD, hn_c[:], ALU.mult, ALU.mult).then_inc(hn_step, 1)
                dve.wait_ge(hn_step, 3 * t + 3)
                nc.vector.reduce_sum(hn_v[:], hn_sq[:], axis=AX.X).then_inc(hn_var, 1)

            def head_scale(t, p):
                dve.wait_ge(hn_rstd, 2 * t + 2)
                ge(dve, hnt_done, t)
                nc.vector.tensor_tensor(hn_o[:], hn_c[:], hn_r[:, 1, :].unsqueeze(2).broadcast_to([P, NPAIR, VD]),
                                        ALU.mult).then_inc(hn_done, 1)

            def statistics(t, p):
                dve.wait_ge(wo_done, t + 1)
                norm.statistics(dve, t, ps_d[:, P:2 * P], residual(t))

            def scaling(t, p):
                ge(dve, back_done, t)
                ge(dve, res_ready, t)
                norm.scaling(dve, t)

            if self_diff:
                dve.wait_ge(ones_ready, 1)
                pipelined(dve, [(1, softmax), (-1, head_centre), (1, value_blocks), (-2, statistics), (-1, head_scale),
                                (0, over_sums), (-2, scaling)])
            else:
                pipelined(dve, [(1, softmax), (-1, statistics), (1, value_blocks), (0, over_sums), (-1, scaling)])

        @block.scalar
        def _(act):
            for n in range(8):
                act.wait_ge(proj_done, n + 1)
                dst = (kt if n < 4 else qt)[:, CHUNK * (n % 4):CHUNK * (n % 4 + 1)]
                bias = w["kb"] if n < 4 else w["qb"]
                if bias is None:
                    nc.scalar.activation(dst, ps_s[n % 2][:], ACT.Copy).then_inc(proj_out, 1)
                else:
                    nc.scalar.activation(dst, ps_s[n % 2][:], ACT.Identity, bias=bias).then_inc(proj_out, 1)
            if self_diff:
                act.wait_ge(lam_step, 2)
                nc.scalar.activation(lam[:, 2:4], lam[:, 0:2], ACT.Exp).then_inc(lam_exp, 1)

            def tokens_twice(t, p):
                ge(act, values_done, 2 * (t - 1))
                nc.scalar.activation(xdup[:, p], kv_src[:, bass.ds(P * t, P)].rearrange("p (u s) -> p u s", u=2).unsqueeze(2)
                                     .broadcast_to([P, 2, 2, S]), ACT.Copy).then_inc(xdup_ready, 1)

            def queries(t, p):
                ge(act, scores_done, 2 * (t - 1))
                for a in range(2):
                    nc.scalar.activation(q2[:, p, :, a, :], qt[:, bass.ds(P * t, P)].rearrange("p (u s) -> p u s", u=2),
                                         ACT.Copy, scale=c["parity"][:, a:a + 1]).then_inc(q2_ready, 1)

            def exponent(t, p):
                for u in range(2):
                    act.wait_ge(score_ready, 2 * t + u + 1)
                    ge(act, transp_done, 2 * (t - 1) + u + 1)
                    nc.scalar.activation(prob[:, u, :], score[:, u, :], ACT.Exp).then_inc(prob_ready, 1)

            def probs_t(t, p):
                for u in range(2):
                    act.wait_ge(transp_done, 2 * t + u + 1)
                    ge(act, pv_done, 2 * (t - 1) + u + 1)
                    nc.scalar.activation(probt[:, u, :], ps_t[u][:], ACT.Copy).then_inc(probt_ready, 1)

            def feature_major(t, p):
                act.wait_ge(back_done, t + 1)
                if self_diff:
                    act.wait_ge(hnt_done, upto(t + 2, NT))
                else:
                    ge(act, gate_done, t)
                    nc.scalar.activation(xnt[:], ps_a[:, 0:P], ACT.Copy).then_inc(xnt_ready, 1)
                nc.scalar.activation(xt_next[:, bass.ds(P * t, P)], ps_a[:, 0:P], ACT.Copy).then_inc(xt_ready, 1)

            def outputs_t(t, p):
                if self_diff:
                    act.wait_ge(hnt_done, t + 1)
                    ge(act, wo_done, t)
                    nc.scalar.activation(ot[:], ps_a[:, P:2 * P], ACT.Identity, bias=w["ob"], scale=w["og"]).then_inc(ot_ready, 1)
                else:
                    act.wait_ge(comb_done, t + 1)
                    ge(act, wo_done, t)
                    nc.scalar.activation(ot[:], ps_d[:, 0:P], ACT.Identity, bias=w["vb"]).then_inc(ot_ready, 1)

            def gate_logits(t, p):
                act.wait_ge(gate_done, t + 1)
                nc.scalar.activation(logits[:, t, :], ps_a[:, 2 * P:2 * P + NE], ACT.Copy).then_inc(gate_out, 1)

            if self_diff:
                pipelined(act, [(-3, feature_major), (-2, outputs_t), (0, probs_t), (1, exponent), (2, tokens_twice), (2, queries)])
            else:
                pipelined(act, [(-1, outputs_t), (-2, feature_major), (0, probs_t), (1, exponent), (2, tokens_twice), (2, queries), (-2, gate_logits)])

        @block.gpsimd
        def _(pool):
            pool.wait_ge(proj_out, 4)

            def keys(t, p):
                for u in range(2):
                    nc.gpsimd.tensor_tensor(km[:, 2 * t + u, :].rearrange("p (h k) -> p h k", h=NPAIR),
                                            kt[:, bass.ds(P * t + S * u, S)].unsqueeze(1).broadcast_to([P, NPAIR, S]),
                                            c["pair"].unsqueeze(2).broadcast_to([P, NPAIR, S]), ALU.mult).then_inc(km_ready, 1)

            def head_power(t, p):
                pool.wait_ge(hn_var, t + 1)
                ge(pool, hn_done, t)
                nc.gpsimd.tensor_tensor(hn_r[:, 0, :], hn_v[:], c["eps"], ALU.add).then_inc(hn_rstd, 1)
                pool.wait_ge(hn_rstd, 2 * t + 1)
                nc.gpsimd.tensor_tensor(hn_r[:, 1, :], hn_r[:, 0, :], c["neghalf"], ALU.pow).then_inc(hn_rstd, 1)

            def power(t, p):
                norm.power(pool, t, c["neghalf"][:, 0:1], c["eps"][:, 0:1])

            def keep_residual(t, p):
                pool.wait_ge(norm.normed, t + 1)
                if self_diff:
                    nc.gpsimd.tensor_tensor(res_next[:, t, :], norm.out[:], w["next_bias"], ALU.add).then_inc(res_ready, 1)
                else:
                    nc.gpsimd.tensor_copy(res_next[:, t, :], norm.out[:]).then_inc(res_ready, 1)

            if self_diff:
                pipelined(pool, [(-1, head_power), (-2, power), (3, keys), (-2, keep_residual)])
            else:
                pipelined(pool, [(-1, power), (3, keys), (-1, keep_residual)])
            pool.wait_ge(res_ready, NT)


def route(nc, ctx, tag, logits, iota, temp):
    sb = lambda name, shape, dt=F32: ctx.enter_context(nc.sbuf_tensor(f"{tag}_{name}", shape, dt))
    sem = lambda name: ctx.enter_context(nc.semaphore(f"{tag}_{name}"))
    ranked, ex = sb("ranked", [P, NT, NE]), sb("ex", [P, NT, NE])
    place, placef = sb("place", [P, NT, NE], U32), sb("placef", [P, NT, 2])
    prob = sb("prob", [P, 2, NT])
    total = sb("total", [P, NT])
    one, two, weight = sb("one", [P, NT, NE]), sb("two", [P, NT, NE]), sb("weight", [P, NT, NE])
    step, ready, exped = sem("step"), sem("ready"), sem("exped")
    weights_ready = sem("weights_ready")

    def before(dve):
        for t in range(NT):
            nc.vector.max(ranked[:, t, :], logits[:, t, :]).then_inc(step, 1)
        for t in range(NT):
            dve.wait_ge(step, t + 1)
            nc.vector.max_index(place[:, t, :], ranked[:, t, :], logits[:, t, :]).then_inc(step, 1)
        nc.vector.tensor_tensor(ex[:], ranked[:], ranked[:, :, 0:1].broadcast_to([P, NT, NE]), ALU.subtract).then_inc(ready, 1)

    def exponent(act):
        act.wait_ge(ready, 1)
        nc.scalar.activation(ex[:], ex[:], ACT.Exp, scale=1.0 / temp).then_inc(exped, 1)

    def after(dve):
        dve.wait_ge(step, 2 * NT)
        nc.vector.tensor_copy(placef[:], place[:, :, 0:2]).then_inc(step, 1)
        dve.wait_ge(exped, 1)
        nc.vector.reduce_sum(total[:], ex[:], axis=AX.X).then_inc(step, 1)
        dve.wait_ge(step, 2 * NT + 2)
        nc.vector.reciprocal(prob[:, 0, :], total[:]).then_inc(step, 1)
        nc.vector.tensor_tensor(one[:], iota.unsqueeze(1).broadcast_to([P, NT, NE]),
                                placef[:, :, 0:1].broadcast_to([P, NT, NE]), ALU.is_equal).then_inc(step, 1)
        nc.vector.tensor_tensor(two[:], iota.unsqueeze(1).broadcast_to([P, NT, NE]),
                                placef[:, :, 1:2].broadcast_to([P, NT, NE]), ALU.is_equal).then_inc(step, 1)
        dve.wait_ge(step, 2 * NT + 3)
        nc.vector.tensor_tensor(prob[:, 1, :], ex[:, :, 1], prob[:, 0, :], ALU.mult).then_inc(step, 1)
        dve.wait_ge(step, 2 * NT + 6)
        nc.vector.tensor_tensor(one[:], one[:], prob[:, 0, :].unsqueeze(2).broadcast_to([P, NT, NE]), ALU.mult).then_inc(step, 1)
        nc.vector.tensor_tensor(two[:], two[:], prob[:, 1, :].unsqueeze(2).broadcast_to([P, NT, NE]), ALU.mult).then_inc(step, 1)
        dve.wait_ge(step, 2 * NT + 8)
        nc.vector.tensor_tensor(weight[:], one[:], two[:], ALU.add).then_inc(weights_ready, 1)
        dve.wait_ge(weights_ready, 1)

    return before, exponent, after, weight


def first_experts(nc, banks, w, xt, x_res, logits, xpos, c):
    with ExitStack() as ctx:
        def sb(name, shape, dt=F32):
            return ctx.enter_context(nc.sbuf_tensor(f"moe_{name}", shape, dt))

        def sem(name):
            return ctx.enter_context(nc.semaphore(f"moe_{name}"))

        xs = sb("xs", [P, 2, P])
        act_out = sb("act_out", [P, 2, NE, P])
        mixed = sb("mixed", [P, 2, 2, P])
        mixt = sb("mixt", [P, P])
        norm = Norm(nc, ctx, "moe")
        before, exponent, after, weight = route(nc, ctx, "moe_route", logits, c["iota"], 1.0)
        xs_ready, expert_done, silu_ready = sem("xs_ready"), sem("expert_done"), sem("silu_ready")
        mix_step, mt_done, mt_ready, comb_done = sem("mix_step"), sem("mt_done"), sem("mt_ready"), sem("comb_done")
        back_done, xp_ready = sem("back_done"), sem("xp_ready")
        ps_e, ps_m, ps_y, ps_b = banks[0:4], banks[4], banks[5], banks[6]
        xpos_v = xpos[:].rearrange("f (p s) -> f s p", s=B)
        block = ctx.enter_context(nc.Block())

        @block.tensor
        def _(pe):
            def experts(t, p):
                pe.wait_ge(xs_ready, t + 1)
                for h in range(2):
                    ge(pe, silu_ready, 2 * (t - 2) + h + 1)
                    cols = slice(CHUNK * h, CHUNK * (h + 1))
                    nc.tensor.matmul(ps_e[2 * p + h][:], c["ones3"], w["eb3"][:, cols], start=True, stop=False)
                    nc.tensor.matmul(ps_e[2 * p + h][:], xs[:, p], w["expert"][:, cols], start=False, stop=True).then_inc(expert_done, 1)

            def mixed_t(t, p):
                pe.wait_ge(mix_step, NE * (t + 1))
                ge(pe, mt_ready, t)
                for k in range(2):
                    last = nc.tensor.matmul(ps_m[:, 0:P], mixed[:, p, k], c["ident"], start=k == 0, stop=k == 1)
                last.then_inc(mt_done, 1)

            def combine(t, p):
                pe.wait_ge(mt_ready, t + 1)
                ge(pe, norm.y_ready, t)
                nc.tensor.matmul(ps_y[:, 0:P], mixt[:], w["combine"], start=True, stop=True).then_inc(comb_done, 1)

            def back(t, p):
                pe.wait_ge(norm.normed, t + 1)
                ge(pe, xp_ready, t)
                nc.tensor.transpose(ps_b[:, 0:P], norm.out[:], c["ident"]).then_inc(back_done, 1)

            pipelined(pe, [(-1, combine), (-2, back), (2, experts), (0, mixed_t)])

        @block.scalar
        def _(act):
            exponent(act)

            def silu(t, p):
                for h in range(2):
                    act.wait_ge(expert_done, 2 * t + h + 1)
                    ge(act, mix_step, NE * (t - 2) + 4 * h + 4)
                    nc.scalar.activation(act_out[:, p, 4 * h:4 * h + 4, :], ps_e[2 * p + h][:].rearrange("p (e d) -> p e d", e=4),
                                         ACT.Silu).then_inc(silu_ready, 1)

            def mixed_t(t, p):
                act.wait_ge(mt_done, t + 1)
                ge(act, comb_done, t)
                nc.scalar.activation(mixt[:], ps_m[:, 0:P], ACT.Copy).then_inc(mt_ready, 1)

            def positions(t, p):
                act.wait_ge(back_done, t + 1)
                nc.scalar.activation(xpos_v[:, bass.ds(2 * t, 2), :], ps_b[:, 0:P].rearrange("f (s p) -> f s p", s=2),
                                     ACT.Copy).then_inc(xp_ready, 1)

            pipelined(act, [(-1, mixed_t), (-2, positions), (2, silu)])

        @block.vector
        def _(dve):
            before(dve)
            after(dve)

            def mix(t, p):
                for e in range(NE):
                    if e % 4 == 0:
                        dve.wait_ge(silu_ready, 2 * t + e // 4 + 1)
                    if e == 0:
                        ge(dve, mt_done, t - 1)
                    if e < 2:
                        ins = nc.vector.tensor_scalar(mixed[:, p, e], act_out[:, p, e, :], weight[:, t, e:e + 1], None, ALU.mult)
                    else:
                        dve.wait_ge(mix_step, NE * t + e - 1)
                        ins = nc.vector.scalar_tensor_tensor(mixed[:, p, e % 2], act_out[:, p, e, :], weight[:, t, e:e + 1],
                                                             mixed[:, p, e % 2],
                                                             ALU.mult, ALU.add)
                    ins.then_inc(mix_step, 1)

            def statistics(t, p):
                dve.wait_ge(comb_done, t + 1)
                norm.statistics(dve, t, ps_y[:, 0:P], x_res[:, t, :])

            def scaling(t, p):
                ge(dve, back_done, t)
                norm.scaling(dve, t)

            pipelined(dve, [(-1, statistics), (1, mix), (-1, scaling)])

        @block.gpsimd
        def _(pool):
            def tokens(t, p):
                ge(pool, expert_done, 2 * (t - 1))
                nc.gpsimd.tensor_copy(xs[:, p], xt[:, bass.ds(P * t, P)]).then_inc(xs_ready, 1)

            def power(t, p):
                norm.power(pool, t, c["neghalf"][:, 0:1], c["eps"][:, 0:1])

            pipelined(pool, [(3, tokens), (-1, power)])


def sequence_attention(nc, banks, w, xpos, ct, res, res_next, xt_next, c):
    with ExitStack() as ctx:
        def sb(name, shape, dt=F32):
            return ctx.enter_context(nc.sbuf_tensor(f"seq_{name}", shape, dt))

        def sem(name):
            return ctx.enter_context(nc.semaphore(f"seq_{name}"))

        xg = sb("xg", [P, 2, 2, P])
        q2 = sb("q2", [P, 2, NJ, 4, 2, B])
        kg = sb("kg", [P, 2, NJ, P])
        vg = sb("vg", [P, 2, 2, 4, P])
        qb = sb("qb", [P, 2, NJ, 4])
        score = sb("score", [P, 2, NJ, 2, B])
        prob = sb("prob", [P, 2, NJ, S])
        probn = sb("probn", [P, 2, NJ, S])
        probt = sb("probt", [P, 2, 4, P])
        top, total, rsum = sb("top", [P, 2, NJ]), sb("total", [P, 2, NJ]), sb("rsum", [P, 2, NJ])
        ot = sb("ot", [P, 2, 4, 2, 2, 2, B])
        csum, context = sb("csum", [P, 4, B]), sb("context", [P, P])
        norm = Norm(nc, ctx, "seq")
        ps_p, ps_s, ps_t, ps_o, ps_y = banks[0:2], banks[2:4], banks[4], banks[5:7], banks[7]

        xg_ready, q_done, k_done, v_done = sem("xg_ready"), sem("q_done"), sem("k_done"), sem("v_done")
        q_out, k_out, v_out = sem("q_out"), sem("k_out"), sem("v_out")
        setup, scores_done, top_ready, score_ready = sem("setup"), sem("scores_done"), sem("top_ready"), sem("score_ready")
        prob_ready, total_ready, rsum_ready, probn_ready = sem("prob_ready"), sem("total_ready"), sem("rsum_ready"), sem("probn_ready")
        transp_done, probt_ready, pv_done, ot_ready = sem("transp_done"), sem("probt_ready"), sem("pv_done"), sem("ot_ready")
        wo_done, rest_done, rest_ready = sem("wo_done"), sem("rest_done"), sem("rest_ready")
        back_done, xt_ready, res_ready = sem("back_done"), sem("xt_ready"), sem("res_ready")
        context_done = sem("context_done")
        block = ctx.enter_context(nc.Block())

        @block.tensor
        def _(pe):
            def queries(n):
                def part(t, p):
                    pe.wait_ge(xg_ready, 2 * t + 1)
                    ge(pe, v_out, 2 * t - 1 + n)
                    for j in range(4):
                        col = P * (4 * n + j)
                        last = nc.tensor.matmul(ps_p[n][:, P * j:P * (j + 1)], w["in"][:, col:col + P], xg[:, p, 0, :],
                                                start=True, stop=True)
                    last.then_inc(q_done, 1)
                return part

            def keys(n):
                def part(t, p):
                    pe.wait_ge(q_out, 4 * t + 2 + 2 * n)
                    for j in range(4):
                        col = P * (NJ + 4 * n + j)
                        last = nc.tensor.matmul(ps_p[n][:, P * j:P * (j + 1)], w["in"][:, col:col + P], xg[:, p, 0, :],
                                                start=True, stop=True)
                    last.then_inc(k_done, 1)
                return part

            def values(n):
                def part(t, p):
                    pe.wait_ge(xg_ready, 2 * t + 2)
                    pe.wait_ge(k_out, 8 * t + 4 + 4 * n)
                    nc.tensor.matmul(ps_p[n][:], xg[:, p, n, :],
                                     w["in"][:, 2 * H1 * D1:].rearrange("p (j a d) -> p a j d", a=2, d=P)[:, n],
                                     start=True, stop=True).then_inc(v_done, 1)
                return part

            def scores(t, p):
                pe.wait_ge(q_out, 4 * t + 4)
                pe.wait_ge(k_out, 8 * t + 8)
                for n in range(2):
                    ge(pe, score_ready, 4 * (t - 1) + 2 * n + 2)
                    for jj in range(4):
                        for s in range(2):
                            j = 2 * jj + (s ^ n)
                            last = nc.tensor.matmul(ps_s[n][:, S * (2 * jj + s):S * (2 * jj + s + 1)],
                                                    q2[:, p, j, 2 * n:2 * n + 2].rearrange("p b a s -> p (b a s)"),
                                                    kg[:, p, j, S * n:S * (n + 1)], start=True, stop=True)
                    last.then_inc(scores_done, 1)

            def transposes(n):
                def part(t, p):
                    pe.wait_ge(probn_ready, 2 * t + n + 1)
                    ge(pe, probt_ready, 2 * t + n)
                    if n == 0:
                        ge(pe, xt_ready, t - 2)
                    for j in range(4):
                        last = nc.tensor.transpose(ps_t[:, P * j:P * (j + 1)],
                                                   probn[:, n, 2 * j:2 * j + 2].rearrange("p a k -> p (a k)"), c["ident"])
                    last.then_inc(transp_done, 1)
                return part

            def weighted(n):
                def part(t, p):
                    pe.wait_ge(probt_ready, 2 * t + n + 1)
                    pe.wait_ge(v_out, 2 * t + 2)
                    ge(pe, ot_ready, 8 * t + 4 * n)
                    for jj in range(4):
                        for s in range(2):
                            rows = slice(64 * s, 64 * (s + 1))
                            last = nc.tensor.matmul(ps_o[s][:, P * jj:P * (jj + 1)], vg[rows, p, s ^ n, jj, :], probt[rows, n, jj, :],
                                                    start=True, stop=True)
                    last.then_inc(pv_done, 1)
                return part

            def project(t, p):
                pe.wait_ge(ot_ready, 8 * t + 8)
                pe.wait_ge(rest_ready, upto(t + 3, NT))
                ge(pe, norm.y_ready, t)
                for j in range(NJ):
                    last = nc.tensor.matmul(ps_y[:, 0:P], ot[:, p, j // 2, j % 2].rearrange("p n b s -> p (n b s)"), w["out"][:, j, :],
                                            start=j == 0, stop=j == NJ - 1)
                last.then_inc(wo_done, 1)

            def residual_t(t, p):
                pe.wait_ge(xg_ready, 2 * t + 1)
                ge(pe, rest_ready, t)
                ge(pe, norm.y_ready, t - 2)
                nc.tensor.transpose(ps_y[:, P:2 * P], xg[:, p, 0, :], c["ident"]).then_inc(rest_done, 1)

            def back(t, p):
                pe.wait_ge(norm.normed, t + 1)
                pe.wait_ge(probt_ready, upto(2 * (t + 3), 2 * NT))
                ge(pe, xt_ready, t)
                nc.tensor.transpose(ps_t[:, 0:P], norm.out[:], c["ident"]).then_inc(back_done, 1)

            pe.wait_ge(setup, 5)
            nc.tensor.matmul(ps_s[0][:, 0:P], csum[:].rearrange("f r b -> f (r b)"), w["x_w2"], start=True, stop=True
                             ).then_inc(context_done, 1)
            pe.wait_ge(setup, 6)
            pipelined(pe, [(1, scores), (2, queries(0)), (2, queries(1)), (-1, project), (0, transposes(0)), (2, keys(0)),
                           (0, transposes(1)), (2, keys(1)), (0, weighted(0)), (2, values(0)), (2, values(1)), (2, residual_t),
                           (0, weighted(1)), (-2, back)])

        @block.vector
        def _(dve):
            nc.vector.memset(score[:], MASKED).then_inc(setup, 1)
            for a in range(2):
                nc.vector.tensor_scalar(qb[:, a], w["in_b"][:, 0:NJ].unsqueeze(2).broadcast_to([P, NJ, 4]), c["h2"][:, a:a + 1],
                                        None, ALU.mult).then_inc(setup, 1)
            nc.vector.reduce_sum(csum[:, 0, :], ct.rearrange("f (b s) -> f b s", b=B), axis=AX.X).then_inc(setup, 1)
            dve.wait_ge(setup, 4)
            nc.vector.tensor_copy(csum[:, 1:4, :], csum[:, 0:1, :].broadcast_to([P, 3, B])).then_inc(setup, 1)
            dve.wait_ge(context_done, 1)
            nc.vector.scalar_tensor_tensor(context[:], ps_s[0][:, 0:P], 1.0 / S, w["x_b"], ALU.mult, ALU.add).then_inc(setup, 1)
            dve.wait_ge(setup, 6)

            def residual(t, p):
                dve.wait_ge(rest_done, t + 1)
                nc.vector.tensor_tensor(res[:, t, :], ps_y[:, P:2 * P], w["out_b"], ALU.add).then_inc(rest_ready, 1)

            def queries(n):
                def part(t, p):
                    dve.wait_ge(q_done, 2 * t + n + 1)
                    ge(dve, scores_done, 2 * (t - 1))
                    for a in range(2):
                        bias = qb[:, a, 4 * n:4 * n + 4].rearrange("p j b -> p (j b)").unsqueeze(2).broadcast_to([P, 16, B])
                        nc.vector.scalar_tensor_tensor(q2[:, p, 4 * n:4 * n + 4, :, a, :].rearrange("p j b s -> p (j b) s"),
                                                       ps_p[n][:].rearrange("p (j s) -> p j s", s=B), c["h2"][:, a:a + 1], bias,
                                                       ALU.mult, ALU.add).then_inc(q_out, 1)
                return part

            def values(n):
                def part(t, p):
                    dve.wait_ge(v_done, 2 * t + n + 1)
                    ge(dve, pv_done, 2 * (t - 1))
                    nc.vector.tensor_tensor(vg[:, p, n], ps_p[n][:].rearrange("p (j d) -> p j d", j=4),
                                            w["v_b"].rearrange("p (j a d) -> p a j d", a=2, d=P)[:, n], ALU.add).then_inc(v_out, 1)
                return part

            def softmax(n):
                def part(t, p):
                    dve.wait_ge(scores_done, 2 * t + n + 1)
                    ge(dve, prob_ready, 2 * (t - 1) + n + 1)
                    for b in range(2):
                        rows = slice(64 * b, 64 * (b + 1))
                        src = ps_s[n][rows].rearrange("p (j b s) -> p j b s", j=NJ, b=2)[:, :, b, :]
                        ge(dve, score_ready, 4 * (t - 1) + 2 * n + b + 1)
                        nc.vector.reduce_max(top[rows, n, :], src, axis=AX.X).then_inc(top_ready, 1)
                    for b in range(2):
                        rows = slice(64 * b, 64 * (b + 1))
                        src = ps_s[n][rows].rearrange("p (j b s) -> p j b s", j=NJ, b=2)[:, :, b, :]
                        dve.wait_ge(top_ready, 4 * t + 2 * n + b + 1)
                        nc.vector.tensor_tensor(score[rows, n, :, b, :], src, top[rows, n, :].unsqueeze(2).broadcast_to([64, NJ, B]),
                                                ALU.subtract).then_inc(score_ready, 1)
                return part

            def sums(t, p):
                for n in range(2):
                    dve.wait_ge(prob_ready, 2 * t + n + 1)
                    ge(dve, probn_ready, 2 * (t - 1) + n + 1)
                    nc.vector.reduce_sum(total[:, n, :], prob[:, n], axis=AX.X).then_inc(total_ready, 1)
                    dve.wait_ge(total_ready, 2 * t + n + 1)
                    nc.vector.reciprocal(rsum[:, n, :], total[:, n, :]).then_inc(rsum_ready, 1)

            def statistics(t, p):
                dve.wait_ge(wo_done, t + 1)
                norm.statistics(dve, t, ps_y[:, 0:P], res[:, t, :])

            def scaling(t, p):
                ge(dve, back_done, t)
                ge(dve, res_ready, t)
                norm.scaling(dve, t)

            pipelined(dve, [(1, softmax(0)), (2, queries(0)), (2, queries(1)), (1, softmax(1)), (-1, statistics), (1, sums),
                            (2, values(0)), (-1, scaling), (2, values(1)), (2, residual)])

        @block.scalar
        def _(act):
            def exponent(t, p):
                for n in range(2):
                    act.wait_ge(score_ready, 4 * t + 2 * n + 2)
                    ge(act, probn_ready, 2 * (t - 1) + n + 1)
                    nc.scalar.activation(prob[:, n], score[:, n].rearrange("p j b s -> p j (b s)"), ACT.Exp).then_inc(prob_ready, 1)

            def keys(n):
                def part(t, p):
                    act.wait_ge(k_done, 2 * t + n + 1)
                    ge(act, scores_done, 2 * (t - 1))
                    for j in range(4 * n, 4 * n + 4):
                        nc.scalar.activation(kg[:, p, j, :], ps_p[n][:, P * (j % 4):P * (j % 4 + 1)], ACT.Identity,
                                             bias=w["in_b"][:, NJ + j:NJ + j + 1]).then_inc(k_out, 1)
                return part

            def probs_t(n):
                def part(t, p):
                    act.wait_ge(transp_done, 2 * t + n + 1)
                    ge(act, pv_done, 2 * (t - 1) + n + 1)
                    nc.scalar.activation(probt[:, n], ps_t[:].rearrange("p (j q) -> p j q", j=4), ACT.Copy).then_inc(probt_ready, 1)
                return part

            def outputs_t(n):
                def part(t, p):
                    act.wait_ge(pv_done, 2 * t + n + 1)
                    ge(act, wo_done, t - 1)
                    for s in range(2):
                        for a in range(2):
                            rows = slice(64 * a, 64 * (a + 1))
                            src = ps_o[s][rows].rearrange("p (j b a s) -> p j b a s", j=4, b=2, a=2)[:, :, :, a, :]
                            nc.scalar.activation(ot[rows, p, :, s ^ n, n], src, ACT.Copy).then_inc(ot_ready, 1)
                return part

            def feature_major(t, p):
                act.wait_ge(back_done, t + 1)
                nc.scalar.activation(xt_next[:, bass.ds(P * t, P)], ps_t[:, 0:P], ACT.Copy).then_inc(xt_ready, 1)

            pipelined(act, [(0, probs_t(0)), (2, keys(0)), (0, probs_t(1)), (2, keys(1)), (1, exponent), (0, outputs_t(0)),
                            (0, outputs_t(1)), (-2, feature_major)])

        @block.gpsimd
        def _(pool):
            def tokens(t, p):
                ge(pool, v_done, 2 * (t - 1))
                ge(pool, rest_done, t - 1)
                nc.gpsimd.tensor_copy(xg[:, p, 0, :], xpos[:, bass.ds(P * t, P)]).then_inc(xg_ready, 1)
                nc.gpsimd.tensor_copy(xg[:, p, 1, 0:S], xpos[:, bass.ds(P * t + S, S)])
                nc.gpsimd.tensor_copy(xg[:, p, 1, S:P], xpos[:, bass.ds(P * t, S)]).then_inc(xg_ready, 1)

            def normalise(t, p):
                for n in range(2):
                    pool.wait_ge(rsum_ready, 2 * t + n + 1)
                    ge(pool, transp_done, 2 * (t - 1) + n + 1)
                    nc.gpsimd.tensor_tensor(probn[:, n], prob[:, n], rsum[:, n, :].unsqueeze(2).broadcast_to([P, NJ, S]),
                                            ALU.mult).then_inc(probn_ready, 1)

            def power(t, p):
                norm.power(pool, t, c["neghalf"][:, 0:1], c["eps"][:, 0:1])

            def keep_residual(t, p):
                pool.wait_ge(norm.normed, t + 1)
                nc.gpsimd.tensor_tensor(res_next[:, t, :], norm.out[:], context[:], ALU.add).then_inc(res_ready, 1)

            pool.wait_ge(setup, 6)
            pipelined(pool, [(1, normalise), (3, tokens), (-1, power), (-1, keep_residual)])
            pool.wait_ge(res_ready, NT)


def position_linear(nc, banks, w, xt, x_res, logits, xn_next, res_next, c):
    with ExitStack() as ctx:
        def sb(name, shape, dt=F32):
            return ctx.enter_context(nc.sbuf_tensor(f"lin_{name}", shape, dt))

        def sem(name):
            return ctx.enter_context(nc.semaphore(f"lin_{name}"))

        xs, xnt = sb("xs", [P, P]), sb("xnt", [P, P])
        outer, inner = Norm(nc, ctx, "lin_outer"), Norm(nc, ctx, "lin_inner")
        xs_ready, lin_done, back_done, xnt_ready = sem("xs_ready"), sem("lin_done"), sem("back_done"), sem("xnt_ready")
        xn_ready, gate_done, gate_out, kept = sem("xn_ready"), sem("gate_done"), sem("gate_out"), sem("kept")
        ps_y, ps_b, ps_g = banks[0], banks[1], banks[2]
        block = ctx.enter_context(nc.Block())

        @block.tensor
        def _(pe):
            def linear(t, p):
                pe.wait_ge(xs_ready, t + 1)
                ge(pe, outer.y_ready, t)
                nc.tensor.matmul(ps_y[:, 0:P], xs[:], w["x_w1"], start=True, stop=True).then_inc(lin_done, 1)

            def back(t, p):
                pe.wait_ge(inner.normed, t + 1)
                ge(pe, xn_ready, t)
                nc.tensor.transpose(ps_b[:, 0:P], inner.out[:], c["ident"]).then_inc(back_done, 1)

            def gate(t, p):
                pe.wait_ge(xnt_ready, t + 1)
                ge(pe, gate_out, t)
                nc.tensor.matmul(ps_g[:, 0:NE], xnt[:], w["router"], start=True, stop=True).then_inc(gate_done, 1)

            pipelined(pe, [(1, linear), (-1, back), (-2, gate)])

        @block.vector
        def _(dve):
            def statistics(t, p):
                dve.wait_ge(lin_done, t + 1)
                outer.statistics(dve, t, ps_y[:, 0:P], x_res[:, t, :])

            def inner_scaling(t, p):
                ge(dve, back_done, t)
                inner.scaling(dve, t, outer.out[:])

            def scaling(t, p):
                ge(dve, inner.normed, t)
                ge(dve, kept, t)
                outer.scaling(dve, t)

            def inner_statistics(t, p):
                dve.wait_ge(outer.normed, t + 1)
                inner.moments(dve, t, outer.out[:])

            pipelined(dve, [(0, statistics), (-1, inner_scaling), (0, scaling), (0, inner_statistics)])

        @block.scalar
        def _(act):
            def feature_major(t, p):
                act.wait_ge(back_done, t + 1)
                ge(act, gate_done, t)
                nc.scalar.activation(xnt[:], ps_b[:, 0:P], ACT.Identity, bias=w["beta"], scale=w["gamma"]).then_inc(xnt_ready, 1)
                nc.scalar.activation(xn_next[:, bass.ds(P * t, P)], ps_b[:, 0:P], ACT.Identity, bias=w["beta"],
                                     scale=w["gamma"]).then_inc(xn_ready, 1)

            def gate_logits(t, p):
                act.wait_ge(gate_done, t + 1)
                nc.scalar.activation(logits[:, t, :], ps_g[:, 0:NE], ACT.Copy).then_inc(gate_out, 1)

            pipelined(act, [(-1, feature_major), (-2, gate_logits)])

        @block.gpsimd
        def _(pool):
            def tokens(t, p):
                ge(pool, lin_done, t)
                nc.gpsimd.tensor_copy(xs[:], xt[:, bass.ds(P * t, P)]).then_inc(xs_ready, 1)

            def powers(t, p):
                outer.power(pool, t, c["neghalf"][:, 0:1], c["eps"][:, 0:1])
                inner.power(pool, t, c["neghalf"][:, 0:1], c["eps"][:, 0:1])

            def keep(t, p):
                nc.gpsimd.tensor_tensor(res_next[:, t, :], outer.out[:], outer.out[:], ALU.add).then_inc(kept, 1)

            pipelined(pool, [(0, powers), (0, keep), (2, tokens)])
            pool.wait_ge(kept, NT)


def last_experts(nc, banks, w1_dram, w2_dram, xn, acc, logits, out_dram, c):
    with ExitStack() as ctx:
        def sb(name, shape, dt=F32):
            return ctx.enter_context(nc.sbuf_tensor(f"ffn_{name}", shape, dt))

        def sem(name):
            return ctx.enter_context(nc.semaphore(f"ffn_{name}"))

        w1 = sb("w1", [P, 2, FF])
        w2 = sb("w2", [P, 2, NF, P])
        ht = sb("ht", [P, 2, NF, CHUNK])
        yout = sb("yout", [P, NT, P])
        norm = Norm(nc, ctx, "ffn")
        before, exponent, after, weight = route(nc, ctx, "ffn_route", logits, c["iota"], ROUTER_TEMP)
        w_in = [sem(f"w_in{k}") for k in range(2)]
        hid_done, silu_ready, out_done, acc_ready, out_sent = sem("hid_done"), sem("silu_ready"), sem("out_done"), sem("acc_ready"), sem("out_sent")
        ps_h, ps_z = banks[0:2], banks[2:4]
        CH = B * S // CHUNK
        block = ctx.enter_context(nc.Block())

        def experts(engine, pair):
            pair(0)
            with engine.Fori(1, NE // 2 - 1) as i:
                pair(i)
            pair(NE // 2 - 1)

        @block.sync
        def _(sp):
            for e in range(NE):
                ge(sp, out_done, CH * (e - 1))
                ge(sp, w_in[e % 2], 32 * (e // 2))
                sp.dma_start(w1[:, e % 2, :], w1_dram[e]).then_inc(w_in[e % 2], 16)
                sp.dma_start(w2[:, e % 2], w2_dram[e].rearrange("(f p) d -> p f d", p=P)).then_inc(w_in[e % 2], 16)
            for t in range(NT):
                sp.wait_ge(norm.normed, t + 1)
                sp.dma_start(out_dram[:, 4 * t:4 * t + 4, :].rearrange("s p d -> p s d"), yout[:, t, :]).then_inc(out_sent, 16)
            sp.wait_ge(out_sent, 16 * NT)

        @block.tensor
        def _(pe):
            def hidden(i, k, ch):
                q = 2 * CH * i + CH * k + ch
                pe.wait_ge(w_in[k], 32 * (i + 1))
                for f in range(NF):
                    ge(pe, silu_ready, NF * q + f - 1)
                    nc.tensor.matmul(ps_h[f % 2][:], w1[:, k, P * f:P * (f + 1)], xn[:, CHUNK * ch:CHUNK * (ch + 1)],
                                     start=True, stop=True).then_inc(hid_done, 1)

            def output(i, k, ch):
                q = 2 * CH * i + CH * k + ch
                pe.wait_ge(silu_ready, NF * (q + 1))
                ge(pe, acc_ready, q - 1)
                for tt in range(4):
                    for f in range(NF):
                        last = nc.tensor.matmul(ps_z[q_parity(ch)][:, P * tt:P * (tt + 1)], ht[:, q_parity(ch), f, P * tt:P * (tt + 1)],
                                                w2[:, k, f, :], start=f == 0, stop=f == NF - 1)
                last.then_inc(out_done, 1)

            def pair(i):
                for u in range(2 * CH):
                    if u < 2 * CH - 1:
                        hidden(i, (u + 1) // CH, (u + 1) % CH)
                    elif not isinstance(i, int) or i < NE // 2 - 1:
                        hidden(i + 1, 0, 0)
                    output(i, u // CH, u % CH)

            hidden(0, 0, 0)
            experts(pe, pair)

        @block.scalar
        def _(act):
            exponent(act)

            def pair(i):
                for u in range(2 * CH):
                    q = 2 * CH * i + u
                    ge(act, out_done, q - 1)
                    for f in range(NF):
                        act.wait_ge(hid_done, NF * q + f + 1)
                        nc.scalar.activation(ht[:, u % 2, f, :], ps_h[f % 2][:], ACT.Silu).then_inc(silu_ready, 1)

            experts(act, pair)

        @block.vector
        def _(dve):
            before(dve)
            after(dve)

            def pair(i):
                for u in range(2 * CH):
                    q = 2 * CH * i + u
                    dve.wait_ge(out_done, q + 1)
                    ge(dve, acc_ready, q - CH + 1)
                    for tt in range(4):
                        t = 4 * (u % CH) + tt
                        e = 2 * i + u // CH
                        last = nc.vector.scalar_tensor_tensor(acc[:, t, :], ps_z[u % 2][:, P * tt:P * (tt + 1)],
                                                              weight[:, t, bass.ds(e, 1)], acc[:, t, :], ALU.mult, ALU.add)
                    last.then_inc(acc_ready, 1)

            experts(dve, pair)

            def statistics(t, p):
                if isinstance(t, int) and t == 0:
                    dve.wait_ge(acc_ready, CH * NE)
                ge(dve, norm.normed, t)
                norm.moments(dve, t, acc[:, t, :])

            def scaling(t, p):
                norm.scaling(dve, t, acc[:, t, :], yout[:, t, :])

            pipelined(dve, [(0, statistics), (0, scaling)])

        @block.gpsimd
        def _(pool):
            pipelined(pool, [(0, lambda t, p: norm.power(pool, t, c["neghalf"][:, 0:1], c["eps"][:, 0:1]))])


def q_parity(ch):
    return ch % 2


def build(nc, a, out_dram):
    with ExitStack() as ctx:
        def sb(name, shape, dt=F32):
            return ctx.enter_context(nc.sbuf_tensor(name, shape, dt))

        banks = [ctx.enter_context(nc.psum_tensor(f"bank{n}", [P, CHUNK], F32)) for n in range(8)]
        xt_a, xt_b, ct = sb("xt_a", [P, B * S]), sb("xt_b", [P, B * S]), sb("ct", [P, B * S])
        res_a, res_b = sb("res_a", [P, NT, P]), sb("res_b", [P, NT, P])
        logits = sb("logits", [P, NT, NE])
        shapes = {name: list(ap.shape) for name, ap in a.items()}
        held = {}
        for name in a:
            if name in ("x", "xt", "ct", "w1", "w2"):
                continue
            held[name] = sb(f"w_{name}", shapes[name])
        early = ["eb", "third", "self_k", "self_q", "self_v", "self_o", "lam", "ln_g", "ln_b", "cross_ob", "ident", "pair",
                 "parity", "half", "first", "second", "neghalf", "eps"]
        late = [name for name in held if name not in early]
        eb3 = sb("eb3", [3, NE * P], BF16)
        ones3 = sb("ones3", [3, P], BF16)

        loaded = ctx.enter_context(nc.semaphore("loaded"))
        loaded_late = ctx.enter_context(nc.semaphore("loaded_late"))
        split = ctx.enter_context(nc.semaphore("split"))
        with ExitStack() as parts:
            part = [parts.enter_context(nc.sbuf_tensor(f"eb_part{n}", [3, NE * P], F32)) for n in range(3)]
            short = [parts.enter_context(nc.sbuf_tensor(f"eb_short{n}", [3, NE * P], BF16)) for n in range(3)]
            block = parts.enter_context(nc.Block())

            @block.sync
            def _(sp):
                for name in early:
                    sp.dma_start(held[name][:], a[name]).then_inc(loaded, 16)
                sp.dma_start(xt_a[:], a["xt"]).then_inc(loaded, 16)
                sp.dma_start(res_a[:], a["x"].rearrange("(t p) d -> p t d", p=P)).then_inc(loaded, 16)
                for name in late:
                    sp.dma_start(held[name][:], a[name]).then_inc(loaded_late, 16)
                sp.dma_start(ct[:], a["ct"]).then_inc(loaded_late, 16)
                sp.wait_ge(loaded, 16 * (len(early) + 2))

            @block.vector
            def _(dve):
                dve.wait_ge(loaded, 16 * (len(early) + 2))
                n = 0
                nc.vector.memset(ones3[:], 1.0)
                for k in range(3):
                    src = held["eb"][:] if k == 0 else part[k - 1][:]
                    if n:
                        dve.wait_ge(split, n)
                    nc.vector.tensor_copy(short[k][:], src).then_inc(split, 1)
                    n += 1
                    dve.wait_ge(split, n)
                    nc.vector.tensor_tensor(part[k][:], src, short[k][:], ALU.subtract).then_inc(split, 1)
                    n += 1
                sel = held["third"]
                dve.wait_ge(split, n)
                nc.vector.tensor_scalar(eb3[:], short[0][:], sel[:, 0:1], None, ALU.mult).then_inc(split, 1)
                for k in (1, 2):
                    n += 1
                    dve.wait_ge(split, n)
                    nc.vector.scalar_tensor_tensor(eb3[:], short[k][:], sel[:, k:k + 1], eb3[:], ALU.mult, ALU.add).then_inc(split, 1)

        h = {name: t[:] for name, t in held.items()}
        c = {name: h[name] for name in ("ident", "pair", "half", "first", "second", "both", "neghalf", "eps", "iota", "h2")}
        c["parity"] = h["parity"]
        c["ones3"] = ones3[:]
        with ExitStack() as keys:
            km = keys.enter_context(nc.sbuf_tensor("km", [P, B, CHUNK], F32))
            vb = keys.enter_context(nc.sbuf_tensor("vb", [P, B, 4, 2, VD + 1], F32))
            w = {"q": h["self_q"], "k": h["self_k"], "v": h["self_v"], "o": h["self_o"], "qb": None, "kb": None,
                 "lam": h["lam"], "og": h["ln_g"], "ob": h["ln_b"], "next_bias": h["cross_ob"]}
            pair_attention(nc, banks, True, w, xt_a, xt_a, km, vb, lambda t: res_a[:, t, :], res_b, xt_b, c)
            late_ready = 16 * (len(late) + 1)
            with nc.Block() as block:
                @block.sync
                def _(sp):
                    sp.wait_ge(loaded_late, late_ready)

            w = {"q": h["cross_q"], "k": h["cross_k"], "v": h["cross_v"], "o": h["cross_o"], "qb": h["cross_qb"],
                 "kb": h["cross_kb"], "vb": h["cross_vb"], "gate": h["gate"]}
            pair_attention(nc, banks, False, w, xt_b, ct, km, vb, lambda t: res_b[:, t, :], res_a, xt_a, c, logits)
        w = {"eb3": eb3[:], "expert": h["expert"], "combine": h["combine"]}
        first_experts(nc, banks, w, xt_a, res_a, logits, xt_b, c)
        w = {"in": h["in"], "in_b": h["in_b"], "v_b": h["v_b"], "out": h["out"], "out_b": h["out_b"],
             "x_w2": h["x_w2"], "x_b": h["x_b"]}
        sequence_attention(nc, banks, w, xt_b, ct[:], res_a, res_b, xt_a, c)
        w = {"x_w1": h["x_w1"], "router": h["router"], "gamma": h["gamma"], "beta": h["beta"]}
        position_linear(nc, banks, w, xt_a, res_b, logits, xt_b, res_a, c)
        last_experts(nc, banks, a["w1"], a["w2"], xt_b, res_a, logits, out_dram, c)


def constants():
    p = np.arange(P)
    f = lambda x: np.ascontiguousarray(x, dtype=np.float32)
    token = np.arange(P)
    place = np.stack([(token[None, :] == S * u + p[:, None] % S) for u in range(2)], axis=1)
    par = (p // S)[:, None, None]
    return {
        "ident": f(np.eye(P)),
        "pair": f(p[:, None] // VD == np.arange(NPAIR)),
        "parity": f(((p // HD) % 2)[:, None] == np.arange(2)) * np.float32(HD ** -0.5),
        "half": f((p // S)[:, None] == np.arange(2)),
        "first": f(place & (par == 0)),
        "second": -f(place & (par == 1)),
        "both": f(p[:, None] % S == np.arange(S)),
        "neghalf": f(np.full((P, NE), -0.5)),
        "eps": f(np.full((P, NE), LN_EPS)),
        "iota": f(np.broadcast_to(np.arange(NE), (P, NE))),
        "h2": f((p // D1)[:, None] == np.arange(2)) * np.float32(D1 ** -0.5),
        "third": f(np.eye(3)),
    }


def kernel(**inputs):
    import concourse.bacc as bacc
    from concourse.bass_utils import run_bass_kernel_spmd

    v = {name: np.asarray(x) for name, x in inputs.items()}
    rows = lambda x, n=P: np.broadcast_to(x.reshape(1, -1), (n, x.size))
    col = lambda x: x.reshape(-1, P).T
    arrays = {
        "x": v["x"].reshape(B * S, E),
        "xt": v["x"].reshape(B * S, E).T,
        "ct": v["ctx_1024"].reshape(B * S, E).T,
        "self_q": v["L0_attn_Wq"], "self_k": v["L0_attn_Wk"], "self_v": v["L0_attn_Wv"], "self_o": v["L0_attn_Wo"],
        "lam": np.broadcast_to(np.stack([v["L0_attn_lq1"], v["L0_attn_lq2"], v["L0_attn_lk1"], v["L0_attn_lk2"]]), (P, 4, HD)),
        "ln_g": np.tile(v["L0_attn_ln_g"], NPAIR).reshape(P, 1), "ln_b": np.tile(v["L0_attn_ln_b"], NPAIR).reshape(P, 1),
        "cross_q": v["L0_xattn_wq_w"].T, "cross_k": v["L0_xattn_wk_w"].T, "cross_v": v["L0_xattn_wv_w"].T,
        "cross_o": v["L0_xattn_wo_w"].T, "cross_qb": col(v["L0_xattn_wq_b"]), "cross_kb": col(v["L0_xattn_wk_b"]),
        "cross_vb": col(v["L0_xattn_wv_b"]), "cross_ob": rows(v["L0_xattn_wo_b"]),
        "gate": v["L0_ffn_gate_w"].T,
        "expert": v["L0_ffn_expert_w"].transpose(2, 0, 1).reshape(E, NE * E),
        "eb": rows(v["L0_ffn_expert_b"], 3), "combine": v["L0_ffn_combine_w"].T,
        "in": v["L1_attn_in_proj_weight"].T, "in_b": col(v["L1_attn_in_proj_bias"]),
        "v_b": rows(v["L1_attn_in_proj_bias"][2 * H1 * D1:]),
        "out": v["L1_attn_out_proj_weight"].T.reshape(NJ, P, E).transpose(1, 0, 2),
        "out_b": rows(v["L1_attn_out_proj_bias"]),
        "x_w1": v["L1_xattn_W"][:, :E].T, "x_w2": v["L1_xattn_W"][:, E:].T, "x_b": rows(v["L1_xattn_b"]),
        "gamma": col(v["L1_ffn_gamma"]), "beta": col(v["L1_ffn_beta"]), "router": v["L1_ffn_router_w"].T,
        "w1": v["L1_ffn_W1"], "w2": v["L1_ffn_W2"],
    }
    arrays.update(constants())
    arrays = {name: np.ascontiguousarray(x) for name, x in arrays.items()}
    nc = bacc.Bacc("TRN2", target_bir_lowering=False, num_devices=1)
    a = {name: nc.dram_tensor(f"in_{name}", x.shape, mybir.dt.from_np(x.dtype), kind="ExternalInput").ap()
         for name, x in arrays.items()}
    out = nc.dram_tensor("out", (B, S, E), F32, kind="ExternalOutput").ap()
    build(nc, a, out)
    r = run_bass_kernel_spmd(nc, [{f"in_{name}": x for name, x in arrays.items()}], core_ids=[0])
    return r.results[0]["out"]
```

```python
from contextlib import ExitStack

import numpy as np

import concourse.bass as bass
from concourse import mybir

F32 = mybir.dt.float32
BF16 = mybir.dt.bfloat16
U32 = mybir.dt.uint32
I32 = mybir.dt.int32
ACT = mybir.ActivationFunctionType
ALU = mybir.AluOpType
AX = mybir.AxisListType

P = 128
B, S, E = 32, 64, 128
NT = B * S // P
LN_EPS = 1e-5
CHUNK = 512

NPAIR, HD, VD = 8, 8, 16
H1, D1 = 16, 64
NJ = H1 // 2
NE = 8
FF = 512
NF = FF // P
LAM_INIT = 0.8 - 0.6 * float(np.exp(-0.3 * 12))
ROUTER_TEMP = 1.5
SLOTS = (2 * B * S + NE * (P - 1)) // P
MASKED = -1e30


def ge(engine, semaphore, value):
    if not isinstance(value, int) or value > 0:
        engine.wait_ge(semaphore, value)


def upto(value, most):
    return min(value, most) if isinstance(value, int) else value


def pipelined(engine, parts, n=NT, before=2):
    most, least = max(lag for lag, _ in parts), min(lag for lag, _ in parts)

    def step(i, parity):
        for lag, part in parts:
            if not isinstance(i, int) or 0 <= i + lag < n:
                part(i + lag, (parity + lag) % 2)

    lo, hi = before - least, n - most
    hi -= (hi - lo) % 2
    for i in range(-most, lo):
        step(i, i % 2)
    with engine.Fori(lo, hi - 1, 2) as i:
        step(i, lo % 2)
        step(i + 1, (lo + 1) % 2)
    for i in range(hi, n - least):
        step(i, i % 2)


class Norm:

    def __init__(self, nc, ctx, tag):
        self.nc = nc
        sb = lambda name, shape: ctx.enter_context(nc.sbuf_tensor(f"{tag}_{name}", shape, F32))
        sem = lambda name: ctx.enter_context(nc.semaphore(f"{tag}_{name}"))
        self.y, self.out = sb("y", [P, P]), sb("normed", [P, P])
        self.stats, self.mv, self.rstd = sb("stats", [P, 6]), sb("mv", [P, 2]), sb("rstd", [P, 2])
        self.y_ready, self.mv_ready = sem("y_ready"), sem("mv_ready")
        self.rstd_ready, self.normed = sem("rstd_ready"), sem("normed_ready")

    def statistics(self, dve, t, src, residual):
        nc = self.nc
        ge(dve, self.normed, t)
        nc.vector.tensor_tensor(self.y[:], src, residual, ALU.add).then_inc(self.y_ready, 1)
        dve.wait_ge(self.y_ready, t + 1)
        self.moments(dve, t, self.y[:])

    def moments(self, dve, t, src):
        nc = self.nc
        nc.vector.bn_stats(self.stats[:], src).then_inc(self.mv_ready, 1)
        dve.wait_ge(self.mv_ready, 2 * t + 1)
        dve.nop(nofuse=True)
        nc.vector.bn_aggr(self.mv[:], self.stats[:]).then_inc(self.mv_ready, 1)

    def power(self, pool, t, neghalf, eps):
        nc = self.nc
        pool.wait_ge(self.mv_ready, 2 * t + 2)
        ge(pool, self.normed, t)
        nc.gpsimd.tensor_tensor(self.rstd[:, 0:1], self.mv[:, 1:2], eps, ALU.add).then_inc(self.rstd_ready, 1)
        pool.wait_ge(self.rstd_ready, 2 * t + 1)
        nc.gpsimd.tensor_tensor(self.rstd[:, 1:2], self.rstd[:, 0:1], neghalf, ALU.pow).then_inc(self.rstd_ready, 1)

    def scaling(self, dve, t, src=None, dst=None):
        dve.wait_ge(self.rstd_ready, 2 * t + 2)
        self.nc.vector.tensor_scalar(self.out[:] if dst is None else dst, self.y[:] if src is None else src, self.mv[:, 0:1],
                                     self.rstd[:, 1:2], ALU.subtract, ALU.mult).then_inc(self.normed, 1)


def pair_attention(nc, banks, self_diff, w, q_src, kv_src, km, vb, residual, res_next, xt_next, c, logits=None,
                   background=None):
    tag = "self" if self_diff else "cross"
    with ExitStack() as ctx:
        def sb(name, shape, dt=F32):
            return ctx.enter_context(nc.sbuf_tensor(f"{tag}_{name}", shape, dt))

        def sem(name):
            return ctx.enter_context(nc.semaphore(f"{tag}_{name}"))

        qt = sb("qt", [P, B * S])
        kt = sb("kt", [P, B * S])
        xdup = sb("xdup", [P, 2, 2, 2, S])
        q2 = sb("q2", [P, 2, 2, 2, S])
        score = sb("score", [P, 2, CHUNK])
        prob = sb("prob", [P, 2, CHUNK])
        probt = sb("probt", [P, 2, CHUNK])
        top = sb("top", [P, 2, NPAIR])
        rsum = sb("rsum", [P, 2, NPAIR])
        rhalf = sb("rhalf", [P, 2, NPAIR, 2])
        on = sb("on", [P, 2, NPAIR, VD])
        ot = sb("ot", [P, P])
        xnt = sb("xnt", [P, P])
        norm = Norm(nc, ctx, tag)
        ps_s, ps_t, ps_o, ps_v, ps_d, ps_a = banks[0:2], banks[2:4], banks[4], banks[5], banks[6], banks[7]
        ps_w = ps_a[:, 2 * P:3 * P] if self_diff else ps_d[:, P:2 * P]

        proj_done, proj_out = sem("proj_done"), sem("proj_out")
        xdup_ready, q2_ready, km_ready = sem("xdup_ready"), sem("q2_ready"), sem("km_ready")
        values_done, scores_done = sem("values_done"), sem("scores_done")
        vb_ready, top_ready, score_ready = sem("vb_ready"), sem("top_ready"), sem("score_ready")
        prob_ready, transp_done, probt_ready = sem("prob_ready"), sem("transp_done"), sem("probt_ready")
        pv_done, rsum_ready, on_ready = sem("pv_done"), sem("rsum_ready"), sem("on_ready")
        comb_done, back_done, ot_ready, xt_ready = sem("comb_done"), sem("back_done"), sem("ot_ready"), sem("xt_ready")
        wo_done, res_ready = sem("wo_done"), sem("res_ready")
        if not self_diff:
            rhalf_ready, xnt_ready, gate_done, gate_out = sem("rhalf_ready"), sem("xnt_ready"), sem("gate_done"), sem("gate_out")
        else:
            hn_c = sb("hn_c", [P, NPAIR, VD])
            hn_sq = sb("hn_sq", [P, NPAIR, VD])
            hn_o = sb("hn_o", [P, NPAIR, VD])
            hn_m, hn_v = sb("hn_m", [P, NPAIR]), sb("hn_v", [P, NPAIR])
            hn_r = sb("hn_r", [P, 2, NPAIR])
            comb = sb("comb", [P, 2, P])
            lam_prod, lam = sb("lam_prod", [P, 2, HD]), sb("lam", [P, 5])
            hn_step, hn_var, hn_rstd, hn_done = sem("hn_step"), sem("hn_var"), sem("hn_rstd"), sem("hn_done")
            lam_step, lam_exp, hnt_done = sem("lam_step"), sem("lam_exp"), sem("hnt_done")

        block = ctx.enter_context(nc.Block())

        if background is not None:
            block.sync(background)

        @block.tensor
        def _(pe):
            for n in range(8):
                src, wgt = (kv_src, w["k"]) if n < 4 else (q_src, w["q"])
                ge(pe, proj_out, n - 1)
                nc.tensor.matmul(ps_s[n % 2][:], wgt, src[:, CHUNK * (n % 4):CHUNK * (n % 4 + 1)],
                                 start=True, stop=True).then_inc(proj_done, 1)
            pe.wait_ge(proj_out, 8)
            if self_diff:
                pe.wait_ge(lam_step, 5)

            def scores(t, p):
                ge(pe, vb_ready, 2 * t)
                pe.wait_ge(xdup_ready, t + 1)
                for u in range(2):
                    nc.tensor.matmul(ps_v[:, P * u:P * (u + 1)], xdup[:, p, u].rearrange("p d s -> p (d s)"), w["v"],
                                     start=True, stop=True).then_inc(values_done, 1)
                pe.wait_ge(q2_ready, 2 * t + 2)
                for u in range(2):
                    pe.wait_ge(km_ready, 2 * t + u + 1)
                    ge(pe, score_ready, 2 * (t - 1) + u + 1)
                    nc.tensor.matmul(ps_s[u][:], q2[:, p, u].rearrange("p d s -> p (d s)"), km[:, 2 * t + u, :],
                                     start=True, stop=True).then_inc(scores_done, 1)

            def transposes(t, p):
                for u in range(2):
                    pe.wait_ge(prob_ready, 2 * t + u + 1)
                    ge(pe, probt_ready, 2 * (t - 1) + u + 1)
                    for j in range(4):
                        last = nc.tensor.transpose(ps_t[u][:, P * j:P * (j + 1)], prob[:, u, P * j:P * (j + 1)], c["ident"])
                    last.then_inc(transp_done, 1)

            def weighted(t, p):
                ge(pe, on_ready, 2 * t)
                for u in range(2):
                    pe.wait_ge(probt_ready, 2 * t + u + 1)
                    pe.wait_ge(vb_ready, 2 * t + 2)
                    for j in range(4):
                        last = nc.tensor.matmul(ps_o[:, 136 * u + 34 * j:136 * u + 34 * (j + 1)],
                                                probt[:, u, P * j:P * (j + 1)],
                                                vb[:, 2 * t + u, j].rearrange("p h d -> p (h d)"), start=True, stop=True)
                    last.then_inc(pv_done, 1)

            def combine(t, p):
                pe.wait_ge(on_ready, 2 * t + 2)
                if self_diff:
                    ge(pe, hn_step, 3 * (t - 1) + 2)
                    for u in range(2):
                        last = nc.tensor.matmul(ps_d[:, 0:P], comb[:, u, :], on[:, u].rearrange("p h d -> p (h d)"),
                                                start=u == 0, stop=u == 1)
                else:
                    ge(pe, norm.y_ready, t)
                    for u in range(2):
                        last = nc.tensor.matmul(ps_d[:, S * u:S * (u + 1)], on[:, u].rearrange("p h d -> p (h d)"),
                                                c["both"], start=True, stop=True)
                last.then_inc(comb_done, 1)

            def back(t, p):
                pe.wait_ge(norm.normed, t + 1)
                ge(pe, xt_ready, t)
                if self_diff:
                    pe.wait_ge(ot_ready, upto(t + 2, NT))
                    pe.wait_ge(norm.y_ready, upto(t + 2, NT))
                else:
                    ge(pe, gate_out, t)
                nc.tensor.transpose(ps_a[:, 0:P], norm.out[:], c["ident"]).then_inc(back_done, 1)

            def heads_back(t, p):
                pe.wait_ge(hn_done, t + 1)
                ge(pe, ot_ready, t)
                ge(pe, xt_ready, t - 2)
                ge(pe, norm.y_ready, t)
                nc.tensor.transpose(ps_a[:, P:2 * P], hn_o[:].rearrange("p h d -> p (h d)"), c["ident"]).then_inc(hnt_done, 1)

            def project(t, p):
                pe.wait_ge(ot_ready, t + 1)
                if self_diff:
                    ge(pe, xt_ready, t - 1)
                nc.tensor.matmul(ps_w, ot[:], w["o"], start=True, stop=True).then_inc(wo_done, 1)

            def gate(t, p):
                pe.wait_ge(xnt_ready, t + 1)
                pe.wait_ge(xt_ready, t + 1)
                nc.tensor.matmul(ps_a[:, 2 * P:2 * P + NE], xnt[:], w["gate"], start=True, stop=True).then_inc(gate_done, 1)

            if self_diff:
                pipelined(pe, [(1, scores), (-1, combine), (-4, back), (-2, heads_back), (0, transposes), (-2, project),
                               (0, weighted)])
            else:
                pipelined(pe, [(1, scores), (-1, combine), (-2, back), (0, transposes), (-1, project), (-2, gate),
                               (0, weighted)])

        @block.vector
        def _(dve):
            if self_diff:
                nc.vector.tensor_tensor(lam_prod[:], w["lam"][:, 0:2, :], w["lam"][:, 2:4, :], ALU.mult).then_inc(lam_step, 1)
                dve.wait_ge(lam_step, 1)
                nc.vector.reduce_sum(lam[:, 0:2], lam_prod[:], axis=AX.X).then_inc(lam_step, 1)
                dve.wait_ge(lam_exp, 1)
                nc.vector.tensor_scalar(lam[:, 4:5], lam[:, 2:3], lam[:, 3:4], LAM_INIT, ALU.subtract, ALU.add).then_inc(lam_step, 1)
                dve.wait_ge(lam_step, 3)
                for u in range(2):
                    nc.vector.scalar_tensor_tensor(comb[:, u, :], c["second"][:, u, :], lam[:, 4:5], c["first"][:, u, :],
                                                   ALU.mult, ALU.add).then_inc(lam_step, 1)
                nc.vector.tensor_copy(vb[:, :, :, :, VD].rearrange("p b j h -> p (b j) h"),
                                      c["half"].unsqueeze(1).broadcast_to([P, B * 4, 2])).then_inc(lam_step, 1)

            def softmax(t, p):
                for u in range(2):
                    pe_tile = ps_s[u][:].rearrange("p (h k) -> p h k", h=NPAIR)
                    dve.wait_ge(scores_done, 2 * t + u + 1)
                    ge(dve, score_ready, 2 * (t - 1) + u + 1)
                    nc.vector.reduce_max(top[:, u, :], pe_tile, axis=AX.X).then_inc(top_ready, 1)
                    dve.wait_ge(top_ready, 2 * t + u + 1)
                    ge(dve, prob_ready, 2 * (t - 1) + u + 1)
                    nc.vector.tensor_tensor(score[:, u].rearrange("p (h k) -> p h k", h=NPAIR), pe_tile,
                                            top[:, u, :].unsqueeze(2).broadcast_to([P, NPAIR, S]),
                                            ALU.subtract).then_inc(score_ready, 1)

            def over_sums(t, p):
                dve.wait_ge(pv_done, 2 * t + 2)
                for u in range(2):
                    o = ps_o[:, 136 * u:136 * (u + 1)].rearrange("p (h d) -> p h d", h=NPAIR)
                    ge(dve, on_ready, 2 * (t - 1) + u + 1)
                    nc.vector.reciprocal(rsum[:, u, :], o[:, :, VD]).then_inc(rsum_ready, 1)
                for u in range(2):
                    o = ps_o[:, 136 * u:136 * (u + 1)].rearrange("p (h d) -> p h d", h=NPAIR)
                    dve.wait_ge(rsum_ready, 2 * t + u + 1)
                    ge(dve, comb_done, t)
                    if self_diff:
                        nc.vector.tensor_tensor(on[:, u], o[:, :, 0:VD], rsum[:, u, :].unsqueeze(2).broadcast_to([P, NPAIR, VD]),
                                                ALU.mult).then_inc(on_ready, 1)
                    else:
                        nc.vector.tensor_tensor(rhalf[:, u], rsum[:, u, :].unsqueeze(2).broadcast_to([P, NPAIR, 2]),
                                                c["half"].unsqueeze(1).broadcast_to([P, NPAIR, 2]), ALU.mult).then_inc(rhalf_ready, 1)
                        dve.wait_ge(rhalf_ready, 2 * t + u + 1)
                        nc.vector.tensor_tensor(on[:, u].rearrange("p h (a d) -> p h a d", a=2),
                                                o[:, :, 0:VD].rearrange("p h (a d) -> p h a d", a=2),
                                                rhalf[:, u].unsqueeze(3).broadcast_to([P, NPAIR, 2, HD]), ALU.mult).then_inc(on_ready, 1)

            def head_centre(t, p):
                d = ps_d[:, 0:P].rearrange("p (h d) -> p h d", h=NPAIR)
                dve.wait_ge(comb_done, t + 1)
                ge(dve, hn_done, t)
                nc.vector.reduce_sum(hn_m[:], d, axis=AX.X).then_inc(hn_step, 1)
                dve.wait_ge(hn_step, 3 * t + 1)
                nc.vector.scalar_tensor_tensor(hn_c[:], hn_m[:].unsqueeze(2).broadcast_to([P, NPAIR, VD]), -1.0 / VD, d,
                                               ALU.mult, ALU.add).then_inc(hn_step, 1)
                dve.wait_ge(hn_step, 3 * t + 2)
                nc.vector.scalar_tensor_tensor(hn_sq[:], hn_c[:], 1.0 / VD, hn_c[:], ALU.mult, ALU.mult).then_inc(hn_step, 1)
                dve.wait_ge(hn_step, 3 * t + 3)
                nc.vector.reduce_sum(hn_v[:], hn_sq[:], axis=AX.X).then_inc(hn_var, 1)

            def head_scale(t, p):
                dve.wait_ge(hn_rstd, 2 * t + 2)
                ge(dve, hnt_done, t)
                nc.vector.tensor_tensor(hn_o[:], hn_c[:], hn_r[:, 1, :].unsqueeze(2).broadcast_to([P, NPAIR, VD]),
                                        ALU.mult).then_inc(hn_done, 1)

            def statistics(t, p):
                dve.wait_ge(wo_done, t + 1)
                norm.statistics(dve, t, ps_w, residual(t))

            def scaling(t, p):
                ge(dve, back_done, t)
                ge(dve, res_ready, t)
                norm.scaling(dve, t)

            if self_diff:
                dve.wait_ge(lam_step, 6)
                dve.wait_ge(*c["x_loaded"])
                pipelined(dve, [(1, softmax), (-3, scaling), (-1, head_centre), (-2, statistics), (0, over_sums),
                                (-1, head_scale)])
            else:
                pipelined(dve, [(1, softmax), (-1, statistics), (0, over_sums), (-1, scaling)])

        @block.scalar
        def _(act):
            if self_diff:
                act.wait_ge(lam_step, 2)
                nc.scalar.activation(lam[:, 2:4], lam[:, 0:2], ACT.Exp).then_inc(lam_exp, 1)
            for n in range(8):
                act.wait_ge(proj_done, n + 1)
                dst = (kt if n < 4 else qt)[:, CHUNK * (n % 4):CHUNK * (n % 4 + 1)]
                bias = w["kb"] if n < 4 else w["qb"]
                if bias is None:
                    nc.scalar.activation(dst, ps_s[n % 2][:], ACT.Copy).then_inc(proj_out, 1)
                else:
                    nc.scalar.activation(dst, ps_s[n % 2][:], ACT.Identity, bias=bias).then_inc(proj_out, 1)

            def tokens_twice(t, p):
                ge(act, values_done, 2 * (t - 1))
                nc.scalar.activation(xdup[:, p], kv_src[:, bass.ds(P * t, P)].rearrange("p (u s) -> p u s", u=2).unsqueeze(2)
                                     .broadcast_to([P, 2, 2, S]), ACT.Copy).then_inc(xdup_ready, 1)

            def queries(t, p):
                ge(act, scores_done, 2 * (t - 1))
                for a in range(2):
                    nc.scalar.activation(q2[:, p, :, a, :], qt[:, bass.ds(P * t, P)].rearrange("p (u s) -> p u s", u=2),
                                         ACT.Copy, scale=c["parity"][:, a:a + 1]).then_inc(q2_ready, 1)

            def value_blocks(t, p):
                act.wait_ge(values_done, 2 * t + 2)
                for h in range(2):
                    nc.scalar.activation(vb[:, bass.ds(2 * t, 2), :, h, 0:VD],
                                         ps_v[:, 0:2 * P].rearrange("p (u j h d) -> p u j h d", u=2, j=4, h=2)[:, :, :, h, :],
                                         ACT.Copy, scale=c["half"][:, h:h + 1]).then_inc(vb_ready, 1)

            def exponent(t, p):
                for u in range(2):
                    act.wait_ge(score_ready, 2 * t + u + 1)
                    ge(act, transp_done, 2 * (t - 1) + u + 1)
                    nc.scalar.activation(prob[:, u, :], score[:, u, :], ACT.Exp).then_inc(prob_ready, 1)

            def probs_t(t, p):
                for u in range(2):
                    act.wait_ge(transp_done, 2 * t + u + 1)
                    ge(act, pv_done, 2 * (t - 1) + u + 1)
                    nc.scalar.activation(probt[:, u, :], ps_t[u][:], ACT.Copy).then_inc(probt_ready, 1)

            def feature_major(t, p):
                act.wait_ge(back_done, t + 1)
                if self_diff:
                    act.wait_ge(hnt_done, upto(t + 3, NT))
                else:
                    ge(act, gate_done, t)
                    nc.scalar.activation(xnt[:], ps_a[:, 0:P], ACT.Copy).then_inc(xnt_ready, 1)
                nc.scalar.activation(xt_next[:, bass.ds(P * t, P)], ps_a[:, 0:P], ACT.Copy).then_inc(xt_ready, 1)

            def outputs_t(t, p):
                if self_diff:
                    act.wait_ge(hnt_done, t + 1)
                    ge(act, wo_done, t)
                    nc.scalar.activation(ot[:], ps_a[:, P:2 * P], ACT.Identity, bias=w["ob"], scale=w["og"]).then_inc(ot_ready, 1)
                else:
                    act.wait_ge(comb_done, t + 1)
                    ge(act, wo_done, t)
                    nc.scalar.activation(ot[:], ps_d[:, 0:P], ACT.Identity, bias=w["vb"]).then_inc(ot_ready, 1)

            def gate_logits(t, p):
                act.wait_ge(gate_done, t + 1)
                nc.scalar.activation(logits[:, t, :], ps_a[:, 2 * P:2 * P + NE], ACT.Copy).then_inc(gate_out, 1)

            if self_diff:
                pipelined(act, [(-4, feature_major), (-2, outputs_t), (0, probs_t), (2, tokens_twice), (2, queries),
                                (1, value_blocks), (1, exponent)])
            else:
                pipelined(act, [(-1, outputs_t), (-2, feature_major), (0, probs_t), (2, tokens_twice), (2, queries),
                                (1, value_blocks), (-2, gate_logits), (1, exponent)])

        @block.gpsimd
        def _(pool):
            pool.wait_ge(proj_out, 4)

            def keys(t, p):
                for u in range(2):
                    nc.gpsimd.tensor_tensor(km[:, 2 * t + u, :].rearrange("p (h k) -> p h k", h=NPAIR),
                                            kt[:, bass.ds(P * t + S * u, S)].unsqueeze(1).broadcast_to([P, NPAIR, S]),
                                            c["pair"].unsqueeze(2).broadcast_to([P, NPAIR, S]), ALU.mult).then_inc(km_ready, 1)

            def head_power(t, p):
                pool.wait_ge(hn_var, t + 1)
                ge(pool, hn_done, t)
                nc.gpsimd.tensor_tensor(hn_r[:, 0, :], hn_v[:], c["eps"], ALU.add).then_inc(hn_rstd, 1)
                pool.wait_ge(hn_rstd, 2 * t + 1)
                nc.gpsimd.tensor_tensor(hn_r[:, 1, :], hn_r[:, 0, :], c["neghalf"], ALU.pow).then_inc(hn_rstd, 1)

            def power(t, p):
                norm.power(pool, t, c["neghalf"][:, 0:1], c["eps"][:, 0:1])

            def keep_residual(t, p):
                pool.wait_ge(norm.normed, t + 1)
                if self_diff:
                    nc.gpsimd.tensor_tensor(res_next[:, t, :], norm.out[:], w["next_bias"], ALU.add).then_inc(res_ready, 1)
                else:
                    nc.gpsimd.tensor_copy(res_next[:, t, :], norm.out[:]).then_inc(res_ready, 1)

            if self_diff:
                pipelined(pool, [(-3, keep_residual), (-1, head_power), (-2, power), (3, keys)])
            else:
                pipelined(pool, [(-1, power), (3, keys), (-1, keep_residual)])
            pool.wait_ge(res_ready, NT)


def route(nc, ctx, tag, logits, iota, temp):
    sb = lambda name, shape, dt=F32: ctx.enter_context(nc.sbuf_tensor(f"{tag}_{name}", shape, dt))
    sem = lambda name: ctx.enter_context(nc.semaphore(f"{tag}_{name}"))
    ranked, ex = sb("ranked", [P, NT, NE]), sb("ex", [P, NT, NE])
    place, placef = sb("place", [P, NT, NE], U32), sb("placef", [P, NT, 2])
    prob = sb("prob", [P, 2, NT])
    total = sb("total", [P, NT])
    one, two, weight = sb("one", [P, NT, NE]), sb("two", [P, NT, NE]), sb("weight", [P, NT, NE])
    step, ready, exped = sem("step"), sem("ready"), sem("exped")
    weights_ready = sem("weights_ready")

    def before(dve):
        for t in range(NT):
            nc.vector.max(ranked[:, t, :], logits[:, t, :]).then_inc(step, 1)
        for t in range(NT):
            dve.wait_ge(step, t + 1)
            nc.vector.max_index(place[:, t, :], ranked[:, t, :], logits[:, t, :]).then_inc(step, 1)
        nc.vector.tensor_tensor(ex[:], ranked[:], ranked[:, :, 0:1].broadcast_to([P, NT, NE]), ALU.subtract).then_inc(ready, 1)

    def exponent(act):
        act.wait_ge(ready, 1)
        nc.scalar.activation(ex[:], ex[:], ACT.Exp, scale=1.0 / temp).then_inc(exped, 1)

    def after(dve):
        dve.wait_ge(step, 2 * NT)
        nc.vector.tensor_copy(placef[:], place[:, :, 0:2]).then_inc(step, 1)
        dve.wait_ge(exped, 1)
        nc.vector.reduce_sum(total[:], ex[:], axis=AX.X).then_inc(step, 1)
        dve.wait_ge(step, 2 * NT + 2)
        nc.vector.reciprocal(prob[:, 0, :], total[:]).then_inc(step, 1)
        nc.vector.tensor_tensor(one[:], iota.unsqueeze(1).broadcast_to([P, NT, NE]),
                                placef[:, :, 0:1].broadcast_to([P, NT, NE]), ALU.is_equal).then_inc(step, 1)
        nc.vector.tensor_tensor(two[:], iota.unsqueeze(1).broadcast_to([P, NT, NE]),
                                placef[:, :, 1:2].broadcast_to([P, NT, NE]), ALU.is_equal).then_inc(step, 1)
        dve.wait_ge(step, 2 * NT + 3)
        nc.vector.tensor_tensor(prob[:, 1, :], ex[:, :, 1], prob[:, 0, :], ALU.mult).then_inc(step, 1)
        dve.wait_ge(step, 2 * NT + 6)
        nc.vector.tensor_tensor(one[:], one[:], prob[:, 0, :].unsqueeze(2).broadcast_to([P, NT, NE]), ALU.mult).then_inc(step, 1)
        nc.vector.tensor_tensor(two[:], two[:], prob[:, 1, :].unsqueeze(2).broadcast_to([P, NT, NE]), ALU.mult).then_inc(step, 1)
        dve.wait_ge(step, 2 * NT + 8)
        nc.vector.tensor_tensor(weight[:], one[:], two[:], ALU.add).then_inc(weights_ready, 1)
        dve.wait_ge(weights_ready, 1)

    return before, exponent, after, weight


def first_experts(nc, banks, w, xt, x_res, logits, xpos, c, background):
    with ExitStack() as ctx:
        def sb(name, shape, dt=F32):
            return ctx.enter_context(nc.sbuf_tensor(f"moe_{name}", shape, dt))

        def sem(name):
            return ctx.enter_context(nc.semaphore(f"moe_{name}"))

        xs = sb("xs", [P, 2, P])
        act_out = sb("act_out", [P, 2, NE, P])
        mixed = sb("mixed", [P, 2, 2, P])
        mixt = sb("mixt", [P, P])
        norm = Norm(nc, ctx, "moe")
        before, exponent, after, weight = route(nc, ctx, "moe_route", logits, c["iota"], 1.0)
        xs_ready, expert_done, silu_ready = sem("xs_ready"), sem("expert_done"), sem("silu_ready")
        mix_step, mt_done, mt_ready, comb_done = sem("mix_step"), sem("mt_done"), sem("mt_ready"), sem("comb_done")
        back_done, xp_ready = sem("back_done"), sem("xp_ready")
        ps_e, ps_m, ps_y, ps_b = banks[0:4], banks[4], banks[5], banks[6]
        xpos_v = xpos[:].rearrange("f (p s) -> f s p", s=B)
        block = ctx.enter_context(nc.Block())
        block.sync(background)

        @block.tensor
        def _(pe):
            def experts(t, p):
                pe.wait_ge(xs_ready, t + 1)
                for h in range(2):
                    ge(pe, silu_ready, 2 * (t - 2) + h + 1)
                    cols = slice(CHUNK * h, CHUNK * (h + 1))
                    nc.tensor.matmul(ps_e[2 * p + h][:], c["ones3"], w["eb3"][:, cols], start=True, stop=False)
                    nc.tensor.matmul(ps_e[2 * p + h][:], xs[:, p], w["expert"][:, cols], start=False, stop=True).then_inc(expert_done, 1)

            def mixed_t(t, p):
                pe.wait_ge(mix_step, NE * (t + 1))
                ge(pe, mt_ready, t)
                for k in range(2):
                    last = nc.tensor.matmul(ps_m[:, 0:P], mixed[:, p, k], c["ident"], start=k == 0, stop=k == 1)
                last.then_inc(mt_done, 1)

            def combine(t, p):
                pe.wait_ge(mt_ready, t + 1)
                ge(pe, norm.y_ready, t)
                nc.tensor.matmul(ps_y[:, 0:P], mixt[:], w["combine"], start=True, stop=True).then_inc(comb_done, 1)

            def back(t, p):
                pe.wait_ge(norm.normed, t + 1)
                ge(pe, xp_ready, t)
                nc.tensor.transpose(ps_b[:, 0:P], norm.out[:], c["ident"]).then_inc(back_done, 1)

            pipelined(pe, [(0, mixed_t), (-1, combine), (-3, back), (2, experts)])

        @block.scalar
        def _(act):
            exponent(act)

            def silu(t, p):
                for h in range(2):
                    act.wait_ge(expert_done, 2 * t + h + 1)
                    ge(act, mix_step, NE * (t - 2) + 4 * h + 4)
                    nc.scalar.activation(act_out[:, p, 4 * h:4 * h + 4, :], ps_e[2 * p + h][:].rearrange("p (e d) -> p e d", e=4),
                                         ACT.Silu).then_inc(silu_ready, 1)

            def mixed_t(t, p):
                act.wait_ge(mt_done, t + 1)
                ge(act, comb_done, t)
                nc.scalar.activation(mixt[:], ps_m[:, 0:P], ACT.Copy).then_inc(mt_ready, 1)

            def positions(t, p):
                act.wait_ge(back_done, t + 1)
                nc.scalar.activation(xpos_v[:, bass.ds(2 * t, 2), :], ps_b[:, 0:P].rearrange("f (s p) -> f s p", s=2),
                                     ACT.Copy).then_inc(xp_ready, 1)

            pipelined(act, [(0, mixed_t), (-3, positions), (2, silu)])

        @block.vector
        def _(dve):
            before(dve)
            after(dve)

            def mix(t, p):
                for e in range(NE):
                    if e % 4 == 0:
                        dve.wait_ge(silu_ready, 2 * t + e // 4 + 1)
                    if e == 0:
                        ge(dve, mt_done, t - 1)
                    if e < 2:
                        ins = nc.vector.tensor_scalar(mixed[:, p, e], act_out[:, p, e, :], weight[:, t, e:e + 1], None, ALU.mult)
                    else:
                        dve.wait_ge(mix_step, NE * t + e - 1)
                        ins = nc.vector.scalar_tensor_tensor(mixed[:, p, e % 2], act_out[:, p, e, :], weight[:, t, e:e + 1],
                                                             mixed[:, p, e % 2],
                                                             ALU.mult, ALU.add)
                    ins.then_inc(mix_step, 1)

            def statistics(t, p):
                dve.wait_ge(comb_done, t + 1)
                norm.statistics(dve, t, ps_y[:, 0:P], x_res[:, t, :])

            def scaling(t, p):
                ge(dve, back_done, t)
                norm.scaling(dve, t)

            pipelined(dve, [(1, mix), (-2, scaling), (-1, statistics)])

        @block.gpsimd
        def _(pool):
            def tokens(t, p):
                ge(pool, expert_done, 2 * (t - 1))
                nc.gpsimd.tensor_copy(xs[:, p], xt[:, bass.ds(P * t, P)]).then_inc(xs_ready, 1)

            def power(t, p):
                norm.power(pool, t, c["neghalf"][:, 0:1], c["eps"][:, 0:1])

            pipelined(pool, [(3, tokens), (-1, power)])


def sequence_attention(nc, banks, w, xpos, ct, res, res_next, xt_next, c):
    with ExitStack() as ctx:
        def sb(name, shape, dt=F32):
            return ctx.enter_context(nc.sbuf_tensor(f"seq_{name}", shape, dt))

        def sem(name):
            return ctx.enter_context(nc.semaphore(f"seq_{name}"))

        xg = sb("xg", [P, 2, 2, P])
        q2 = sb("q2", [P, 2, NJ, 4, 2, B])
        kg = sb("kg", [P, 2, NJ, P])
        vg = sb("vg", [P, 2, 2, 4, P])
        qb = sb("qb", [P, 2, NJ, 4])
        score = sb("score", [P, 2, NJ, 2, B])
        prob = sb("prob", [P, 2, NJ, S])
        probn = sb("probn", [P, 2, NJ, S])
        probt = sb("probt", [P, 2, 4, P])
        top, total, rsum = sb("top", [P, 2, NJ]), sb("total", [P, 2, NJ]), sb("rsum", [P, 2, NJ])
        ot = sb("ot", [P, 2, 4, 2, 2, 2, B])
        csum, context = sb("csum", [P, 4, B]), sb("context", [P, P])
        norm = Norm(nc, ctx, "seq")
        ps_p, ps_s, ps_t, ps_o, ps_y = banks[0:2], banks[2:4], banks[4], banks[5:7], banks[7]

        xg_ready, q_done, k_done, v_done = sem("xg_ready"), sem("q_done"), sem("k_done"), sem("v_done")
        q_out, k_out, v_out = sem("q_out"), sem("k_out"), sem("v_out")
        setup, scores_done, top_ready, score_ready = sem("setup"), sem("scores_done"), sem("top_ready"), sem("score_ready")
        prob_ready, total_ready, rsum_ready, probn_ready = sem("prob_ready"), sem("total_ready"), sem("rsum_ready"), sem("probn_ready")
        transp_done, probt_ready, pv_done, ot_ready = sem("transp_done"), sem("probt_ready"), sem("pv_done"), sem("ot_ready")
        wo_done, rest_done, rest_ready = sem("wo_done"), sem("rest_done"), sem("rest_ready")
        back_done, xt_ready, res_ready = sem("back_done"), sem("xt_ready"), sem("res_ready")
        context_done = sem("context_done")
        block = ctx.enter_context(nc.Block())

        @block.tensor
        def _(pe):
            def queries(n):
                def part(t, p):
                    pe.wait_ge(xg_ready, 2 * t + 1)
                    ge(pe, v_out, 2 * t - 1 + n)
                    for j in range(4):
                        col = P * (4 * n + j)
                        last = nc.tensor.matmul(ps_p[n][:, P * j:P * (j + 1)], w["in"][:, col:col + P], xg[:, p, 0, :],
                                                start=True, stop=True)
                    last.then_inc(q_done, 1)
                return part

            def keys(n):
                def part(t, p):
                    pe.wait_ge(q_out, 4 * t + 2 + 2 * n)
                    for j in range(4):
                        col = P * (NJ + 4 * n + j)
                        last = nc.tensor.matmul(ps_p[n][:, P * j:P * (j + 1)], w["in"][:, col:col + P], xg[:, p, 0, :],
                                                start=True, stop=True)
                    last.then_inc(k_done, 1)
                return part

            def values(n):
                def part(t, p):
                    pe.wait_ge(xg_ready, 2 * t + 2)
                    pe.wait_ge(k_out, 8 * t + 4 + 4 * n)
                    nc.tensor.matmul(ps_p[n][:], xg[:, p, n, :],
                                     w["in"][:, 2 * H1 * D1:].rearrange("p (j a d) -> p a j d", a=2, d=P)[:, n],
                                     start=True, stop=True).then_inc(v_done, 1)
                return part

            def scores(t, p):
                if isinstance(t, int) and t == 0:
                    pe.wait_ge(setup, 5)
                    nc.tensor.matmul(ps_s[0][:, 0:P], csum[:].rearrange("f r b -> f (r b)"), w["x_w2"], start=True, stop=True
                                     ).then_inc(context_done, 1)
                    pe.wait_ge(setup, 6)
                pe.wait_ge(q_out, 4 * t + 4)
                pe.wait_ge(k_out, 8 * t + 8)
                for n in range(2):
                    ge(pe, score_ready, 4 * (t - 1) + 2 * n + 2)
                    for jj in range(4):
                        for s in range(2):
                            j = 2 * jj + (s ^ n)
                            last = nc.tensor.matmul(ps_s[n][:, S * (2 * jj + s):S * (2 * jj + s + 1)],
                                                    q2[:, p, j, 2 * n:2 * n + 2].rearrange("p b a s -> p (b a s)"),
                                                    kg[:, p, j, S * n:S * (n + 1)], start=True, stop=True)
                    last.then_inc(scores_done, 1)

            def transposes(n):
                def part(t, p):
                    pe.wait_ge(probn_ready, 2 * t + n + 1)
                    ge(pe, probt_ready, 2 * t + n)
                    if n == 0:
                        ge(pe, xt_ready, t - 2)
                    for j in range(4):
                        last = nc.tensor.transpose(ps_t[:, P * j:P * (j + 1)],
                                                   probn[:, n, 2 * j:2 * j + 2].rearrange("p a k -> p (a k)"), c["ident"])
                    last.then_inc(transp_done, 1)
                return part

            def weighted(n):
                def part(t, p):
                    pe.wait_ge(probt_ready, 2 * t + n + 1)
                    pe.wait_ge(v_out, 2 * t + 2)
                    ge(pe, ot_ready, 8 * t + 4 * n)
                    for jj in range(4):
                        for s in range(2):
                            rows = slice(64 * s, 64 * (s + 1))
                            last = nc.tensor.matmul(ps_o[s][:, P * jj:P * (jj + 1)], vg[rows, p, s ^ n, jj, :], probt[rows, n, jj, :],
                                                    start=True, stop=True)
                    last.then_inc(pv_done, 1)
                return part

            def project(t, p):
                pe.wait_ge(ot_ready, 8 * t + 8)
                pe.wait_ge(rest_ready, upto(t + 3, NT))
                ge(pe, norm.y_ready, t)
                for j in range(NJ):
                    last = nc.tensor.matmul(ps_y[:, 0:P], ot[:, p, j // 2, j % 2].rearrange("p n b s -> p (n b s)"), w["out"][:, j, :],
                                            start=j == 0, stop=j == NJ - 1)
                last.then_inc(wo_done, 1)

            def residual_t(t, p):
                pe.wait_ge(xg_ready, 2 * t + 1)
                ge(pe, rest_ready, t)
                ge(pe, norm.y_ready, t - 2)
                nc.tensor.transpose(ps_y[:, P:2 * P], xg[:, p, 0, :], c["ident"]).then_inc(rest_done, 1)

            def back(t, p):
                pe.wait_ge(norm.normed, t + 1)
                pe.wait_ge(probt_ready, upto(2 * (t + 3), 2 * NT))
                ge(pe, xt_ready, t)
                nc.tensor.transpose(ps_t[:, 0:P], norm.out[:], c["ident"]).then_inc(back_done, 1)

            pipelined(pe, [(1, scores), (2, queries(0)), (2, queries(1)), (-1, project), (0, transposes(0)), (2, keys(0)),
                           (0, transposes(1)), (2, keys(1)), (0, weighted(0)), (2, values(0)), (2, values(1)), (2, residual_t),
                           (0, weighted(1)), (-2, back)])

        @block.vector
        def _(dve):
            for a in range(2):
                nc.vector.tensor_scalar(qb[:, a], w["in_b"][:, 0:NJ].unsqueeze(2).broadcast_to([P, NJ, 4]), c["h2"][:, a:a + 1],
                                        None, ALU.mult).then_inc(setup, 1)
            nc.vector.memset(score[:], MASKED).then_inc(setup, 1)
            dve.wait_ge(setup, 3)

            def context_sum(t, p):
                if isinstance(t, int) and t == 0:
                    nc.vector.reduce_sum(csum[:, 0, :], ct.rearrange("f (b s) -> f b s", b=B), axis=AX.X).then_inc(setup, 1)
                    dve.wait_ge(setup, 4)
                    nc.vector.tensor_copy(csum[:, 1:4, :], csum[:, 0:1, :].broadcast_to([P, 3, B])).then_inc(setup, 1)

            def context_out(t, p):
                if isinstance(t, int) and t == 0:
                    dve.wait_ge(context_done, 1)
                    nc.vector.scalar_tensor_tensor(context[:], ps_s[0][:, 0:P], 1.0 / S, w["x_b"], ALU.mult, ALU.add).then_inc(setup, 1)

            def residual(t, p):
                dve.wait_ge(rest_done, t + 1)
                nc.vector.tensor_tensor(res[:, t, :], ps_y[:, P:2 * P], w["out_b"], ALU.add).then_inc(rest_ready, 1)

            def queries(n):
                def part(t, p):
                    dve.wait_ge(q_done, 2 * t + n + 1)
                    ge(dve, scores_done, 2 * (t - 1))
                    for a in range(2):
                        bias = qb[:, a, 4 * n:4 * n + 4].rearrange("p j b -> p (j b)").unsqueeze(2).broadcast_to([P, 16, B])
                        nc.vector.scalar_tensor_tensor(q2[:, p, 4 * n:4 * n + 4, :, a, :].rearrange("p j b s -> p (j b) s"),
                                                       ps_p[n][:].rearrange("p (j s) -> p j s", s=B), c["h2"][:, a:a + 1], bias,
                                                       ALU.mult, ALU.add).then_inc(q_out, 1)
                return part

            def values(n):
                def part(t, p):
                    dve.wait_ge(v_done, 2 * t + n + 1)
                    ge(dve, pv_done, 2 * (t - 1))
                    nc.vector.tensor_tensor(vg[:, p, n], ps_p[n][:].rearrange("p (j d) -> p j d", j=4),
                                            w["v_b"].rearrange("p (j a d) -> p a j d", a=2, d=P)[:, n], ALU.add).then_inc(v_out, 1)
                return part

            def softmax(n):
                def part(t, p):
                    dve.wait_ge(scores_done, 2 * t + n + 1)
                    ge(dve, prob_ready, 2 * (t - 1) + n + 1)
                    for b in range(2):
                        rows = slice(64 * b, 64 * (b + 1))
                        src = ps_s[n][rows].rearrange("p (j b s) -> p j b s", j=NJ, b=2)[:, :, b, :]
                        ge(dve, score_ready, 4 * (t - 1) + 2 * n + b + 1)
                        nc.vector.reduce_max(top[rows, n, :], src, axis=AX.X).then_inc(top_ready, 1)
                    for b in range(2):
                        rows = slice(64 * b, 64 * (b + 1))
                        src = ps_s[n][rows].rearrange("p (j b s) -> p j b s", j=NJ, b=2)[:, :, b, :]
                        dve.wait_ge(top_ready, 4 * t + 2 * n + b + 1)
                        nc.vector.tensor_tensor(score[rows, n, :, b, :], src, top[rows, n, :].unsqueeze(2).broadcast_to([64, NJ, B]),
                                                ALU.subtract).then_inc(score_ready, 1)
                return part

            def sums(t, p):
                for n in range(2):
                    dve.wait_ge(prob_ready, 2 * t + n + 1)
                    ge(dve, probn_ready, 2 * (t - 1) + n + 1)
                    nc.vector.reduce_sum(total[:, n, :], prob[:, n], axis=AX.X).then_inc(total_ready, 1)
                    dve.wait_ge(total_ready, 2 * t + n + 1)
                    nc.vector.reciprocal(rsum[:, n, :], total[:, n, :]).then_inc(rsum_ready, 1)

            def statistics(t, p):
                dve.wait_ge(wo_done, t + 1)
                norm.statistics(dve, t, ps_y[:, 0:P], res[:, t, :])

            def scaling(t, p):
                ge(dve, back_done, t)
                ge(dve, res_ready, t)
                norm.scaling(dve, t)

            pipelined(dve, [(1, context_out), (1, softmax(0)), (2, queries(0)), (2, queries(1)), (2, context_sum),
                            (1, softmax(1)), (-1, statistics), (1, sums),
                            (2, values(0)), (-1, scaling), (2, values(1)), (2, residual)])

        @block.scalar
        def _(act):
            def exponent(t, p):
                for n in range(2):
                    act.wait_ge(score_ready, 4 * t + 2 * n + 2)
                    ge(act, probn_ready, 2 * (t - 1) + n + 1)
                    nc.scalar.activation(prob[:, n], score[:, n].rearrange("p j b s -> p j (b s)"), ACT.Exp).then_inc(prob_ready, 1)

            def keys(n):
                def part(t, p):
                    act.wait_ge(k_done, 2 * t + n + 1)
                    ge(act, scores_done, 2 * (t - 1))
                    for j in range(4 * n, 4 * n + 4):
                        nc.scalar.activation(kg[:, p, j, :], ps_p[n][:, P * (j % 4):P * (j % 4 + 1)], ACT.Identity,
                                             bias=w["in_b"][:, NJ + j:NJ + j + 1]).then_inc(k_out, 1)
                return part

            def probs_t(n):
                def part(t, p):
                    act.wait_ge(transp_done, 2 * t + n + 1)
                    ge(act, pv_done, 2 * (t - 1) + n + 1)
                    nc.scalar.activation(probt[:, n], ps_t[:].rearrange("p (j q) -> p j q", j=4), ACT.Copy).then_inc(probt_ready, 1)
                return part

            def outputs_t(n):
                def part(t, p):
                    act.wait_ge(pv_done, 2 * t + n + 1)
                    ge(act, wo_done, t - 1)
                    for s in range(2):
                        for a in range(2):
                            rows = slice(64 * a, 64 * (a + 1))
                            src = ps_o[s][rows].rearrange("p (j b a s) -> p j b a s", j=4, b=2, a=2)[:, :, :, a, :]
                            nc.scalar.activation(ot[rows, p, :, s ^ n, n], src, ACT.Copy).then_inc(ot_ready, 1)
                return part

            def feature_major(t, p):
                act.wait_ge(back_done, t + 1)
                nc.scalar.activation(xt_next[:, bass.ds(P * t, P)], ps_t[:, 0:P], ACT.Copy).then_inc(xt_ready, 1)

            pipelined(act, [(0, probs_t(0)), (2, keys(0)), (0, probs_t(1)), (2, keys(1)), (1, exponent), (0, outputs_t(0)),
                            (0, outputs_t(1)), (-2, feature_major)])

        @block.gpsimd
        def _(pool):
            def tokens(t, p):
                ge(pool, v_done, 2 * (t - 1))
                ge(pool, rest_done, t - 1)
                nc.gpsimd.tensor_copy(xg[:, p, 0, :], xpos[:, bass.ds(P * t, P)]).then_inc(xg_ready, 1)
                nc.gpsimd.tensor_copy(xg[:, p, 1, 0:S], xpos[:, bass.ds(P * t + S, S)])
                nc.gpsimd.tensor_copy(xg[:, p, 1, S:P], xpos[:, bass.ds(P * t, S)]).then_inc(xg_ready, 1)

            def normalise(t, p):
                for n in range(2):
                    pool.wait_ge(rsum_ready, 2 * t + n + 1)
                    ge(pool, transp_done, 2 * (t - 1) + n + 1)
                    nc.gpsimd.tensor_tensor(probn[:, n], prob[:, n], rsum[:, n, :].unsqueeze(2).broadcast_to([P, NJ, S]),
                                            ALU.mult).then_inc(probn_ready, 1)

            def power(t, p):
                norm.power(pool, t, c["neghalf"][:, 0:1], c["eps"][:, 0:1])

            def keep_residual(t, p):
                if isinstance(t, int) and t == 0:
                    pool.wait_ge(setup, 6)
                pool.wait_ge(norm.normed, t + 1)
                nc.gpsimd.tensor_tensor(res_next[:, t, :], norm.out[:], context[:], ALU.add).then_inc(res_ready, 1)

            pipelined(pool, [(1, normalise), (3, tokens), (-1, power), (-1, keep_residual)])
            pool.wait_ge(res_ready, NT)


def position_linear(nc, banks, w, xt, x_res, logits, rows, rows_dram, stored, res_next, c):
    with ExitStack() as ctx:
        def sb(name, shape, dt=F32):
            return ctx.enter_context(nc.sbuf_tensor(f"lin_{name}", shape, dt))

        def sem(name):
            return ctx.enter_context(nc.semaphore(f"lin_{name}"))

        xs, xnt = sb("xs", [P, 2, P]), sb("xnt", [P, 2, P])
        y, z, zn = sb("y", [P, 2, P]), sb("z", [P, 2, P]), sb("zn", [P, 2, P])
        stats, zstats = sb("stats", [P, 6]), sb("zstats", [P, 6])
        mv = sb("mv", [P, 2, 2, 2])
        rstd = sb("rstd", [P, 2, 2, 2])
        xs_ready, lin_done, back_done, xnt_ready = sem("xs_ready"), sem("lin_done"), sem("back_done"), sem("xnt_ready")
        outer_step, inner_step, rstd_step, zn_ready = sem("outer_step"), sem("inner_step"), sem("rstd_step"), sem("zn_ready")
        rows_ready, gate_done, gate_out, kept = sem("rows_ready"), sem("gate_done"), sem("gate_out"), sem("kept")
        ps_y, ps_b, ps_g = banks[0:2], banks[2:4], banks[4:6]
        block = ctx.enter_context(nc.Block())

        @block.tensor
        def _(pe):
            def linear(t, p):
                pe.wait_ge(xs_ready, t + 1)
                ge(pe, outer_step, 3 * (t - 2) + 1)
                nc.tensor.matmul(ps_y[p][:, 0:P], xs[:, p], w["x_w1"], start=True, stop=True).then_inc(lin_done, 1)

            def back(t, p):
                pe.wait_ge(zn_ready, t + 1)
                ge(pe, xnt_ready, t - 1)
                nc.tensor.transpose(ps_b[p][:, 0:P], zn[:, p], c["ident"]).then_inc(back_done, 1)

            def gate(t, p):
                pe.wait_ge(xnt_ready, t + 1)
                ge(pe, gate_out, t - 1)
                nc.tensor.matmul(ps_g[p][:, 0:NE], xnt[:, p], w["router"], start=True, stop=True).then_inc(gate_done, 1)

            pipelined(pe, [(1, linear), (-4, back), (-5, gate)])

        @block.vector
        def _(dve):
            def inner_scaling(t, p):
                dve.wait_ge(rstd_step, 2 * (t + 2) + 2)
                ge(dve, rows_ready, t - 1)
                ge(dve, back_done, t - 1)
                nc.vector.tensor_scalar(zn[:, p], z[:, p], mv[:, p, 1, 0:1], rstd[:, p, 1, 1:2],
                                        ALU.subtract, ALU.mult).then_inc(zn_ready, 1)

            def scaling(t, p):
                dve.wait_ge(rstd_step, 2 * t + 2)
                ge(dve, kept, t - 1)
                ge(dve, zn_ready, t - 1)
                nc.vector.tensor_scalar(z[:, p], y[:, p], mv[:, p, 0, 0:1], rstd[:, p, 1, 0:1],
                                        ALU.subtract, ALU.mult).then_inc(inner_step, 1)

            def total(t, p):
                dve.wait_ge(lin_done, t + 1)
                ge(dve, inner_step, 3 * (t - 2) + 1)
                nc.vector.tensor_tensor(y[:, p], ps_y[p][:, 0:P], x_res[:, t, :], ALU.add).then_inc(outer_step, 1)

            def inner_statistics(t, p):
                dve.wait_ge(inner_step, 3 * t + 1)
                nc.vector.bn_stats(zstats[:], z[:, p]).then_inc(inner_step, 1)

            def statistics(t, p):
                dve.wait_ge(outer_step, 3 * t + 1)
                nc.vector.bn_stats(stats[:], y[:, p]).then_inc(outer_step, 1)

            def inner_moments(t, p):
                dve.wait_ge(inner_step, 3 * t + 2)
                ge(dve, zn_ready, t - 1)
                dve.nop(nofuse=True)
                nc.vector.bn_aggr(mv[:, p, 1, :], zstats[:]).then_inc(inner_step, 1)

            def moments(t, p):
                dve.wait_ge(outer_step, 3 * t + 2)
                dve.nop(nofuse=True)
                nc.vector.bn_aggr(mv[:, p, 0, :], stats[:]).then_inc(outer_step, 1)

            pipelined(dve, [(-4, inner_scaling), (-2, scaling), (0, total), (-2, inner_statistics), (0, statistics),
                            (-2, inner_moments), (0, moments)])

        @block.scalar
        def _(act):
            def tokens(t, p):
                ge(act, lin_done, t - 1)
                nc.scalar.activation(xs[:, p], xt[:, bass.ds(P * t, P)], ACT.Copy).then_inc(xs_ready, 1)

            def keep(t, p):
                act.wait_ge(inner_step, 3 * t + 1)
                nc.scalar.activation(res_next[:, t, :], z[:, p], ACT.Copy, scale=2.0).then_inc(kept, 1)

            def keep_rows(t, p):
                act.wait_ge(zn_ready, t + 1)
                nc.scalar.activation(rows[:, bass.ds(P * t, P)], zn[:, p], ACT.Copy).then_inc(rows_ready, 1)

            def feature_major(t, p):
                act.wait_ge(back_done, t + 1)
                ge(act, gate_done, t - 1)
                nc.scalar.activation(xnt[:, p], ps_b[p][:, 0:P], ACT.Identity, bias=w["beta"], scale=w["gamma"]).then_inc(xnt_ready, 1)

            def gate_logits(t, p):
                act.wait_ge(gate_done, t + 1)
                nc.scalar.activation(logits[:, t, :], ps_g[p][:, 0:NE], ACT.Copy).then_inc(gate_out, 1)

            pipelined(act, [(2, tokens), (-5, gate_logits), (-2, keep), (-4, keep_rows), (-4, feature_major)])
            act.wait_ge(kept, NT)
            act.wait_ge(rows_ready, NT)

        @block.sync
        def _(sp):
            for t in range(0, NT, 4):
                sp.wait_ge(rows_ready, t + 4)
                sp.dma_start(rows_dram[P * t:P * (t + 4), :].rearrange("(t p) d -> p t d", p=P),
                             rows[:, P * t:P * (t + 4)].rearrange("p (t d) -> p t d", d=P)).then_inc(stored, 16)

        @block.gpsimd
        def _(pool):
            def powers(t, p, which=slice(0, 2)):
                if which.start == 0:
                    pool.wait_ge(outer_step, 3 * t + 3)
                ge(pool, inner_step, 3 * (t - 2) + 3)
                ge(pool, zn_ready, t - 3)
                nc.gpsimd.tensor_tensor(rstd[:, p, 0, which], mv[:, p, which, 1], c["eps"][:, which], ALU.add).then_inc(rstd_step, 1)
                pool.wait_ge(rstd_step, 2 * t + 1)
                nc.gpsimd.tensor_tensor(rstd[:, p, 1, which], rstd[:, p, 0, which], c["neghalf"][:, which],
                                        ALU.pow).then_inc(rstd_step, 1)

            def step(t, p):
                powers(t, p, slice(0, 1) if isinstance(t, int) and t < 2 else slice(0, 2))

            pipelined(pool, [(0, step)], before=4)
            for t in (NT, NT + 1):
                powers(t, t % 2, slice(1, 2))


def last_experts(nc, banks, w, prepared, rows_dram, x_res, logits, results, out_dram, c):
    with ExitStack() as ctx:
        def sb(name, shape, dt=F32):
            return ctx.enter_context(nc.sbuf_tensor(f"ffn_{name}", shape, dt))

        def sem(name):
            return ctx.enter_context(nc.semaphore(f"ffn_{name}"))

        ranked, ex, place = sb("ranked", [P, NT, NE]), sb("ex", [P, NT, NE]), sb("place", [P, NT, NE], U32)
        placef, total, prob = sb("placef", [P, NT, 2]), sb("total", [P, NT]), sb("prob", [P, 2, NT])
        mask = sb("mask", [P, 2, NT, NE])
        chosen = sb("chosen", [P, NT, NE])
        upto_t = [sb(f"upto{k}", [P, NT, NE]) for k in range(2)]
        rank, picked = sb("rank", [P, NT, NE]), sb("picked", [P, 2, NT, NE])
        many, low = sb("many", [P, NE, NT]), sb("low", [P, NE, NE])
        tiles, base, end, offset = sb("tiles", [P, NE]), sb("base", [P, NE]), sb("end", [P, NE]), sb("offset", [P, NE])
        slotf, slot = sb("slotf", [P, 2, NT]), sb("slot", [P, 2, NT], U32)
        past, ownerf, owner = sb("past", [P, SLOTS, NE]), sb("ownerf", [P, SLOTS]), sb("owner", [P, SLOTS], I32)
        owners = sb("owners", [P, SLOTS], I32)
        tile_u, place_u = sb("tile_u", [P, 2, NT], U32), sb("place_u", [P, 2, NT], U32)
        tilef, inf = sb("tilef", [P, 2, NT]), sb("inf", [P, 2, NT])
        in_tile, at_place = sb("in_tile", [P, 2 * NT, SLOTS]), sb("at_place", [P, 2 * NT, P], BF16)
        takes = sb("takes", [P, 2 * NT, 2, SLOTS], BF16)
        taken_f = sb("taken_f", [P, SLOTS])
        second, source_f, sources = sb("second", [P, SLOTS]), sb("source_f", [P, SLOTS]), sb("sources", [P, SLOTS], U32)
        empty, spare, targets = sb("empty", [P, SLOTS]), sb("spare", [P, SLOTS]), sb("targets", [P, SLOTS], U32)
        xs, xst = sb("xs", [P, 2, P]), sb("xst", [P, 2, P])
        source, target = sb("source", [P, 2], U32), sb("target", [P, 2], U32)
        hid, hidt = sb("hid", [P, 2, FF]), sb("hidt", [P, 2, NF, P])
        ys = sb("ys", [P, 2, P])
        taken = sb("taken", [P, NT, 2, P])
        part_sum, y = sb("part_sum", [P, NT, P]), sb("y", [P, NT, P])
        stats, mv, rstd = sb("stats", [P, NT, 6]), sb("mv", [P, NT, 2]), sb("rstd", [P, 2, NT])
        shift = sb("shift", [P, 2, NT])
        yout = sb("yout", [P, NT, P])

        GROUP = 4
        step, exped, counted, inverted = sem("step"), sem("exped"), sem("counted"), sem("inverted")
        in_tile_ready = sem("in_tile_ready")
        xs_in = [sem(f"xs_in{k}") for k in range(2)]
        ys_sent = [sem(f"ys_sent{k}") for k in range(2)]
        taken_in = [sem(f"taken_in{k}") for k in range(NT // GROUP)]
        xst_done, xst_ready, hid_done, silu_ready = sem("xst_done"), sem("xst_ready"), sem("hid_done"), sem("silu_ready")
        hidt_done, hidt_ready, out_done, ys_ready = sem("hidt_done"), sem("hidt_ready"), sem("out_done"), sem("ys_ready")
        source_ready, target_ready = sem("source_ready"), sem("target_ready")
        sum_step, rstd_ready, normed, out_sent = sem("sum_step"), sem("rstd_ready"), sem("normed"), sem("out_sent")
        ps_x, ps_h, ps_t, ps_z, ps_r = banks[0], banks[1:3], banks[3:5], banks[5:7], banks[7]
        ps_i = banks[6]
        PLACED = 2 * NT
        EX, PLACEF, MASKS, CHOSEN, SUMS, RANK = (PLACED + n for n in (1, 2, 4, 5, 13, 14))
        TOTAL, FIRST, PROBS, MANY, TILES, LOW, BASE, OFFSET = (RANK + n for n in range(1, 9))
        SLOTALL, PICKED, SLOTF, SLOT, SPLIT, SPLITF = (OFFSET + n for n in (1, 2, 3, 4, 6, 8))
        PART = NT // 2
        MASKED_ROWS = SPLITF + 2 * (2 * NT // PART)
        END, PAST, OWNERF, OWNER, OWNERS, REST = (MASKED_ROWS + n for n in range(1, 7))
        TAKEN, SECOND, EMPTY, SOURCEF, SPARE, LISTS = (REST + n for n in (1, 2, 3, 4, 5, 7))
        block = ctx.enter_context(nc.Block())

        def arrived(p, t):
            return 8 * t + 16 - 8 * p

        def outputs(engine, tiles):
            for t in tiles:
                engine.wait_ge(normed, t + 1)
                engine.dma_start(out_dram[:, 4 * t:4 * t + 4, :].rearrange("s p d -> p s d"), yout[:, t, :]).then_inc(out_sent, 16)

        @block.sync
        def _(sp):
            for p in range(2):
                sp.wait_ge(ys_sent[p], arrived(p, SLOTS - 1 - (SLOTS - 1 - p) % 2))
            for g in range(NT // GROUP):
                tiles_of = slice(GROUP * g, GROUP * (g + 1))
                for k in range(2):
                    src = results[0:2 * B * S, :].rearrange("(k t p) d -> k p t d", k=2, p=P)[k, :, tiles_of, :]
                    sp.dma_start(taken[:, tiles_of, k, :], src).then_inc(taken_in[g], 16)
            outputs(sp, range(0, NT, 2))
            sp.wait_ge(out_sent, 16 * NT)

        @block.tensor
        def _(pe):
            pe.wait_ge(step, SUMS)
            nc.tensor.matmul(ps_r[:, 0:NE], c["earlier"], upto_t[1][:, NT - 1, :], start=True, stop=True)
            nc.tensor.matmul(ps_r[:, NE:2 * NE], c["all"], upto_t[1][:, NT - 1, :], start=True, stop=True).then_inc(counted, 1)
            for n in range(2 * NT):
                if n % PART == 0:
                    pe.wait_ge(step, SPLITF + 2 * (n // PART + 1))
                    pe.wait_ge(in_tile_ready, 2 * (n // PART + 1))
                last = nc.tensor.matmul(ps_i[:, 0:2 * SLOTS], at_place[:, n, :], takes[:, n].rearrange("p a s -> p (a s)"),
                                        start=n == 0, stop=n == 2 * NT - 1)
            last.then_inc(inverted, 1)
            pe.wait_ge(prepared[0], prepared[1])
            pe.wait_ge(step, OWNERS)

            def tokens_t(t, p):
                pe.wait_ge(xs_in[p], arrived(p, t))
                ge(pe, xst_ready, t)
                nc.tensor.transpose(ps_x[:, 0:P], xs[:, p], c["ident"]).then_inc(xst_done, 1)

            held = {}

            def fetch_owners(t, p):
                if isinstance(t, int):
                    held["hidden"] = nc.tensor.value_load(owner[0:1, t:t + 1], min_val=0, max_val=NE - 1)
                else:
                    both = nc.tensor.value_load(owners[0:1, bass.ds(t, 1)], min_val=0, max_val=NE * NE - 1)
                    held["hidden"], held["output"] = both // NE, both % NE

            def hidden(t, p):
                pe.wait_ge(xst_ready, t + 1)
                ge(pe, silu_ready, t - 1)
                nc.tensor.matmul(ps_h[p][:], xst[:, p], w["w1"][:, bass.ds(held["hidden"], 1), :].rearrange("p e f -> p (e f)"),
                                 start=True, stop=True).then_inc(hid_done, 1)

            def hidden_t(t, p):
                pe.wait_ge(silu_ready, t + 1)
                ge(pe, hidt_ready, t - 1)
                for f in range(NF):
                    last = nc.tensor.transpose(ps_t[p][:, P * f:P * (f + 1)], hid[:, p, P * f:P * (f + 1)], c["ident"])
                last.then_inc(hidt_done, 1)

            def output(t, p):
                pe.wait_ge(hidt_ready, t + 1)
                ge(pe, ys_ready, t - 1)
                if isinstance(t, int):
                    e = nc.tensor.value_load(owner[0:1, t:t + 1], min_val=0, max_val=NE - 1)
                else:
                    e = held["output"]
                for f in range(NF):
                    last = nc.tensor.matmul(ps_z[p][:, 0:P], hidt[:, p, f, :], w["w2"][:, bass.ds(e, 1), f, :].rearrange("p e d -> p (e d)"),
                                            start=f == 0, stop=f == NF - 1)
                last.then_inc(out_done, 1)

            pipelined(pe, [(1, fetch_owners), (0, hidden_t), (2, tokens_t), (1, hidden), (-1, output)], SLOTS)

        @block.scalar
        def _(act):
            act.wait_ge(step, EX)
            nc.scalar.activation(ex[:], ex[:], ACT.Exp, scale=1.0 / ROUTER_TEMP).then_inc(exped, 1)

            def feature_major(t, p):
                act.wait_ge(xst_done, t + 1)
                ge(act, hid_done, t - 1)
                nc.scalar.activation(xst[:, p], ps_x[:, 0:P], ACT.Identity, bias=w["beta"], scale=w["gamma"]).then_inc(xst_ready, 1)

            def silu(t, p):
                act.wait_ge(hid_done, t + 1)
                ge(act, hidt_done, t - 1)
                nc.scalar.activation(hid[:, p], ps_h[p][:], ACT.Silu).then_inc(silu_ready, 1)

            pipelined(act, [(2, feature_major), (1, silu)], SLOTS)
            for g in range(NT // GROUP):
                act.wait_ge(rstd_ready, 4 * (g + 1))
                for t in range(GROUP * g, GROUP * (g + 1)):
                    nc.scalar.activation(yout[:, t, :], y[:, t, :], ACT.Identity, bias=shift[:, 1, t:t + 1],
                                         scale=rstd[:, 1, t:t + 1]).then_inc(normed, 1)
                outputs(act, range(GROUP * g + 1, GROUP * (g + 1), 2))

        @block.vector
        def _(dve):
            for t in range(NT):
                nc.vector.max(ranked[:, t, :], logits[:, t, :]).then_inc(step, 1)
            for t in range(NT):
                dve.wait_ge(step, t + 1)
                nc.vector.max_index(place[:, t, :], ranked[:, t, :], logits[:, t, :]).then_inc(step, 1)
            nc.vector.tensor_tensor(ex[:], ranked[:], ranked[:, :, 0:1].broadcast_to([P, NT, NE]), ALU.subtract).then_inc(step, 1)
            dve.wait_ge(step, PLACED)
            nc.vector.tensor_copy(placef[:], place[:, :, 0:2]).then_inc(step, 1)
            dve.wait_ge(step, PLACEF)
            for k in range(2):
                nc.vector.tensor_tensor(mask[:, k], c["iota"].unsqueeze(1).broadcast_to([P, NT, NE]),
                                        placef[:, :, k:k + 1].broadcast_to([P, NT, NE]), ALU.is_equal).then_inc(step, 1)
            dve.wait_ge(step, MASKS)
            nc.vector.tensor_tensor(chosen[:], mask[:, 0], mask[:, 1], ALU.add).then_inc(step, 1)
            for n in range(4):
                src, dst, back = (chosen if n == 0 else upto_t[(n - 1) % 2]), upto_t[n % 2], 2 ** n
                dve.wait_ge(step, CHOSEN + 2 * n)
                nc.vector.tensor_tensor(dst[:, back:], src[:, back:], src[:, :NT - back], ALU.add).then_inc(step, 1)
                nc.vector.tensor_copy(dst[:, :back], src[:, :back]).then_inc(step, 1)
            dve.wait_ge(step, SUMS)
            nc.vector.tensor_tensor(rank[:], upto_t[1][:], chosen[:], ALU.subtract).then_inc(step, 1)
            dve.wait_ge(exped, 1)
            nc.vector.reduce_sum(total[:], ex[:], axis=AX.X).then_inc(step, 1)
            dve.wait_ge(step, TOTAL)
            nc.vector.reciprocal(prob[:, 0, :], total[:]).then_inc(step, 1)
            dve.wait_ge(step, FIRST)
            nc.vector.tensor_tensor(prob[:, 1, :], ex[:, :, 1], prob[:, 0, :], ALU.mult).then_inc(step, 1)
            dve.wait_ge(counted, 1)
            nc.vector.tensor_tensor(many[:], ps_r[:, NE:2 * NE].unsqueeze(2).broadcast_to([P, NE, NT]),
                                    c["fills"].unsqueeze(1).broadcast_to([P, NE, NT]), ALU.is_gt).then_inc(step, 1)
            dve.wait_ge(step, MANY)
            nc.vector.reduce_sum(tiles[:], many[:], axis=AX.X).then_inc(step, 1)
            dve.wait_ge(step, TILES)
            nc.vector.tensor_tensor(low[:], tiles[:].unsqueeze(1).broadcast_to([P, NE, NE]), c["lower"], ALU.mult).then_inc(step, 1)
            dve.wait_ge(step, LOW)
            nc.vector.reduce_sum(base[:], low[:], axis=AX.X).then_inc(step, 1)
            dve.wait_ge(step, BASE)
            nc.vector.scalar_tensor_tensor(offset[:], base[:], float(P), ps_r[:, 0:NE], ALU.mult, ALU.add).then_inc(step, 1)
            dve.wait_ge(step, OFFSET)
            nc.vector.tensor_tensor(rank[:], rank[:], offset[:].unsqueeze(1).broadcast_to([P, NT, NE]), ALU.add).then_inc(step, 1)
            dve.wait_ge(step, SLOTALL)
            nc.vector.tensor_tensor(picked[:], mask[:], rank[:].unsqueeze(1).broadcast_to([P, 2, NT, NE]), ALU.mult).then_inc(step, 1)
            dve.wait_ge(step, PICKED)
            nc.vector.reduce_sum(slotf[:], picked[:], axis=AX.X).then_inc(step, 1)
            dve.wait_ge(step, SLOTF)
            nc.vector.tensor_copy(slot[:], slotf[:]).then_inc(step, 1)
            dve.wait_ge(step, SLOT)
            nc.vector.tensor_scalar(tile_u[:], slot[:], int(np.log2(P)), None, ALU.logical_shift_right).then_inc(step, 1)
            nc.vector.tensor_scalar(place_u[:], slot[:], P - 1, None, ALU.bitwise_and).then_inc(step, 1)
            dve.wait_ge(step, SPLIT)
            nc.vector.tensor_copy(tilef[:], tile_u[:]).then_inc(step, 1)
            nc.vector.tensor_copy(inf[:], place_u[:]).then_inc(step, 1)
            dve.wait_ge(step, SPLITF)
            for n in range(0, 2 * NT, PART):
                k, t = n // NT, n % NT
                nc.vector.tensor_tensor(in_tile[:, n:n + PART, :], c["slots"].unsqueeze(1).broadcast_to([P, PART, SLOTS]),
                                        tilef[:, k, t:t + PART].unsqueeze(2).broadcast_to([P, PART, SLOTS]), ALU.is_equal).then_inc(step, 1)
                nc.vector.tensor_tensor(at_place[:, n:n + PART, :], c["places"].unsqueeze(1).broadcast_to([P, PART, P]),
                                        inf[:, k, t:t + PART].unsqueeze(2).broadcast_to([P, PART, P]), ALU.is_equal).then_inc(step, 1)
            nc.vector.tensor_tensor(end[:], base[:], tiles[:], ALU.add).then_inc(step, 1)
            dve.wait_ge(step, END)
            nc.vector.tensor_tensor(past[:], end[:].unsqueeze(1).broadcast_to([P, SLOTS, NE]),
                                    c["slots"].unsqueeze(2).broadcast_to([P, SLOTS, NE]), ALU.is_le).then_inc(step, 1)
            dve.wait_ge(step, PAST)
            nc.vector.reduce_sum(ownerf[:], past[:], axis=AX.X).then_inc(step, 1)
            dve.wait_ge(step, OWNERF)
            nc.vector.tensor_scalar(owner[:], ownerf[:], float(NE - 1), None, ALU.min).then_inc(step, 1)
            dve.wait_ge(step, OWNER)
            nc.vector.scalar_tensor_tensor(owners[:, 2:], owner[:, 2:], float(NE), owner[:, :-2], ALU.mult, ALU.add).then_inc(step, 1)
            dve.wait_ge(inverted, 1)
            nc.vector.tensor_copy(taken_f[:], ps_i[:, SLOTS:2 * SLOTS]).then_inc(step, 1)
            dve.wait_ge(step, REST)
            nc.vector.scalar_tensor_tensor(taken_f[:], ps_i[:, 0:SLOTS], float(P), taken_f[:], ALU.mult, ALU.add).then_inc(step, 1)
            dve.wait_ge(step, TAKEN)
            nc.vector.tensor_scalar(second[:], taken_f[:], B * S + 0.5, float(-B * S), ALU.is_gt, ALU.mult).then_inc(step, 1)
            nc.vector.tensor_scalar(empty[:], taken_f[:], 0.5, None, ALU.is_lt).then_inc(step, 1)
            dve.wait_ge(step, SECOND)
            nc.vector.tensor_tensor(source_f[:], taken_f[:], second[:], ALU.add).then_inc(step, 1)
            dve.wait_ge(step, EMPTY)
            nc.vector.tensor_tensor(spare[:], empty[:], c["behind"], ALU.mult).then_inc(step, 1)
            dve.wait_ge(step, SOURCEF)
            nc.vector.tensor_scalar(sources[:], source_f[:], 1.0, 0.0, ALU.subtract, ALU.max).then_inc(step, 1)
            dve.wait_ge(step, SPARE)
            nc.vector.scalar_tensor_tensor(targets[:], taken_f[:], 1.0, spare[:], ALU.subtract, ALU.add).then_inc(step, 1)
            dve.wait_ge(step, LISTS)

            def source_rows(t, p):
                ge(dve, xs_in[p], arrived(p, t - 2))
                nc.vector.tensor_copy(source[:, p:p + 1], sources[:, bass.ds(t, 1)]).then_inc(source_ready, 1)

            def target_rows(t, p):
                ge(dve, ys_sent[p], arrived(p, t - 2))
                nc.vector.tensor_copy(target[:, p:p + 1], targets[:, bass.ds(t, 1)]).then_inc(target_ready, 1)

            def hidden_out(t, p):
                dve.wait_ge(hidt_done, t + 1)
                ge(dve, out_done, t - 1)
                nc.vector.tensor_copy(hidt[:, p], ps_t[p][:].rearrange("p (f s) -> p f s", f=NF)).then_inc(hidt_ready, 1)

            def output(t, p):
                dve.wait_ge(out_done, t + 1)
                ge(dve, ys_sent[p], arrived(p, t - 2))
                nc.vector.tensor_copy(ys[:, p], ps_z[p][:, 0:P]).then_inc(ys_ready, 1)

            pipelined(dve, [(4, source_rows), (0, hidden_out), (-1, target_rows), (-1, output)], SLOTS)

            for g in range(NT // GROUP):
                group = range(GROUP * g, GROUP * (g + 1))
                done = 4 * GROUP * g
                dve.wait_ge(taken_in[g], 32)
                for t in group:
                    nc.vector.scalar_tensor_tensor(part_sum[:, t, :], taken[:, t, 0, :], prob[:, 0, t:t + 1], x_res[:, t, :],
                                                   ALU.mult, ALU.add).then_inc(sum_step, 1)
                for n, t in enumerate(group):
                    dve.wait_ge(sum_step, done + n + 1)
                    nc.vector.scalar_tensor_tensor(y[:, t, :], taken[:, t, 1, :], prob[:, 1, t:t + 1], part_sum[:, t, :],
                                                   ALU.mult, ALU.add).then_inc(sum_step, 1)
                for n, t in enumerate(group):
                    dve.wait_ge(sum_step, done + GROUP + n + 1)
                    nc.vector.bn_stats(stats[:, t, :], y[:, t, :]).then_inc(sum_step, 1)
                for n, t in enumerate(group):
                    dve.wait_ge(sum_step, done + 2 * GROUP + n + 1)
                    nc.vector.bn_aggr(mv[:, t, :], stats[:, t, :]).then_inc(sum_step, 1)

        @block.gpsimd
        def _(pool):
            for n in range(0, 2 * NT, PART):
                part = in_tile[:, n:n + PART, :]
                pool.wait_ge(step, SPLITF + 2 * (n // PART) + 1)
                nc.gpsimd.tensor_tensor(takes[:, n:n + PART, 0, :], part, c["groups"][:, n:n + PART].unsqueeze(2).broadcast_to([P, PART, SLOTS]),
                                        ALU.mult).then_inc(in_tile_ready, 1)
                nc.gpsimd.tensor_tensor(takes[:, n:n + PART, 1, :], part, c["one_more"].unsqueeze(2).broadcast_to([P, PART, SLOTS]),
                                        ALU.mult).then_inc(in_tile_ready, 1)
            pool.wait_ge(prepared[0], prepared[1])

            def gather(t, p):
                pool.wait_ge(source_ready, t + 1)
                ge(pool, xst_done, t - 1)
                ge(pool, xs_in[p], arrived(p, t - 2))
                nc.gpsimd.nop(nofuse=True)
                nc.gpsimd.indirect_dma_start(xs[:, p], None, rows_dram, bass.IndirectOffsetOnAxis(source[:, p:p + 1], axis=0)
                                             ).then_inc(xs_in[p], 16)

            def store(t, p):
                pool.wait_ge(ys_ready, t + 1)
                pool.wait_ge(target_ready, t + 1)
                nc.gpsimd.nop(nofuse=True)
                nc.gpsimd.indirect_dma_start(results, bass.IndirectOffsetOnAxis(target[:, p:p + 1], axis=0), ys[:, p], None
                                             ).then_inc(ys_sent[p], 16)

            pipelined(pool, [(4, gather), (-1, store)], SLOTS)
            for g in range(1, NT // GROUP + 1):
                tiles_of = slice(GROUP * (g - 1), GROUP * g)
                pool.wait_ge(sum_step, 4 * GROUP * g)
                nc.gpsimd.tensor_tensor(rstd[:, 0, tiles_of], mv[:, tiles_of, 1], c["eps"][:, 0:GROUP], ALU.add).then_inc(rstd_ready, 1)
                nc.gpsimd.tensor_tensor(shift[:, 0, tiles_of], mv[:, tiles_of, 0], c["minus"][:, 0:GROUP], ALU.mult).then_inc(rstd_ready, 1)
                pool.wait_ge(rstd_ready, 4 * g - 3)
                nc.gpsimd.tensor_tensor(rstd[:, 1, tiles_of], rstd[:, 0, tiles_of], c["neghalf"][:, 0:GROUP],
                                        ALU.pow).then_inc(rstd_ready, 1)
                pool.wait_ge(rstd_ready, 4 * g - 1)
                nc.gpsimd.tensor_tensor(shift[:, 1, tiles_of], shift[:, 0, tiles_of], rstd[:, 1, tiles_of], ALU.mult).then_inc(rstd_ready, 1)


EARLY = ("eb", "self_k", "self_q", "self_v", "self_o", "lam", "ln_g", "ln_b", "cross_ob", "ident", "pair", "parity", "half",
         "first", "second", "neghalf", "eps")
ALONE = ("x", "xt", "ct", "w1", "w2")


def pack(arrays):
    packs, places = {"early": [], "late": []}, {}
    for name in [*EARLY, *(name for name in arrays if name not in EARLY + ALONE)]:
        into = "early" if name in EARLY else "late"
        flat = arrays[name].reshape(P, -1)
        places[name] = (into, sum(part.shape[1] for part in packs[into]), arrays[name].shape)
        packs[into].append(flat)
    return {name: arrays[name] for name in ALONE} | {into: np.concatenate(parts, axis=1) for into, parts in packs.items()}, places


def view(tile, start, shape):
    columns = tile[:, start:start + int(np.prod(shape[1:]))]
    return columns.rearrange("p (a b) -> p a b", b=shape[2]) if len(shape) == 3 else columns


def build(nc, a, places, out_dram):
    with ExitStack() as ctx:
        def sb(name, shape, dt=F32):
            return ctx.enter_context(nc.sbuf_tensor(name, shape, dt))

        banks = [ctx.enter_context(nc.psum_tensor(f"bank{n}", [P, CHUNK], F32)) for n in range(8)]
        xt_a, xt_b, ct = sb("xt_a", [P, B * S]), sb("xt_b", [P, B * S]), sb("ct", [P, B * S])
        res_a, res_b = sb("res_a", [P, NT, P]), sb("res_b", [P, NT, P])
        logits = sb("logits", [P, NT, NE])
        packed = {pack: sb(pack, list(a[pack].shape)) for pack in ("early", "late")}
        h = {name: view(packed[pack], start, shape) for name, (pack, start, shape) in places.items()}
        eb3 = sb("eb3", [3, NE * P], BF16)
        ones3 = sb("ones3", [3, P], BF16)

        loaded = ctx.enter_context(nc.semaphore("loaded"))
        x_loaded = ctx.enter_context(nc.semaphore("x_loaded"))
        loaded_late = ctx.enter_context(nc.semaphore("loaded_late"))
        split = ctx.enter_context(nc.semaphore("split"))
        part = [sb(f"eb_part{n}", [P, NE]) for n in range(3)]
        short = [sb(f"eb_short{n}", [P, NE], BF16) for n in range(3)]
        with nc.Block() as block:
            @block.sync
            def _(sp):
                sp.dma_start(packed["early"][:], a["early"]).then_inc(loaded, 16)
                sp.dma_start(xt_a[:], a["xt"]).then_inc(loaded, 16)
                sp.wait_ge(loaded, 32)

            @block.vector
            def _(dve):
                dve.wait_ge(loaded, 32)
                nc.vector.memset(ones3[:], 1.0)
                for k in range(3):
                    src = h["eb"] if k == 0 else part[k - 1][:]
                    if k:
                        dve.wait_ge(split, 2 * k)
                    nc.vector.tensor_copy(short[k][:], src).then_inc(split, 1)
                    dve.wait_ge(split, 2 * k + 1)
                    nc.vector.tensor_tensor(part[k][:], src, short[k][:], ALU.subtract).then_inc(split, 1)

        def load_late(sp):
            sp.dma_start(res_a[:], a["x"].rearrange("(t p) d -> p t d", p=P)).then_inc(x_loaded, 16)
            sp.dma_start(ct[:], a["ct"]).then_inc(loaded_late, 16)
            sp.dma_start(packed["late"][:], a["late"]).then_inc(loaded_late, 16)
            sp.wait_ge(split, 6)
            for k in range(3):
                sp.dma_start(eb3[k:k + 1, :], short[k][:]).then_inc(loaded_late, 16)

        c = {name: h[name] for name in ("ident", "pair", "half", "first", "second", "both", "neghalf", "minus", "eps", "iota", "h2", "earlier",
                                    "all", "fills", "lower", "slots", "groups", "one_more", "places", "behind")}
        c["parity"] = h["parity"]
        c["ones3"] = ones3[:]
        c["x_loaded"] = (x_loaded, 16)
        with ExitStack() as keys:
            km = keys.enter_context(nc.sbuf_tensor("km", [P, B, CHUNK], F32))
            vb = keys.enter_context(nc.sbuf_tensor("vb", [P, B, 4, 2, VD + 1], F32))
            w = {"q": h["self_q"], "k": h["self_k"], "v": h["self_v"], "o": h["self_o"], "qb": None, "kb": None,
                 "lam": h["lam"], "og": h["ln_g"], "ob": h["ln_b"], "next_bias": h["cross_ob"]}
            pair_attention(nc, banks, True, w, xt_a, xt_a, km, vb, lambda t: res_a[:, t, :], res_b, xt_b, c,
                           background=load_late)
            late_ready = 16 * 5
            with nc.Block() as block:
                @block.sync
                def _(sp):
                    sp.wait_ge(loaded_late, late_ready)

            w = {"q": h["cross_q"], "k": h["cross_k"], "v": h["cross_v"], "o": h["cross_o"], "qb": h["cross_qb"],
                 "kb": h["cross_kb"], "vb": h["cross_vb"], "gate": h["gate"]}
            pair_attention(nc, banks, False, w, xt_b, ct, km, vb, lambda t: res_b[:, t, :], res_a, xt_a, c, logits)
        x_w1 = sb("last_w1", [P, NE, FF])
        x_w2 = sb("last_w2", [P, NE, NF, P])
        prepared = ctx.enter_context(nc.semaphore("prepared"))
        rows_dram = nc.dram_tensor("rows", (B * S, E), F32, kind="Internal").ap()
        results = nc.dram_tensor("results", (2 * B * S + SLOTS * P, E), F32, kind="Internal").ap()

        def load_weights(sp):
            for e in range(NE):
                sp.dma_start(x_w1[:, e, :], a["w1"][e]).then_inc(prepared, 16)
                sp.dma_start(x_w2[:, e], a["w2"][e].rearrange("(f p) d -> p f d", p=P)).then_inc(prepared, 16)

        w = {"eb3": eb3[:], "expert": h["expert"], "combine": h["combine"]}
        first_experts(nc, banks, w, xt_a, res_a, logits, xt_b, c, load_weights)
        w = {"in": h["in"], "in_b": h["in_b"], "v_b": h["v_b"], "out": h["out"], "out_b": h["out_b"],
             "x_w2": h["x_w2"], "x_b": h["x_b"]}
        sequence_attention(nc, banks, w, xt_b, ct[:], res_a, res_b, xt_a, c)
        w = {"x_w1": h["x_w1"], "router": h["router"], "gamma": h["gamma"], "beta": h["beta"]}
        position_linear(nc, banks, w, xt_a, res_b, logits, xt_b, rows_dram, prepared, res_a, c)
        w = {"w1": x_w1, "w2": x_w2, "gamma": h["gamma"], "beta": h["beta"]}
        last_experts(nc, banks, w, (prepared, 16 * (2 * NE + NT // 4)), rows_dram, res_a, logits, results, out_dram, c)


def constants():
    p = np.arange(P)
    f = lambda x: np.ascontiguousarray(x, dtype=np.float32)
    token = np.arange(P)
    place = np.stack([(token[None, :] == S * u + p[:, None] % S) for u in range(2)], axis=1)
    par = (p // S)[:, None, None]
    return {
        "ident": f(np.eye(P)),
        "pair": f(p[:, None] // VD == np.arange(NPAIR)),
        "parity": f(((p // HD) % 2)[:, None] == np.arange(2)) * np.float32(HD ** -0.5),
        "half": f((p // S)[:, None] == np.arange(2)),
        "first": f(place & (par == 0)),
        "second": -f(place & (par == 1)),
        "both": f(p[:, None] % S == np.arange(S)),
        "neghalf": f(np.full((P, NE), -0.5)),
        "minus": f(np.full((P, NE), -1)),
        "eps": f(np.full((P, NE), LN_EPS)),
        "iota": f(np.broadcast_to(np.arange(NE), (P, NE))),
        "h2": f((p // D1)[:, None] == np.arange(2)) * np.float32(D1 ** -0.5),
        "earlier": f(p[:, None] < p),
        "all": f(np.ones((P, P))),
        "fills": f(np.broadcast_to(P * np.arange(NT), (P, NT))),
        "lower": f(np.broadcast_to(np.arange(NE)[:, None] > np.arange(NE), (P, NE, NE))),
        "slots": f(np.broadcast_to(np.arange(SLOTS), (P, SLOTS))),
        "groups": f(np.broadcast_to(np.arange(2 * NT), (P, 2 * NT))),
        "one_more": f(np.broadcast_to(p[:, None] + 1, (P, NT // 2))),
        "behind": f(1 + 2 * B * S + np.arange(SLOTS * P).reshape(SLOTS, P).T),
        "places": f(np.broadcast_to(p, (P, P))),
    }


def kernel(**inputs):
    import concourse.bacc as bacc
    from concourse.bass_utils import run_bass_kernel_spmd

    v = {name: np.asarray(x) for name, x in inputs.items()}
    rows = lambda x, n=P: np.broadcast_to(x.reshape(1, -1), (n, x.size))
    col = lambda x: x.reshape(-1, P).T
    arrays = {
        "x": v["x"].reshape(B * S, E),
        "xt": v["x"].reshape(B * S, E).T,
        "ct": v["ctx_1024"].reshape(B * S, E).T,
        "self_q": v["L0_attn_Wq"], "self_k": v["L0_attn_Wk"], "self_v": v["L0_attn_Wv"], "self_o": v["L0_attn_Wo"],
        "lam": np.broadcast_to(np.stack([v["L0_attn_lq1"], v["L0_attn_lq2"], v["L0_attn_lk1"], v["L0_attn_lk2"]]), (P, 4, HD)),
        "ln_g": np.tile(v["L0_attn_ln_g"], NPAIR).reshape(P, 1), "ln_b": np.tile(v["L0_attn_ln_b"], NPAIR).reshape(P, 1),
        "cross_q": v["L0_xattn_wq_w"].T, "cross_k": v["L0_xattn_wk_w"].T, "cross_v": v["L0_xattn_wv_w"].T,
        "cross_o": v["L0_xattn_wo_w"].T, "cross_qb": col(v["L0_xattn_wq_b"]), "cross_kb": col(v["L0_xattn_wk_b"]),
        "cross_vb": col(v["L0_xattn_wv_b"]), "cross_ob": rows(v["L0_xattn_wo_b"]),
        "gate": v["L0_ffn_gate_w"].T,
        "expert": v["L0_ffn_expert_w"].transpose(2, 0, 1).reshape(E, NE * E),
        "eb": v["L0_ffn_expert_b"].reshape(P, NE), "combine": v["L0_ffn_combine_w"].T,
        "in": v["L1_attn_in_proj_weight"].T, "in_b": col(v["L1_attn_in_proj_bias"]),
        "v_b": rows(v["L1_attn_in_proj_bias"][2 * H1 * D1:]),
        "out": v["L1_attn_out_proj_weight"].T.reshape(NJ, P, E).transpose(1, 0, 2),
        "out_b": rows(v["L1_attn_out_proj_bias"]),
        "x_w1": v["L1_xattn_W"][:, :E].T, "x_w2": v["L1_xattn_W"][:, E:].T, "x_b": rows(v["L1_xattn_b"]),
        "gamma": col(v["L1_ffn_gamma"]), "beta": col(v["L1_ffn_beta"]), "router": v["L1_ffn_router_w"].T,
        "w1": v["L1_ffn_W1"], "w2": v["L1_ffn_W2"],
    }
    arrays.update(constants())
    arrays, places = pack(arrays)
    arrays = {name: np.ascontiguousarray(x) for name, x in arrays.items()}
    nc = bacc.Bacc("TRN2", target_bir_lowering=False, num_devices=1)
    a = {name: nc.dram_tensor(f"in_{name}", x.shape, mybir.dt.from_np(x.dtype), kind="ExternalInput").ap()
         for name, x in arrays.items()}
    out = nc.dram_tensor("out", (B, S, E), F32, kind="ExternalOutput").ap()
    build(nc, a, places, out)
    r = run_bass_kernel_spmd(nc, [{f"in_{name}": x for name, x in arrays.items()}], core_ids=[0])
    return r.results[0]["out"]
```
